# Optimizing a Trainium2 kernel written in Bass

```python
import numpy as np
import jax
import jax.numpy as jnp

def _softmax(x, axis=-1):
    return jax.nn.softmax(x, axis=axis)

def _gelu(x):
    return jax.nn.gelu(x, approximate=True)

def _silu(x):
    return jax.nn.silu(x)

def _sigmoid(x):
    return jax.nn.sigmoid(x)

def _layernorm(x, axis=-1, eps=1e-05):
    m = jnp.mean(x, axis=axis, keepdims=True)
    v = jnp.var(x, axis=axis, keepdims=True)
    return (x - m) / jnp.sqrt(v + eps)

def _scatter_add(tgt, idx, src, axis=0):
    return tgt.at[idx].add(src)

def _segment_sum(src, seg, n):
    return jax.ops.segment_sum(src, seg, n)
kernel_name = 'mk_xattn_ffn_d4_seqx_r8_06ce9f'

def setup_inputs(seed: int=0):
    np.random.seed(seed)
    _w = jnp.asarray

    def _rec_inputs():
        import jax
        import jax.numpy as jnp
        _rk = jax.random.key(seed)
        x = -0.0002928 + 1 * jax.random.normal(jax.random.fold_in(_rk, 1), (32, 128, 128), jnp.float32)
        _lenS = 128 - jax.random.randint(jax.random.fold_in(_rk, 7), (32,), 0, max(1, 128 // 4) + 1, jnp.int32)
        _lenS2 = 128 - jax.random.randint(jax.random.fold_in(_rk, 8), (32,), 0, max(1, 128 // 4) + 1, jnp.int32)
        _ctx_1024P = jax.random.normal(jax.random.fold_in(_rk, 11), (32, 16, 128), jnp.float32)
        _ctx_1024c = jax.random.dirichlet(jax.random.fold_in(_rk, 511), 0.3 * jnp.ones((16,), jnp.float32), (32, 128))
        _ctx_1024t = jnp.einsum('bsk,bkd->bsd', _ctx_1024c, _ctx_1024P)
        _ctx_1024t = _ctx_1024t * jax.lax.rsqrt(jnp.mean(jnp.square(_ctx_1024t)) + 1e-12) * 0.953939
        ctx_1024 = -1.39393e-06 + 0.999914 * (_ctx_1024t + 0.3 * jax.random.normal(jax.random.fold_in(_rk, 611), (32, 128, 128), jnp.float32))
        _validS = jnp.arange(128)[None, :] < _lenS[:, None]
        _validS2 = jnp.arange(128)[None, :] < _lenS2[:, None]
        _causal = jnp.tril(jnp.ones((128, 128), dtype=bool))
        mask_Bx1xSxS2_bk0 = jnp.logical_not(jnp.broadcast_to(_validS2[:, None, None, :], (32, 1, 128, 128)))
        return (x, ctx_1024, mask_Bx1xSxS2_bk0)
    x, ctx_1024, mask_Bx1xSxS2_bk0 = _rec_inputs()

    def _L0_xattn_setup():
        import jax, jax.numpy as jnp
        import numpy as np
        D_MODEL = 128
        H = 16
        D_K = D_MODEL // H
        key = jax.random.key(seed)
        ks = jax.random.split(key, 11)
        B, S = (2, 256)
        scale = 1.0 / np.sqrt(D_MODEL)
        inp = {'q': jax.random.normal(ks[0], (B, S, D_MODEL), jnp.float32), 'k': jax.random.normal(ks[1], (B, S, D_MODEL), jnp.float32), 'v': jax.random.normal(ks[2], (B, S, D_MODEL), jnp.float32), 'w_q': jax.random.normal(ks[3], (D_MODEL, D_MODEL), jnp.float32) * scale, 'b_q': jnp.zeros((D_MODEL,), jnp.float32), 'w_k': jax.random.normal(ks[4], (D_MODEL, D_MODEL), jnp.float32) * scale, 'b_k': jnp.zeros((D_MODEL,), jnp.float32), 'w_v': jax.random.normal(ks[5], (D_MODEL, D_MODEL), jnp.float32) * scale, 'b_v': jnp.zeros((D_MODEL,), jnp.float32), 'w_o': jax.random.normal(ks[6], (D_MODEL, D_MODEL), jnp.float32) * scale, 'b_o': jnp.zeros((D_MODEL,), jnp.float32)}
        return inp
    _L0_xattn_all = _L0_xattn_setup()
    _L0_xattn_in = {k: v for k, v in _L0_xattn_all.items() if k in ('w_q', 'b_q', 'w_k', 'b_k', 'w_v', 'b_v', 'w_o', 'b_o')}
    del _L0_xattn_all

    def _L0_ffn_setup():
        import jax, jax.numpy as jnp
        import numpy as np
        N, T, D = (4, 512, 128)
        NUM_EXPERTS = 8
        EXPERT_CAP = 2.0
        MLP_RATIO = 4
        HIDDEN = MLP_RATIO * D
        key = jax.random.key(seed)
        k1, k2, k3, k4 = jax.random.split(key, 4)
        x = jax.random.normal(k1, (N, T, D), dtype=jnp.float32)
        gate_w = jax.random.truncated_normal(k2, -2.0, 2.0, (D, NUM_EXPERTS), dtype=jnp.float32) * 0.02
        w1 = jax.random.normal(k3, (NUM_EXPERTS, D, HIDDEN), dtype=jnp.float32) * 0.02
        w2 = jax.random.normal(k4, (NUM_EXPERTS, HIDDEN, D), dtype=jnp.float32) * 0.02
        return {'x': x, 'gate_w': gate_w, 'w1': w1, 'w2': w2}
    _L0_ffn_all = _L0_ffn_setup()
    _L0_ffn_in = {k: v for k, v in _L0_ffn_all.items() if k in ('gate_w', 'w1', 'w2')}
    del _L0_ffn_all

    def _L1_xattn_setup():
        import jax, jax.numpy as jnp
        import numpy as np
        from jax import lax
        NUM_HEADS = 16
        DIM = 128
        BATCH = 4
        SEQ = 256
        key = jax.random.key(seed)
        ks = jax.random.split(key, 12)
        f32 = jnp.float32
        q = jax.random.normal(ks[0], (BATCH, SEQ, DIM), dtype=f32)
        k = jax.random.normal(ks[1], (BATCH, SEQ, DIM), dtype=f32)
        v = jax.random.normal(ks[2], (BATCH, SEQ, DIM), dtype=f32)
        lim = 1.0 / np.sqrt(DIM)
        Wi = jax.random.uniform(ks[3], (DIM, DIM), minval=-lim, maxval=lim, dtype=f32)
        bi = jax.random.uniform(ks[4], (DIM,), minval=-lim, maxval=lim, dtype=f32)
        Wg = jax.random.uniform(ks[5], (DIM, DIM), minval=-lim, maxval=lim, dtype=f32)
        bg = jax.random.uniform(ks[6], (DIM,), minval=-lim, maxval=lim, dtype=f32)
        Wo = jax.random.uniform(ks[7], (DIM, DIM), minval=-lim, maxval=lim, dtype=f32)
        bo = jax.random.uniform(ks[8], (DIM,), minval=-lim, maxval=lim, dtype=f32)
        A = jax.random.normal(ks[9], (DIM, DIM), dtype=f32) * 0.1
        Bm = jax.random.normal(ks[10], (DIM, DIM), dtype=f32) * 0.1
        decay = jnp.full((1, NUM_HEADS, 1), 0.9, dtype=f32)
        return dict(q=q, k=k, v=v, Wi=Wi, bi=bi, Wg=Wg, bg=bg, A=A, Bm=Bm, Wo=Wo, bo=bo, decay=decay)
    _L1_xattn_all = _L1_xattn_setup()
    _L1_xattn_in = {k: v for k, v in _L1_xattn_all.items() if k in ('Wi', 'bi', 'Wg', 'bg', 'A', 'Bm', 'Wo', 'bo', 'decay')}
    del _L1_xattn_all

    def _L1_ffn_setup():
        import jax, jax.numpy as jnp
        import numpy as np
        import math
        D = 128
        H = 16
        E = 8
        TOPK = 2
        LAT = D // 2
        KPH = LAT // H
        HD = D // H

        def _forward(hs, q_w, q_b, k_w, k_b, v_w, v_b, o_w, o_b, router_w, router_b, w1, b1, w2, b2):
            B, S, _ = hs.shape
            Q = (hs @ q_w + q_b).reshape(B, S, H, HD).transpose(0, 2, 1, 3)
            K = (hs @ k_w + k_b).reshape(B, S, H, KPH).transpose(0, 2, 1, 3)
            V = (hs @ v_w + v_b).reshape(B, S, H, KPH).transpose(0, 2, 1, 3)
            scores = jnp.einsum('bhsk,bhtk->bhst', Q[..., :KPH], K) / math.sqrt(KPH)
            attn = jax.nn.softmax(scores, axis=-1)
            ao = jnp.einsum('bhst,bhtv->bhsv', attn, V)
            ao = ao.transpose(0, 2, 1, 3).reshape(B, S, H * KPH)
            ao = jnp.concatenate([ao, jnp.zeros((B, S, D - LAT), ao.dtype)], axis=-1)
            mla_out = ao @ o_w + o_b
            probs = jax.nn.softmax(mla_out @ router_w + router_b, axis=-1)
            topw, topi = jax.lax.top_k(probs, TOPK)
            topw = topw / (topw.sum(-1, keepdims=True) + 1e-08)
            combine = jnp.sum(jax.nn.one_hot(topi, E, dtype=probs.dtype) * topw[..., None], axis=-2)
            h1 = jnp.einsum('bsd,edf->ebsf', mla_out, w1) + b1[:, None, None, :]
            h1 = jax.nn.gelu(h1, approximate=False)
            h2 = jnp.einsum('ebsf,efd->ebsd', h1, w2) + b2[:, None, None, :]
            moe_out = jnp.einsum('bse,ebsd->bsd', combine, h2)
            return hs + 0.3 * moe_out
        key = jax.random.key(seed)
        ks = jax.random.split(key, 16)
        s = 0.02
        inp = {'hidden_states': jax.random.normal(ks[0], (2, 256, D), jnp.float32), 'q_w': jax.random.normal(ks[1], (D, D), jnp.float32) * s, 'q_b': jnp.zeros((D,), jnp.float32), 'k_w': jax.random.normal(ks[2], (D, LAT), jnp.float32) * s, 'k_b': jnp.zeros((LAT,), jnp.float32), 'v_w': jax.random.normal(ks[3], (D, LAT), jnp.float32) * s, 'v_b': jnp.zeros((LAT,), jnp.float32), 'o_w': jax.random.normal(ks[4], (D, D), jnp.float32) * s, 'o_b': jnp.zeros((D,), jnp.float32), 'router_w': jax.random.normal(ks[5], (D, E), jnp.float32) * s, 'router_b': jnp.zeros((E,), jnp.float32), 'w1': jax.random.normal(ks[6], (E, D, 2 * D), jnp.float32) * s, 'b1': jnp.zeros((E, 2 * D), jnp.float32), 'w2': jax.random.normal(ks[7], (E, 2 * D, D), jnp.float32) * s, 'b2': jnp.zeros((E, D), jnp.float32)}
        return inp
    _L1_ffn_all = _L1_ffn_setup()
    _L1_ffn_in = {k: v for k, v in _L1_ffn_all.items() if k in ('q_w', 'q_b', 'k_w', 'k_b', 'v_w', 'v_b', 'o_w', 'o_b', 'router_w', 'router_b', 'w1', 'b1', 'w2', 'b2')}
    del _L1_ffn_all

    def _L2_xattn_setup():
        import jax, jax.numpy as jnp
        import numpy as np
        D = 128
        H = 16
        B = 4
        S = 256
        NEG = -1000000000.0
        key = jax.random.key(seed)
        ks = jax.random.split(key, 12)
        s = 0.02
        inp = {'Q': jax.random.normal(ks[0], (B, S, D), jnp.float32), 'K': jax.random.normal(ks[1], (B, S, D), jnp.float32), 'V': jax.random.normal(ks[2], (B, S, D), jnp.float32), 'mask': jnp.broadcast_to(jnp.tril(jnp.ones((S, S), bool)), (B, 1, S, S)), 'Wq': jax.random.normal(ks[3], (D, D), jnp.float32) * s, 'bq': jnp.zeros((D,), jnp.float32), 'Wk': jax.random.normal(ks[4], (D, D), jnp.float32) * s, 'bk': jnp.zeros((D,), jnp.float32), 'Wv': jax.random.normal(ks[5], (D, D), jnp.float32) * s, 'bv': jnp.zeros((D,), jnp.float32), 'Wo': jax.random.normal(ks[6], (D, D), jnp.float32) * s, 'bo': jnp.zeros((D,), jnp.float32)}
        return inp
    _L2_xattn_all = _L2_xattn_setup()
    _L2_xattn_in = {k: v for k, v in _L2_xattn_all.items() if k in ('Wq', 'bq', 'Wk', 'bk', 'Wv', 'bv', 'Wo', 'bo')}
    del _L2_xattn_all

    def _L2_ffn_setup():
        import jax, jax.numpy as jnp
        import numpy as np
        E = 8
        TOPK = 2
        PRIME = 11
        HASH_OFF = 7919
        N_SHARED = 1
        key = jax.random.key(seed)
        ks = jax.random.split(key, 8)
        B, T, C, Hs, Hr = (4, 1024, 128, 256, 128)
        sc = lambda k, shape, fan: jax.random.normal(k, shape, jnp.float32) * fan ** (-0.5)
        return {'x': jax.random.normal(ks[0], (B, T, C), jnp.float32), 't_emb': jax.random.normal(ks[1], (B, C), jnp.float32), 'sw1': sc(ks[2], (C, Hs), C), 'sb1': jnp.zeros((Hs,), jnp.float32), 'sw3': sc(ks[3], (C, Hs), C), 'sb3': jnp.zeros((Hs,), jnp.float32), 'sw2': sc(ks[4], (Hs, C), Hs), 'sb2': jnp.zeros((C,), jnp.float32), 'w1': sc(ks[5], (E, C, Hr), C), 'b1': jnp.zeros((E, Hr), jnp.float32), 'w2': sc(ks[6], (E, Hr, C), Hr), 'b2': jnp.zeros((E, C), jnp.float32)}
    _L2_ffn_all = _L2_ffn_setup()
    _L2_ffn_in = {k: v for k, v in _L2_ffn_all.items() if k in ('t_emb', 'sw1', 'sb1', 'sw3', 'sb3', 'sw2', 'sb2', 'w1', 'b1', 'w2', 'b2')}
    del _L2_ffn_all

    def _L3_xattn_setup():
        import jax, jax.numpy as jnp
        import numpy as np
        import math
        EMBED_DIM = 128
        NUM_HEADS = 16
        HEAD_DIM = EMBED_DIM // NUM_HEADS
        SUB_HEAD_DIM = HEAD_DIM // 2
        SCALING = 1.0 / math.sqrt(SUB_HEAD_DIM)
        LAMBDA_INIT = 0.8 - 0.6 * math.exp(-0.3 * 0)
        key = jax.random.key(seed)
        ks = jax.random.split(key, 10)
        B, T, D = (2, 256, EMBED_DIM)
        xav = math.sqrt(6.0 / (D + D))
        return {'query': jax.random.normal(ks[0], (B, T, D), jnp.float32), 'key': jax.random.normal(ks[1], (B, T, D), jnp.float32), 'value': jax.random.normal(ks[2], (B, T, D), jnp.float32), 'in_proj_weight': jax.random.uniform(ks[3], (3 * D, D), jnp.float32, -xav, xav), 'in_proj_bias': jnp.zeros((3 * D,), jnp.float32), 'out_proj_weight': jax.random.uniform(ks[4], (D, D), jnp.float32, -xav, xav), 'out_proj_bias': jnp.zeros((D,), jnp.float32), 'lambda_q1': 0.1 * jax.random.normal(ks[5], (SUB_HEAD_DIM,), jnp.float32), 'lambda_k1': 0.1 * jax.random.normal(ks[6], (SUB_HEAD_DIM,), jnp.float32), 'lambda_q2': 0.1 * jax.random.normal(ks[7], (SUB_HEAD_DIM,), jnp.float32), 'lambda_k2': 0.1 * jax.random.normal(ks[8], (SUB_HEAD_DIM,), jnp.float32)}
    _L3_xattn_all = _L3_xattn_setup()
    _L3_xattn_in = {k: v for k, v in _L3_xattn_all.items() if k in ('in_proj_weight', 'in_proj_bias', 'out_proj_weight', 'out_proj_bias', 'lambda_q1', 'lambda_k1', 'lambda_q2', 'lambda_k2')}
    del _L3_xattn_all

    def _L3_ffn_setup():
        import jax, jax.numpy as jnp
        import numpy as np
        D_MODEL = 128
        D_FF = 512
        N_ZONES = 8
        TOP_K = 3
        ROUTER_H = 32
        BATCH = 16
        SEQ = 256
        key = jax.random.key(seed)
        ks = jax.random.split(key, 8)
        s = lambda *dims: 1.0 / np.sqrt(dims[-2] if len(dims) > 1 else dims[-1])
        x = jax.random.normal(ks[0], (BATCH, SEQ, D_MODEL), dtype=jnp.float32)
        W1 = jax.random.normal(ks[1], (D_MODEL, ROUTER_H), dtype=jnp.float32) / np.sqrt(D_MODEL)
        b1 = jnp.zeros((ROUTER_H,), dtype=jnp.float32)
        W2 = jax.random.normal(ks[2], (ROUTER_H, N_ZONES), dtype=jnp.float32) / np.sqrt(ROUTER_H)
        b2 = jnp.zeros((N_ZONES,), dtype=jnp.float32)
        Wa = jax.random.normal(ks[3], (N_ZONES, D_MODEL, D_FF), dtype=jnp.float32) / np.sqrt(D_MODEL)
        Wb = jax.random.normal(ks[4], (N_ZONES, D_FF, D_MODEL), dtype=jnp.float32) / np.sqrt(D_FF)
        return {'x': x, 'W1': W1, 'b1': b1, 'W2': W2, 'b2': b2, 'Wa': Wa, 'Wb': Wb}
    _L3_ffn_all = _L3_ffn_setup()
    _L3_ffn_in = {k: v for k, v in _L3_ffn_all.items() if k in ('W1', 'b1', 'W2', 'b2', 'Wa', 'Wb')}
    del _L3_ffn_all
    return {'x': x, 'ctx_1024': ctx_1024, 'mask_Bx1xSxS2_bk0': mask_Bx1xSxS2_bk0, 'L0_xattn_w_q': _L0_xattn_in['w_q'], 'L0_xattn_b_q': _L0_xattn_in['b_q'], 'L0_xattn_w_k': _L0_xattn_in['w_k'], 'L0_xattn_b_k': _L0_xattn_in['b_k'], 'L0_xattn_w_v': _L0_xattn_in['w_v'], 'L0_xattn_b_v': _L0_xattn_in['b_v'], 'L0_xattn_w_o': _L0_xattn_in['w_o'], 'L0_xattn_b_o': _L0_xattn_in['b_o'], 'L0_ffn_gate_w': _L0_ffn_in['gate_w'], 'L0_ffn_w1': _L0_ffn_in['w1'], 'L0_ffn_w2': _L0_ffn_in['w2'], 'L1_xattn_Wi': _L1_xattn_in['Wi'], 'L1_xattn_bi': _L1_xattn_in['bi'], 'L1_xattn_Wg': _L1_xattn_in['Wg'], 'L1_xattn_bg': _L1_xattn_in['bg'], 'L1_xattn_A': _L1_xattn_in['A'], 'L1_xattn_Bm': _L1_xattn_in['Bm'], 'L1_xattn_Wo': _L1_xattn_in['Wo'], 'L1_xattn_bo': _L1_xattn_in['bo'], 'L1_xattn_decay': _L1_xattn_in['decay'], 'L1_ffn_q_w': _L1_ffn_in['q_w'], 'L1_ffn_q_b': _L1_ffn_in['q_b'], 'L1_ffn_k_w': _L1_ffn_in['k_w'], 'L1_ffn_k_b': _L1_ffn_in['k_b'], 'L1_ffn_v_w': _L1_ffn_in['v_w'], 'L1_ffn_v_b': _L1_ffn_in['v_b'], 'L1_ffn_o_w': _L1_ffn_in['o_w'], 'L1_ffn_o_b': _L1_ffn_in['o_b'], 'L1_ffn_router_w': _L1_ffn_in['router_w'], 'L1_ffn_router_b': _L1_ffn_in['router_b'], 'L1_ffn_w1': _L1_ffn_in['w1'], 'L1_ffn_b1': _L1_ffn_in['b1'], 'L1_ffn_w2': _L1_ffn_in['w2'], 'L1_ffn_b2': _L1_ffn_in['b2'], 'L2_xattn_Wq': _L2_xattn_in['Wq'], 'L2_xattn_bq': _L2_xattn_in['bq'], 'L2_xattn_Wk': _L2_xattn_in['Wk'], 'L2_xattn_bk': _L2_xattn_in['bk'], 'L2_xattn_Wv': _L2_xattn_in['Wv'], 'L2_xattn_bv': _L2_xattn_in['bv'], 'L2_xattn_Wo': _L2_xattn_in['Wo'], 'L2_xattn_bo': _L2_xattn_in['bo'], 'L2_ffn_t_emb': _L2_ffn_in['t_emb'], 'L2_ffn_sw1': _L2_ffn_in['sw1'], 'L2_ffn_sb1': _L2_ffn_in['sb1'], 'L2_ffn_sw3': _L2_ffn_in['sw3'], 'L2_ffn_sb3': _L2_ffn_in['sb3'], 'L2_ffn_sw2': _L2_ffn_in['sw2'], 'L2_ffn_sb2': _L2_ffn_in['sb2'], 'L2_ffn_w1': _L2_ffn_in['w1'], 'L2_ffn_b1': _L2_ffn_in['b1'], 'L2_ffn_w2': _L2_ffn_in['w2'], 'L2_ffn_b2': _L2_ffn_in['b2'], 'L3_xattn_in_proj_weight': _L3_xattn_in['in_proj_weight'], 'L3_xattn_in_proj_bias': _L3_xattn_in['in_proj_bias'], 'L3_xattn_out_proj_weight': _L3_xattn_in['out_proj_weight'], 'L3_xattn_out_proj_bias': _L3_xattn_in['out_proj_bias'], 'L3_xattn_lambda_q1': _L3_xattn_in['lambda_q1'], 'L3_xattn_lambda_k1': _L3_xattn_in['lambda_k1'], 'L3_xattn_lambda_q2': _L3_xattn_in['lambda_q2'], 'L3_xattn_lambda_k2': _L3_xattn_in['lambda_k2'], 'L3_ffn_W1': _L3_ffn_in['W1'], 'L3_ffn_b1': _L3_ffn_in['b1'], 'L3_ffn_W2': _L3_ffn_in['W2'], 'L3_ffn_b2': _L3_ffn_in['b2'], 'L3_ffn_Wa': _L3_ffn_in['Wa'], 'L3_ffn_Wb': _L3_ffn_in['Wb']}

def reference(x, ctx_1024, mask_Bx1xSxS2_bk0, L0_xattn_w_q, L0_xattn_b_q, L0_xattn_w_k, L0_xattn_b_k, L0_xattn_w_v, L0_xattn_b_v, L0_xattn_w_o, L0_xattn_b_o, L0_ffn_gate_w, L0_ffn_w1, L0_ffn_w2, L1_xattn_Wi, L1_xattn_bi, L1_xattn_Wg, L1_xattn_bg, L1_xattn_A, L1_xattn_Bm, L1_xattn_Wo, L1_xattn_bo, L1_xattn_decay, L1_ffn_q_w, L1_ffn_q_b, L1_ffn_k_w, L1_ffn_k_b, L1_ffn_v_w, L1_ffn_v_b, L1_ffn_o_w, L1_ffn_o_b, L1_ffn_router_w, L1_ffn_router_b, L1_ffn_w1, L1_ffn_b1, L1_ffn_w2, L1_ffn_b2, L2_xattn_Wq, L2_xattn_bq, L2_xattn_Wk, L2_xattn_bk, L2_xattn_Wv, L2_xattn_bv, L2_xattn_Wo, L2_xattn_bo, L2_ffn_t_emb, L2_ffn_sw1, L2_ffn_sb1, L2_ffn_sw3, L2_ffn_sb3, L2_ffn_sw2, L2_ffn_sb2, L2_ffn_w1, L2_ffn_b1, L2_ffn_w2, L2_ffn_b2, L3_xattn_in_proj_weight, L3_xattn_in_proj_bias, L3_xattn_out_proj_weight, L3_xattn_out_proj_bias, L3_xattn_lambda_q1, L3_xattn_lambda_k1, L3_xattn_lambda_q2, L3_xattn_lambda_k2, L3_ffn_W1, L3_ffn_b1, L3_ffn_W2, L3_ffn_b2, L3_ffn_Wa, L3_ffn_Wb):
    import jax
    import jax.numpy as jnp

    def _L0_xattn_ref(q, k, v, w_q, b_q, w_k, b_k, w_v, b_v, w_o, b_o):
        import jax, jax.numpy as jnp
        import numpy as np
        D_MODEL = 128
        H = 16
        D_K = D_MODEL // H
        B, S, _ = q.shape
        query = q @ w_q.T + b_q
        key_ = k @ w_k.T + b_k
        value = v @ w_v.T + b_v
        query = query.reshape(B, S, H, D_K).transpose(0, 2, 1, 3)
        key_ = key_.reshape(B, S, H, D_K).transpose(0, 2, 1, 3)
        value = value.reshape(B, S, H, D_K).transpose(0, 2, 1, 3)
        scores = jnp.einsum('bhqd,bhkd->bhqk', query, key_) / jnp.sqrt(jnp.asarray(D_K, query.dtype))
        attn = jax.nn.softmax(scores, axis=-1)
        x = jnp.einsum('bhqk,bhkd->bhqd', attn, value)
        x = x.transpose(0, 2, 1, 3).reshape(B, S, D_MODEL)
        return x @ w_o.T + b_o

    def _L0_ffn_ref(x, gate_w, w1, w2):
        import jax, jax.numpy as jnp
        import numpy as np
        N, T, D = (4, 512, 128)
        NUM_EXPERTS = 8
        EXPERT_CAP = 2.0
        MLP_RATIO = 4
        HIDDEN = MLP_RATIO * D
        x = x.astype(jnp.float32)
        n, t, d = x.shape
        k = int(EXPERT_CAP * t / NUM_EXPERTS)
        scores = jnp.einsum('ntd,de->nte', x, gate_w)
        probs = jax.nn.softmax(scores, axis=-1)
        probs = jnp.transpose(probs, (0, 2, 1))
        g, m = jax.lax.top_k(probs, k)
        xin = jax.vmap(lambda xb, mb: xb[mb])(x, m)
        h = jax.nn.gelu(jnp.einsum('nekd,edf->nekf', xin, w1))
        h = jnp.einsum('nekf,efd->nekd', h, w2)
        weighted = g[..., None] * h
        flat_idx = (m + jnp.arange(n, dtype=m.dtype)[:, None, None] * t).reshape(-1)
        out = jnp.zeros((n * t, d), dtype=jnp.float32).at[flat_idx].add(weighted.reshape(-1, d))
        out = out.reshape(n, t, d)
        return out.astype(jnp.bfloat16)

    def _L1_xattn_ref(q, k, v, Wi, bi, Wg, bg, A, Bm, Wo, bo, decay):
        import jax, jax.numpy as jnp
        import numpy as np
        from jax import lax
        NUM_HEADS = 16
        DIM = 128
        BATCH = 4
        SEQ = 256
        B, S, D = q.shape
        H = decay.shape[1]
        hd = D // H
        qh = jnp.moveaxis(q.reshape(B, S, H, hd), 1, 0)
        kh = jnp.moveaxis(k.reshape(B, S, H, hd), 1, 0)
        vh = jnp.moveaxis(v.reshape(B, S, H, hd), 1, 0)

        def step(carry, xs):
            r, state = carry
            qt, kt, vt = xs
            r = decay * r + kt * vt
            retained = (qt * r).reshape(B, D)
            inp = retained @ Wi.T + bi
            gate = jax.nn.sigmoid(inp @ Wg.T + bg)
            blended = gate * state + (1.0 - gate) * inp
            state = jnp.tanh(blended @ A.T + inp @ Bm.T)
            out = state @ Wo.T + bo
            return ((r, state), out)
        r0 = jnp.zeros((B, H, hd), dtype=q.dtype)
        s0 = jnp.zeros((B, D), dtype=q.dtype)
        _, outs = lax.scan(step, (r0, s0), (qh, kh, vh))
        return jnp.moveaxis(outs, 0, 1)

    def _L1_ffn_ref(hidden_states, q_w, q_b, k_w, k_b, v_w, v_b, o_w, o_b, router_w, router_b, w1, b1, w2, b2):
        import jax, jax.numpy as jnp
        import numpy as np
        import math
        D = 128
        H = 16
        E = 8
        TOPK = 2
        LAT = D // 2
        KPH = LAT // H
        HD = D // H

        def _forward(hs, q_w, q_b, k_w, k_b, v_w, v_b, o_w, o_b, router_w, router_b, w1, b1, w2, b2):
            B, S, _ = hs.shape
            Q = (hs @ q_w + q_b).reshape(B, S, H, HD).transpose(0, 2, 1, 3)
            K = (hs @ k_w + k_b).reshape(B, S, H, KPH).transpose(0, 2, 1, 3)
            V = (hs @ v_w + v_b).reshape(B, S, H, KPH).transpose(0, 2, 1, 3)
            scores = jnp.einsum('bhsk,bhtk->bhst', Q[..., :KPH], K) / math.sqrt(KPH)
            attn = jax.nn.softmax(scores, axis=-1)
            ao = jnp.einsum('bhst,bhtv->bhsv', attn, V)
            ao = ao.transpose(0, 2, 1, 3).reshape(B, S, H * KPH)
            ao = jnp.concatenate([ao, jnp.zeros((B, S, D - LAT), ao.dtype)], axis=-1)
            mla_out = ao @ o_w + o_b
            probs = jax.nn.softmax(mla_out @ router_w + router_b, axis=-1)
            topw, topi = jax.lax.top_k(probs, TOPK)
            topw = topw / (topw.sum(-1, keepdims=True) + 1e-08)
            combine = jnp.sum(jax.nn.one_hot(topi, E, dtype=probs.dtype) * topw[..., None], axis=-2)
            h1 = jnp.einsum('bsd,edf->ebsf', mla_out, w1) + b1[:, None, None, :]
            h1 = jax.nn.gelu(h1, approximate=False)
            h2 = jnp.einsum('ebsf,efd->ebsd', h1, w2) + b2[:, None, None, :]
            moe_out = jnp.einsum('bse,ebsd->bsd', combine, h2)
            return hs + 0.3 * moe_out
        return _forward(hidden_states, q_w, q_b, k_w, k_b, v_w, v_b, o_w, o_b, router_w, router_b, w1, b1, w2, b2)

    def _L2_xattn_ref(Q, K, V, mask, Wq, bq, Wk, bk, Wv, bv, Wo, bo):
        import jax, jax.numpy as jnp
        import numpy as np
        D = 128
        H = 16
        B = 4
        S = 256
        NEG = -1000000000.0
        d = D // H

        def split(x):
            Bx, Sx, _ = x.shape
            return x.reshape(Bx, Sx, H, d).transpose(0, 2, 1, 3)
        q = split(Q @ Wq + bq)
        k = split(K @ Wk + bk)
        v = split(V @ Wv + bv)
        scores = jnp.einsum('bhsd,bhtd->bhst', q, k) / jnp.sqrt(jnp.float32(d))
        scores = jnp.where(mask, scores, NEG)
        attn = jax.nn.softmax(scores, axis=-1)
        out = jnp.einsum('bhst,bhtd->bhsd', attn, v)
        out = out.transpose(0, 2, 1, 3).reshape(Q.shape[0], Q.shape[1], D)
        return out @ Wo + bo

    def _L2_ffn_ref(x, t_emb, sw1, sb1, sw3, sb3, sw2, sb2, w1, b1, w2, b2):
        import jax, jax.numpy as jnp
        import numpy as np
        E = 8
        TOPK = 2
        PRIME = 11
        HASH_OFF = 7919
        N_SHARED = 1
        B, T, C = x.shape
        N = B * T
        xf = x.reshape(N, C)
        shared = jax.nn.silu(xf @ sw1 + sb1) * (xf @ sw3 + sb3) @ sw2 + sb2
        tok = jnp.arange(N)
        out = jnp.zeros((N, C), x.dtype)
        for k in range(TOPK):
            exp_ids = (tok * PRIME + k * HASH_OFF) % E
            sort_idx = jnp.argsort(exp_ids)
            xs = xf[sort_idx].reshape(E, N // E, C)
            h = jax.nn.gelu(jnp.einsum('enc,ech->enh', xs, w1) + b1[:, None, :], approximate=False)
            y = jnp.einsum('enh,ehc->enc', h, w2) + b2[:, None, :]
            out = out.at[sort_idx].add(y.reshape(N, C))
        out = out / TOPK
        return ((shared + out) / (N_SHARED + 1)).reshape(B, T, C)

    def _L3_xattn_ref(query, key, value, in_proj_weight, in_proj_bias, out_proj_weight, out_proj_bias, lambda_q1, lambda_k1, lambda_q2, lambda_k2):
        import jax, jax.numpy as jnp
        import numpy as np
        import math
        EMBED_DIM = 128
        NUM_HEADS = 16
        HEAD_DIM = EMBED_DIM // NUM_HEADS
        SUB_HEAD_DIM = HEAD_DIM // 2
        SCALING = 1.0 / math.sqrt(SUB_HEAD_DIM)
        LAMBDA_INIT = 0.8 - 0.6 * math.exp(-0.3 * 0)
        B, T, D = query.shape
        S = key.shape[1]
        H, hd, sd = (NUM_HEADS, HEAD_DIM, SUB_HEAD_DIM)
        qw, kw, vw = jnp.split(in_proj_weight, 3, axis=0)
        qb, kb, vb = jnp.split(in_proj_bias, 3, axis=0)
        q = query @ qw.T + qb
        k = key @ kw.T + kb
        v = value @ vw.T + vb
        q = q.reshape(B, T, H, hd).transpose(0, 2, 1, 3)
        k = k.reshape(B, S, H, hd).transpose(0, 2, 1, 3)
        v = v.reshape(B, S, H, hd).transpose(0, 2, 1, 3)
        q1, q2 = (q[..., :sd], q[..., sd:])
        k1, k2 = (k[..., :sd], k[..., sd:])
        logits_1 = jnp.einsum('bhtd,bhsd->bhts', q1, k1) * SCALING
        logits_2 = jnp.einsum('bhtd,bhsd->bhts', q2, k2) * SCALING
        a1 = jax.nn.softmax(logits_1, axis=-1)
        a2 = jax.nn.softmax(logits_2, axis=-1)
        lam = jnp.exp(jnp.dot(lambda_q1, lambda_k1)) - jnp.exp(jnp.dot(lambda_q2, lambda_k2)) + LAMBDA_INIT
        diff_weights = a1 - lam * a2
        attn_output = jnp.einsum('bhts,bhsd->bhtd', diff_weights, v)
        attn_output = attn_output * (1.0 - LAMBDA_INIT)
        attn_output = attn_output.transpose(0, 2, 1, 3).reshape(B, T, D)
        output = attn_output @ out_proj_weight.T + out_proj_bias
        return output

    def _L3_ffn_ref(x, W1, b1, W2, b2, Wa, Wb):
        import jax, jax.numpy as jnp
        import numpy as np
        D_MODEL = 128
        D_FF = 512
        N_ZONES = 8
        TOP_K = 3
        ROUTER_H = 32
        BATCH = 16
        SEQ = 256
        pooled = x.mean(axis=1)
        h = jnp.tanh(pooled @ W1 + b1)
        logits = h @ W2 + b2
        probs = jax.nn.softmax(logits, axis=-1)
        top_p, top_i = jax.lax.top_k(probs, TOP_K)
        top_w = top_p / top_p.sum(axis=-1, keepdims=True)
        onehot = jax.nn.one_hot(top_i, N_ZONES, dtype=x.dtype)
        w = jnp.einsum('bk,bke->be', top_w, onehot)
        zone_outputs = jnp.zeros_like(x)
        for e in range(N_ZONES):
            z = jax.nn.gelu(x @ Wa[e]) @ Wb[e]
            zone_outputs = zone_outputs + z * w[:, e, None, None]
        return x + zone_outputs
    x = x + _L0_xattn_ref(_layernorm(x, axis=-1), ctx_1024, ctx_1024, L0_xattn_w_q, L0_xattn_b_q, L0_xattn_w_k, L0_xattn_b_k, L0_xattn_w_v, L0_xattn_b_v, L0_xattn_w_o, L0_xattn_b_o)
    x = x + _L0_ffn_ref(_layernorm(x, axis=-1), L0_ffn_gate_w, L0_ffn_w1, L0_ffn_w2)
    x = x + _L1_xattn_ref(_layernorm(x, axis=-1), ctx_1024, ctx_1024, L1_xattn_Wi, L1_xattn_bi, L1_xattn_Wg, L1_xattn_bg, L1_xattn_A, L1_xattn_Bm, L1_xattn_Wo, L1_xattn_bo, L1_xattn_decay)
    x = x + _L1_ffn_ref(_layernorm(x, axis=-1), L1_ffn_q_w, L1_ffn_q_b, L1_ffn_k_w, L1_ffn_k_b, L1_ffn_v_w, L1_ffn_v_b, L1_ffn_o_w, L1_ffn_o_b, L1_ffn_router_w, L1_ffn_router_b, L1_ffn_w1, L1_ffn_b1, L1_ffn_w2, L1_ffn_b2)
    x = x + _L2_xattn_ref(_layernorm(x, axis=-1), ctx_1024, ctx_1024, mask_Bx1xSxS2_bk0, L2_xattn_Wq, L2_xattn_bq, L2_xattn_Wk, L2_xattn_bk, L2_xattn_Wv, L2_xattn_bv, L2_xattn_Wo, L2_xattn_bo)
    x = x + _L2_ffn_ref(_layernorm(x, axis=-1), L2_ffn_t_emb, L2_ffn_sw1, L2_ffn_sb1, L2_ffn_sw3, L2_ffn_sb3, L2_ffn_sw2, L2_ffn_sb2, L2_ffn_w1, L2_ffn_b1, L2_ffn_w2, L2_ffn_b2)
    x = x + _L3_xattn_ref(_layernorm(x, axis=-1), ctx_1024, ctx_1024, L3_xattn_in_proj_weight, L3_xattn_in_proj_bias, L3_xattn_out_proj_weight, L3_xattn_out_proj_bias, L3_xattn_lambda_q1, L3_xattn_lambda_k1, L3_xattn_lambda_q2, L3_xattn_lambda_k2)
    x = x + _L3_ffn_ref(_layernorm(x, axis=-1), L3_ffn_W1, L3_ffn_b1, L3_ffn_W2, L3_ffn_b2, L3_ffn_Wa, L3_ffn_Wb)
    return x

_drawn_inputs = setup_inputs


def setup_inputs(seed=0):
    import zlib

    import numpy as np

    out = dict(_drawn_inputs(seed))
    spreads = {'L0_xattn_b_q': (0.0, 0.1),
     'L0_xattn_b_k': (0.0, 2.0),
     'L0_xattn_b_v': (0.0, 0.1),
     'L0_xattn_b_o': (0.0, 0.1),
     'L1_xattn_decay': (0.8999999761581421, 0.2),
     'L1_ffn_q_b': (0.0, 0.8),
     'L1_ffn_k_b': (0.0, 2.0),
     'L1_ffn_v_b': (0.0, 0.8),
     'L1_ffn_o_b': (0.0, 0.8),
     'L1_ffn_router_b': (0.0, 0.377),
     'L1_ffn_b1': (0.0, 0.8),
     'L1_ffn_b2': (0.0, 0.467),
     'L2_xattn_bq': (0.0, 2.0),
     'L2_xattn_bk': (0.0, 2.0),
     'L2_xattn_bv': (0.0, 0.368),
     'L2_xattn_bo': (0.0, 0.1),
     'L2_ffn_sb1': (0.0, 0.383),
     'L2_ffn_sb3': (0.0, 0.316),
     'L2_ffn_sb2': (0.0, 0.294),
     'L2_ffn_b1': (0.0, 0.336),
     'L2_ffn_b2': (0.0, 0.401),
     'L3_xattn_in_proj_bias': (0.0, 0.1),
     'L3_xattn_out_proj_bias': (0.0, 0.1),
     'L3_ffn_b1': (0.0, 0.1),
     'L3_ffn_b2': (0.0, 0.1)}
    factors = {'L1_xattn_bi': 7.069,
     'L1_xattn_bg': 8.0,
     'L1_ffn_q_w': 8.0,
     'L1_ffn_k_w': 8.0,
     'L1_ffn_v_w': 8.0,
     'L1_ffn_o_w': 8.0,
     'L1_ffn_router_w': 8.0,
     'L1_ffn_w1': 8.0,
     'L1_ffn_w2': 5.576,
     'L2_xattn_Wq': 8.0,
     'L2_xattn_Wk': 8.0,
     'L2_xattn_Wv': 2.764,
     'L3_xattn_lambda_q1': 7.816,
     'L3_xattn_lambda_k1': 7.816,
     'L3_xattn_lambda_q2': 6.865,
     'L3_xattn_lambda_k2': 6.865}
    for name, (base, spread) in spreads.items():
        noise = np.random.default_rng([zlib.crc32(name.encode()), seed]).standard_normal(out[name].shape)
        drawn = base * np.exp(spread * noise) if base else spread * noise
        out[name] = jnp.asarray(drawn.astype(out[name].dtype))
    for name, factor in factors.items():
        out[name] = (out[name] * factor).astype(out[name].dtype)
    return out
```

```python
from contextlib import ExitStack

import numpy as np
import concourse.bass as bass
from concourse import mybir
from concourse.alu_op_type import AluOpType as ALU

F32 = mybir.dt.float32
F16 = mybir.dt.float16
BF16 = mybir.dt.bfloat16
U32 = mybir.dt.uint32
I32 = mybir.dt.int32
U8 = mybir.dt.uint8
ACT = mybir.ActivationFunctionType
AX = mybir.AxisListType

P = 128
B = 32
D = 128
H = 16
E = 8
EPS = 1e-5
NEG = -1.0e9
LAMBDA_INIT = 0.2
HASHED = [[(11 * r + k * 7919) % 8 for r in range(8)] for k in range(2)]

MATS = ["a0_q", "a0_k", "a0_v", "a0_o", "r_wi", "r_wg", "r_a", "r_bm", "r_wo", "a1_q", "a1_k", "a1_v", "a1_o",
        "a2_q", "a2_k", "a2_v", "a2_o", "a3_q", "a3_k", "a3_v", "a3_o", "ident", "tri"]
COLS = ["a0_q", "a0_k", "a1_q", "a1_k", "a1_o", "a2_q", "a2_k", "a3_q", "a3_k", "r_bi", "r_bg", "decay",
        "sb1_0", "sb1_1", "sb3_0", "sb3_1"] + [f"m_b1_{i}" for i in range(16)]
ROWS = ["a0_v", "a0_o", "a1_v", "a2_v", "a2_o", "a3_v", "a3_o", "r_bo", "router_b", "z_b1", "z_b2"]


class Chain:

    def __init__(self, eng, sem, at=0):
        self.eng, self.sem, self.at, self.n = eng, sem, at, 0

    def link(self, ins):
        ins.then_inc(self.sem, 1)
        self.n += 1
        self.eng.wait_ge(self.sem, self.at + self.n)

    def __call__(self, ins):
        self.link(ins)


class Semaphores:

    def __init__(self, nc, ctx, name):
        self.nc, self.ctx, self.name, self.taken = nc, ctx, name, []

    def __call__(self, n):
        self.taken.append(self.ctx.enter_context(self.nc.semaphore(f"{self.name}_{n}")))
        return self.taken[-1]

    def clear(self):
        with self.nc.Block() as block:

            @block.gpsimd
            def _(pool):
                for s in self.taken:
                    pool.sem_clear(s)


def wait(eng, sem, value):
    if isinstance(value, int) and value < 1:
        return
    eng.wait_ge(sem, value)


def over_batches(eng, step, n=B):
    step(0, 0)
    step(1, 1)
    with eng.Fori(1, n // 2 - 1) as i:
        for u in range(2):
            step(2 * i + u, u)
    step(n - 2, 0, n - 1)
    step(n - 1, 1, n - 1)


def attention(nc, m, name, nsub, hd, vd, scale, own, masked, differs, ends, sel, ahead=(), ahead_in=None):
    nblk = nsub // 4
    NH = nblk // 4
    NQ = nblk
    R = 3 * hd
    V1 = vd + 1
    VW = H * vd
    with ExitStack() as ctx:
        def sb(n, shape, dt):
            return ctx.enter_context(nc.sbuf_tensor(f"{name}_{n}", shape, dt))

        def ps(n, shape, dt=F32):
            return ctx.enter_context(nc.psum_tensor(f"{name}_{n}", shape, dt))

        sem = Semaphores(nc, ctx, name)

        selq, selk = m[sel]
        xn = sb("xn", [P, 2, D], F32)
        xb = sb("xb", [P, 2, D], F32)
        xnT = sb("xnT", [P, 2, P], F32)
        src = xnT if own else sb("ctxs", [P, 2, P], F32)
        hi = sb("hi", [P, 2, 2, P], F16)
        lo = sb("lo", [P, 2, 2, P], F16)
        qst = sb("qst", [P, 2, nblk, P], F16)
        kst = sb("kst", [P, 2, nblk, P], F16)
        vx = sb("vx", [P, 2, H, V1], F32)
        mx = sb("mx", [P, 2, 4], BF16)
        pr = sb("pr", [P, 2, 4, P], F32)
        rec = sb("rec", [P, nsub], F32)
        on = sb("on", [P, 2, D], F32)
        on2 = sb("on2", [P, D], F32)
        oT = sb("oT", [P, 2, P], F32)
        lnv = sb("lnv", [P, 6, B], F32)
        rstd = sb("rstd", [P, B], F32)
        nmr = sb("nmr", [P, B], F32)
        qm = sb("qm", [P, 2, P], F32) if masked else None
        nbq = sb("nbq", [P, 2, P], BF16) if masked else None
        nbk = sb("nbk", [P, 2, P], BF16) if masked else None
        keepb = sb("keepb", [P, 2, P], BF16) if masked else None
        anyq = sb("anyq", [P, 2], F32) if masked else None
        anyb = sb("anyb", [P, 2, P], F32) if masked else None
        mT = sb("mT", [P, 2, P], F32) if ends == "moe" else None

        s_ps = ps("s", [P, 2, 4, P])
        st_ps = ps("st", [P, 2, 4, P])
        stack_ps = ps("stack", [P, 4, P])
        q_ps = ps("q", [P, 4, P])
        k_ps = ps("k", [P, 4, P])
        o_ps = ps("o", [P, 512])
        o_h = o_ps[:, 0:nsub * V1].rearrange("p (h c) -> p h c", c=V1)

        ln_ready = sem("ln_ready")
        pow_ready = sem("pow_ready")
        xn_ready, xT_done, xnT_ready = sem("xn_ready"), sem("xT_done"), sem("xnT_ready")
        src_ready, xb_ready = sem("src_ready"), sem("xb_ready")
        kv_done, q_done = sem("kv_done"), sem("q_done")
        khi, klo, qhi, qlo, v_ready = sem("khi"), sem("klo"), sem("qhi"), sem("qlo"), sem("v_ready")
        kstack, qstack, kst_ready, qst_ready = sem("kstack"), sem("qstack"), sem("kst_ready"), sem("qst_ready")
        s_done, mx_ready, st_done, exp_done, pv_done = (sem("s_done"), sem("mx_ready"), sem("st_done"),
                                                        sem("exp_done"), sem("pv_done"))
        on_done, oT_done, oT_ready, y_done, x_done = (sem("on_done"), sem("oT_done"), sem("oT_ready"),
                                                      sem("y_done"), sem("x_done"))
        steps, ones_set = sem("steps"), sem("ones_set")
        mask_ready, cnt_done, any_ready = sem("mask_ready"), sem("cnt_done"), sem("any_ready")
        mT_ready, lg_done, lg_ready, mT_kept = sem("mT_ready"), sem("lg_done"), sem("lg_ready"), sem("mT_kept")
        x_sum, nbk_ready, qm_ready = sem("x_sum"), sem("nbk_ready"), sem("qm_ready")

        def nxt(b, last):
            return not (isinstance(b, int) and b == last)

        with nc.Block() as block:

            @block.sync
            def _(sp):
                if ahead:
                    sp.wait_ge(m["weights_in"], m["weights_count"])
                for to, frm in ahead:
                    sp.dma_start(to, frm).then_inc(ahead_in, 16)

            @block.gpsimd
            def _(pool):
                pool.memset(vx[:], 1.0).then_inc(ones_set, 1)
                pool.memset(on[:], 0.0).then_inc(ones_set, 1)
                pool.memset(lnv[:, 5, :], -0.5).then_inc(ones_set, 1)
                pool.wait_ge(ones_set, 3)
                pool.wait_ge(ln_ready, 1)
                nc.gpsimd.tensor_tensor(rstd[:], lnv[:, 4, :], lnv[:, 5, :], ALU.pow).then_inc(pow_ready, 1)

                def step(b, u, last=None):
                    if own:
                        pool.wait_ge(xn_ready, b + 1)
                        nc.gpsimd.tensor_tensor(m["x"][:, b, :], m["x"][:, b, :], xn[:, u, :], ALU.add).then_inc(x_sum, 1)
                        pool.wait_ge(mT_ready, b + 1)
                        nc.gpsimd.tensor_copy(m["big"][:, b, :], mT[:, u, :]).then_inc(mT_kept, 1)
                    else:
                        wait(pool, kv_done, b - 1)
                        nc.gpsimd.tensor_copy(src[:, u, :], m["ctxT"][:, b, :]).then_inc(src_ready, 1)
                        wait(pool, x_done, b - 1)
                        nc.gpsimd.tensor_tensor(xb[:, u, :], m["x"][:, b, :], m["row"][f"{name}_o"], ALU.add)\
                            .then_inc(xb_ready, 1)

                over_batches(pool, step)

            @block.vector
            def _(dve):
                layernorm_stats(nc, dve, m, lnv, rstd, nmr, steps, ln_ready, pow_ready)
                LN = LN_STEPS
                per = 5 if differs else 1

                def normalise(b, u):
                    wait(dve, xT_done, b - 1)
                    if own:
                        wait(dve, x_sum, b - 1)
                    dve.tensor_scalar(xn[:, u, :], m["x"][:, b, :], rstd[:, bass.ds(b, 1)], nmr[:, bass.ds(b, 1)],
                                      ALU.mult, ALU.add).then_inc(xn_ready, 1)

                def mask_tiles(b, u):
                    wait(dve, s_done, NQ * (b - 1))
                    wait(dve, st_done, NQ * (b - 1))
                    c = Chain(dve, mask_ready, 3 * b)
                    c(dve.tensor_reduce(anyq[:, u:u + 1], m["maskq"][:, b, :], AX.X, ALU.max))
                    c(dve.tensor_scalar(nbq[:, u, :], m["maskq"][:, b, :], -1.0, -NEG, ALU.add, ALU.mult))
                    dve.tensor_copy(keepb[:, u, :], m["maskk"][:, b, :]).then_inc(mask_ready, 1)

                def mask_rows(b, u):
                    dve.wait_ge(cnt_done, b + 1)
                    dve.wait_ge(xnT_ready, b + 1)
                    c = Chain(dve, any_ready, 3 * b)
                    c(dve.tensor_scalar(anyb[:, u, :], q_ps[:, 2, :], 1.0, None, ALU.min))
                    dve.tensor_scalar(nbq[:, u, :], nbq[:, u, :], anyq[:, u:u + 1], None, ALU.mult).then_inc(any_ready, 1)
                    dve.wait_ge(mask_ready, 3 * b + 3)
                    dve.scalar_tensor_tensor(nbk[:, u, :], keepb[:, u, :], -1.0, anyb[:, u, :], ALU.add, ALU.mult)\
                        .then_inc(any_ready, 1)
                    dve.wait_ge(any_ready, 3 * b + 3)
                    dve.tensor_scalar(nbk[:, u, :], nbk[:, u, :], -NEG, None, ALU.mult).then_inc(nbk_ready, 1)

                def k_low(b, u):
                    dve.wait_ge(khi, b + 1)
                    wait(dve, kstack, NH * (b - 1))
                    dve.scalar_tensor_tensor(lo[:, u, 1, :], k_ps[:, 0, :], m["col"][f"{name}_k"], hi[:, u, 1, :],
                                             ALU.add, ALU.subtract).then_inc(klo, 1)

                def v_bias(b, u):
                    dve.wait_ge(khi, b + 1)
                    wait(dve, pv_done, NQ * (b - 1))
                    dve.wait_ge(ones_set, 3)
                    dve.tensor_tensor(vx[:, u, :, 0:vd], k_ps[:, 1, 0:VW].rearrange("p (h c) -> p h c", c=vd),
                                      m["row"][f"{name}_v"][:, 0:VW].rearrange("p (h c) -> p h c", c=vd), ALU.add)\
                        .then_inc(v_ready, 1)

                def q_low(b, u):
                    if masked:
                        dve.wait_ge(q_done, b + 1)
                        dve.wait_ge(any_ready, 3 * b + 3)
                        wait(dve, qhi, b - 1)
                        dve.scalar_tensor_tensor(qm[:, u, :], q_ps[:, 1, :], m["col"][f"{name}_q"], anyb[:, u, :],
                                                 ALU.add, ALU.mult).then_inc(qm_ready, 1)
                        dve.wait_ge(qm_ready, b + 1)
                        dve.wait_ge(qhi, b + 1)
                        wait(dve, qstack, NH * (b - 1))
                        dve.tensor_tensor(lo[:, u, 0, :], qm[:, u, :], hi[:, u, 0, :], ALU.subtract).then_inc(qlo, 1)
                        return
                    dve.wait_ge(qhi, b + 1)
                    wait(dve, qstack, NH * (b - 1))
                    dve.scalar_tensor_tensor(lo[:, u, 0, :], q_ps[:, 1, :], m["col"][f"{name}_q"], hi[:, u, 0, :],
                                             ALU.add, ALU.subtract).then_inc(qlo, 1)

                def q_keep(b, u, half):
                    dve.wait_ge(qstack, NH * b + half + 1)
                    wait(dve, st_done, NQ * (b - 1))
                    dve.tensor_copy(qst[:, u, 4 * half:4 * half + 4, :], stack_ps[:]).then_inc(qst_ready, 1)

                def maximum(b, j):
                    n = NQ * b + j
                    dve.wait_ge(s_done, n + 1)
                    wait(dve, st_done, n - 1)
                    dve.tensor_reduce(mx[:, j % 2, :], s_ps[:, j % 2], AX.X, ALU.max).then_inc(mx_ready, 1)

                def divide(b, u):
                    dve.wait_ge(pv_done, NQ * (b + 1))
                    wait(dve, oT_done, b - 1)
                    c = Chain(dve, steps, LN + per * b)
                    c(dve.reciprocal(rec[:], o_h[:, :, vd]))
                    out = on[:, u, 0:VW].rearrange("p (h c) -> p h c", c=vd)
                    if differs:
                        o4 = o_h.rearrange("p (h s) c -> p h s c", s=2)
                        r4 = rec[:].rearrange("p (h s) -> p h s", s=2)
                        c(dve.tensor_scalar(rec[:], rec[:], 1.0 - LAMBDA_INIT, None, ALU.mult))
                        c(dve.tensor_tensor(r4[:, :, 1], r4[:, :, 1], m["lam"][:, 0:1].broadcast_to([P, H]), ALU.mult))
                        c(dve.tensor_tensor(on2[:].rearrange("p (h c) -> p h c", c=vd), o4[:, :, 1, 0:vd],
                                            r4[:, :, 1].unsqueeze(2).broadcast_to([P, H, vd]), ALU.mult))
                        c(dve.tensor_tensor(out, o4[:, :, 0, 0:vd], r4[:, :, 0].unsqueeze(2).broadcast_to([P, H, vd]), ALU.mult))
                        dve.scalar_tensor_tensor(on[:, u, :], on2[:], -1.0, on[:, u, :], ALU.mult, ALU.add).then_inc(on_done, 1)
                    else:
                        dve.tensor_tensor(out, o_h[:, :, 0:vd], rec[:].unsqueeze(2).broadcast_to([P, H, vd]), ALU.mult)\
                            .then_inc(on_done, 1)

                def finish(b, u):
                    if own:
                        dve.wait_ge(lg_done, b + 1)
                        dve.tensor_tensor(m["logits"][:, b, :], k_ps[:, 0, 0:E], m["row"]["router_b"][:, 0:E], ALU.add)\
                            .then_inc(lg_ready, 1)
                        return
                    dve.wait_ge(y_done, b + 1)
                    dve.wait_ge(xb_ready, b + 1)
                    dve.tensor_tensor(m["x"][:, b, :], k_ps[:, 3, :], xb[:, u, :], ALU.add).then_inc(x_done, 1)
                    dve.wait_ge(x_done, b + 1)
                    dve.bn_stats(m["stats"][:, b, :], m["x"][:, b, :])

                def prepare(b, u, j):
                    if j == 0:
                        normalise(b, u)
                        if masked:
                            mask_tiles(b, u)
                    if j == 1:
                        if masked:
                            mask_rows(b, u)
                        v_bias(b, u)
                        k_low(b, u)
                    if j == 2:
                        q_low(b, u)
                    if j == 3:
                        for half in range(NH):
                            q_keep(b, u, half)

                for j in range(4):
                    prepare(0, 0, j)

                def step(b, u, last=None):
                    more, before = nxt(b, last), nxt(b, 0)
                    if more:
                        prepare(b + 1, 1 - u, 0)
                    maximum(b, 0)
                    if before:
                        divide(b - 1, 1 - u)
                    if more:
                        prepare(b + 1, 1 - u, 1)
                    maximum(b, 1)
                    if more:
                        prepare(b + 1, 1 - u, 2)
                    maximum(b, 2)
                    if NQ == 4:
                        if more:
                            prepare(b + 1, 1 - u, 3)
                        if before:
                            finish(b - 1, 1 - u)
                        maximum(b, 3)
                    else:
                        maximum(b, 3)
                        if before:
                            finish(b - 1, 1 - u)
                        maximum(b, 4)
                        if more:
                            q_keep(b + 1, 1 - u, 0)
                        maximum(b, 5)
                        if more:
                            q_keep(b + 1, 1 - u, 1)
                        maximum(b, 6)
                        maximum(b, 7)

                over_batches(dve, step)
                divide(B - 1, 1)
                finish(B - 1, 1)

            @block.scalar
            def _(act):
                act.preload_act_table(ACT.Exp)

                def x_keep(b, u):
                    act.wait_ge(xT_done, b + 1)
                    wait(act, q_done, b - 1)
                    if own:
                        wait(act, kv_done, b - 1)
                    act.activation(xnT[:, u, :], q_ps[:, 0, :], ACT.Copy).then_inc(xnT_ready, 1)

                def k_high(b, u):
                    act.wait_ge(kv_done, b + 1)
                    wait(act, kstack, NH * (b - 1))
                    act.activation(hi[:, u, 1, :], k_ps[:, 0, :], ACT.Identity, bias=m["col"][f"{name}_k"]).then_inc(khi, 1)

                def q_high(b, u):
                    wait(act, qstack, NH * (b - 1))
                    if masked:
                        act.wait_ge(qm_ready, b + 1)
                        act.activation(hi[:, u, 0, :], qm[:, u, :], ACT.Copy).then_inc(qhi, 1)
                        return
                    act.wait_ge(q_done, b + 1)
                    act.activation(hi[:, u, 0, :], q_ps[:, 1, :], ACT.Identity, bias=m["col"][f"{name}_q"]).then_inc(qhi, 1)

                def k_keep(b, u, half):
                    act.wait_ge(kstack, NH * b + half + 1)
                    wait(act, st_done, NQ * (b - 1))
                    act.activation(kst[:, u, 4 * half:4 * half + 4, :], stack_ps[:], ACT.Copy).then_inc(kst_ready, 1)

                def exp(b, j):
                    n = NQ * b + j
                    act.wait_ge(st_done, n + 1)
                    wait(act, pv_done, n - 1)
                    act.activation(pr[:, j % 2], st_ps[:, j % 2], ACT.Exp, scale=scale).then_inc(exp_done, 1)

                def o_keep(b, u):
                    act.wait_ge(oT_done, b + 1)
                    wait(act, y_done, b - 1)
                    act.activation(oT[0:VW, u, :], k_ps[0:VW, 2, :], ACT.Copy).then_inc(oT_ready, 1)

                def m_keep(b, u):
                    act.wait_ge(y_done, b + 1)
                    wait(act, lg_done, b - 1)
                    wait(act, mT_kept, b - 1)
                    act.activation(mT[:, u, :], k_ps[:, 3, :], ACT.Identity, bias=m["col"]["a1_o"]).then_inc(mT_ready, 1)

                def prepare(b, u, j):
                    if j == 0:
                        x_keep(b, u)
                        k_high(b, u)
                    if j == 1:
                        q_high(b, u)
                        k_keep(b, u, 0)

                for j in range(2):
                    prepare(0, 0, j)
                if NH == 2:
                    k_keep(0, 0, 1)

                def step(b, u, last=None):
                    more, before = nxt(b, last), nxt(b, 0)
                    exp(b, 0)
                    if more:
                        prepare(b + 1, 1 - u, 0)
                    exp(b, 1)
                    if more:
                        prepare(b + 1, 1 - u, 1)
                    if before:
                        o_keep(b - 1, 1 - u)
                    exp(b, 2)
                    if more and NH == 2:
                        k_keep(b + 1, 1 - u, 1)
                    if before and own:
                        m_keep(b - 1, 1 - u)
                    for j in range(3, NQ):
                        exp(b, j)

                over_batches(act, step)
                o_keep(B - 1, 1)
                if own:
                    m_keep(B - 1, 1)

            @block.tensor
            def _(pe):
                def x_turn(b, u):
                    pe.wait_ge(xn_ready, b + 1)
                    wait(pe, qlo, b)
                    pe.transpose(q_ps[:, 0, :], xn[:, u, :], m["mat"]["ident"]).then_inc(xT_done, 1)

                def k_dense(b, u):
                    pe.wait_ge(xnT_ready if own else src_ready, b + 1)
                    wait(pe, klo, b)
                    wait(pe, lg_ready if own else x_done, b - 2)
                    pe.matmul(k_ps[:, 0, :], m["mat"][f"{name}_k"], src[:, u, :], start=True, stop=True)
                    pe.matmul(k_ps[:, 1, 0:VW], src[:, u, :], m["mat"][f"{name}_v"][:, 0:VW], start=True, stop=True)\
                        .then_inc(kv_done, 1)

                def q_dense(b, u):
                    pe.wait_ge(xnT_ready, b + 1)
                    if masked:
                        pe.wait_ge(any_ready, 3 * b + 1)
                    pe.matmul(q_ps[:, 1, :], m["mat"][f"{name}_q"], xnT[:, u, :], start=True, stop=True).then_inc(q_done, 1)

                def mask_count(b, u):
                    pe.wait_ge(mask_ready, 3 * b + 3)
                    wait(pe, qlo, b)
                    pe.matmul(q_ps[:, 2, :], m["onesb"][:], keepb[:, u, :], start=True, stop=True).then_inc(cnt_done, 1)

                def stack(b, u, which, half):
                    pe.wait_ge(klo if which else qlo, b + 1)
                    if which:
                        wait(pe, qst_ready, NH * b)
                        wait(pe, kst_ready, NH * b + half)
                    else:
                        pe.wait_ge(kst_ready, NH * (b + 1))
                        wait(pe, qst_ready, NH * b + half)
                    w = selk if which else selq
                    for blk in range(4):
                        c = 4 * half + blk
                        pe.matmul(stack_ps[:, blk, :], w[:, 0, c, :], hi[:, u, which, :], start=True, stop=False)
                        last = pe.matmul(stack_ps[:, blk, :], w[:, 1, c, :], lo[:, u, which, :], start=False, stop=True)
                    last.then_inc(kstack if which else qstack, 1)

                def heads(j):
                    return (j % 4, 4 * (j // 4)) if nblk == 4 else (j // 2, 4 * (j % 2))

                def head(g, blk):
                    return 4 * blk + g

                def scores(b, u, j):
                    n = NQ * b + j
                    if j == 0:
                        pe.wait_ge(kst_ready, NH * (b + 1))
                        pe.wait_ge(qst_ready, NH * (b + 1))
                        if masked:
                            pe.wait_ge(nbk_ready, b + 1)
                    wait(pe, mx_ready, n - 1)
                    g, b0 = heads(j)
                    r = slice(32 * g, 32 * g + R)
                    if masked:
                        for i in range(4):
                            pe.matmul(s_ps[:, j % 2, i, :], m["identb"][:], nbq[:, u, :], start=(i == 0), stop=False,
                                      skip_group_check=True)
                    for i in range(4):
                        last = pe.matmul(s_ps[:, j % 2, i, :], qst[r, u, b0 + i, :], kst[r, u, b0 + i, :],
                                         start=not masked, stop=True, skip_group_check=masked)
                    last.then_inc(s_done, 1)

                def scores_by_key(b, u, j):
                    n = NQ * b + j
                    pe.wait_ge(mx_ready, n + 1)
                    wait(pe, exp_done, n - 1)
                    g, b0 = heads(j)
                    r = slice(32 * g, 32 * g + R)
                    for i in range(4):
                        pe.matmul(st_ps[:, j % 2, i, :], mx[:, j % 2, i:i + 1].broadcast_to([P, P]), m["negident"][:],
                                  start=(i == 0), stop=False, skip_group_check=True)
                        if masked:
                            pe.matmul(st_ps[:, j % 2, i, :], m["identb"][:], nbk[:, u, :], start=False, stop=False,
                                      skip_group_check=True)
                    for i in range(4):
                        last = pe.matmul(st_ps[:, j % 2, i, :], kst[r, u, b0 + i, :], qst[r, u, b0 + i, :],
                                         start=False, stop=True, skip_group_check=True)
                    last.then_inc(st_done, 1)

                def values(b, u, j):
                    n = NQ * b + j
                    if j == 0:
                        pe.wait_ge(v_ready, b + 1)
                        wait(pe, on_done, b)
                    pe.wait_ge(exp_done, n + 1)
                    g, b0 = heads(j)
                    for i in range(4):
                        h = head(g, b0 + i)
                        last = pe.matmul(o_h[:, h, :], pr[:, j % 2, i, :], vx[:, u, h // 2 if differs else h, :],
                                         start=True, stop=True)
                    last.then_inc(pv_done, 1)

                def o_turn(b, u):
                    pe.wait_ge(on_done, b + 1)
                    ahead_of = min(b + 3, B) if isinstance(b, int) else b + 3
                    pe.wait_ge(klo, ahead_of)
                    pe.wait_ge(v_ready, ahead_of)
                    pe.transpose(k_ps[:, 2, :], on[:, u, :], m["mat"]["ident"]).then_inc(oT_done, 1)

                def project(b, u):
                    pe.wait_ge(oT_ready, b + 1)
                    if own:
                        pe.matmul(k_ps[:, 3, :], m["mat"]["a1_o"][0:VW, :], oT[0:VW, u, :], start=True, stop=True)\
                            .then_inc(y_done, 1)
                    else:
                        pe.matmul(k_ps[:, 3, :], oT[:, u, :], m["mat"][f"{name}_o"], start=True, stop=True).then_inc(y_done, 1)

                def route(b, u):
                    pe.wait_ge(mT_ready, b + 1)
                    pe.matmul(k_ps[:, 0, 0:E], mT[:, u, :], m["router_w"][:], start=True, stop=True).then_inc(lg_done, 1)

                def prepare(b, u, j):
                    if j == 0:
                        if masked:
                            mask_count(b, u)
                        x_turn(b, u)
                        k_dense(b, u)
                    if j == 1:
                        q_dense(b, u)
                        stack(b, u, 1, 0)

                prepare(0, 0, 0)
                prepare(0, 0, 1)
                if NH == 2:
                    stack(0, 0, 1, 1)
                for half in range(NH):
                    stack(0, 0, 0, half)
                scores(0, 0, 0)

                def step(b, u, last=None):
                    more, before = nxt(b, last), nxt(b, 0)
                    for j in range(NQ):
                        if own and before and j == 3:
                            route(b - 1, 1 - u)
                        if j < NQ - 1:
                            scores(b, u, j + 1)
                        elif more:
                            scores(b + 1, 1 - u, 0)
                        scores_by_key(b, u, j)
                        if j > 0:
                            values(b, u, j - 1)
                        elif before:
                            values(b - 1, 1 - u, NQ - 1)
                        if more and j < 2:
                            prepare(b + 1, 1 - u, j)
                        if before and j == 1:
                            o_turn(b - 1, 1 - u)
                        if NH == 1 and more and j == 2:
                            stack(b + 1, 1 - u, 0, 0)
                        if NH == 2 and more and j == 2:
                            stack(b + 1, 1 - u, 1, 1)
                        if NH == 2 and more and j in (3, 4):
                            stack(b + 1, 1 - u, 0, j - 3)
                        if before and j == 2:
                            project(b - 1, 1 - u)

                over_batches(pe, step)
                values(B - 1, 1, NQ - 1)
                o_turn(B - 1, 1)
                project(B - 1, 1)
                if own:
                    route(B - 1, 1)

        sem.clear()


LN_STEPS = 7


def layernorm_stats(nc, dve, m, lnv, rstd, nmr, steps, ln_ready, pow_ready):
    st = m["stats"]
    c = Chain(dve, steps)
    c(dve.tensor_tensor(lnv[:, 0, :], st[:, :, 1], st[:, :, 4], ALU.add))
    c(dve.tensor_tensor(lnv[:, 1, :], st[:, :, 1], st[:, :, 4], ALU.subtract))
    c(dve.tensor_tensor(lnv[:, 2, :], st[:, :, 2], st[:, :, 5], ALU.add))
    c(dve.tensor_tensor(lnv[:, 3, :], lnv[:, 1, :], lnv[:, 1, :], ALU.mult))
    c(dve.tensor_scalar(lnv[:, 2, :], lnv[:, 2, :], 1.0 / D, EPS, ALU.mult, ALU.add))
    c(dve.scalar_tensor_tensor(lnv[:, 4, :], lnv[:, 3, :], 0.25, lnv[:, 2, :], ALU.mult, ALU.add))
    dve.sem_inc(ln_ready, 1)
    dve.wait_ge(pow_ready, 1)
    c(dve.scalar_tensor_tensor(nmr[:], lnv[:, 0, :], -0.5, rstd[:], ALU.mult, ALU.mult))


def recurrence(nc, m):
    T = P
    with ExitStack() as ctx:
        def sb(n, shape, dt=F32):
            return ctx.enter_context(nc.sbuf_tensor(f"r_{n}", shape, dt))

        def ps(n, shape):
            return ctx.enter_context(nc.psum_tensor(f"r_{n}", shape, F32))

        sem = Semaphores(nc, ctx, "r")

        inp, gate, rest = (m["pool"][:, i].rearrange("p (t b) -> p t b", b=B) for i in range(3))
        state = m["big"][:].rearrange("p b t -> p (b t)").rearrange("p (t b) -> p t b", b=B)
        G = 4
        xn = sb("xn", [P, 2, G, D])
        kv = sb("kv", [P, 2, G, T])
        r = sb("r", [P, 2, G, T])
        ret = sb("ret", [P, 2, G, T])
        gi = sb("gi", [P, G, T])
        ms = sb("ms", [P, 2, B])
        sT = sb("sT", [P, 2, T])
        xb = sb("xb", [P, 2, D])
        lnv, rstd, nmr = sb("lnv", [P, 6, B]), sb("rstd", [P, B]), sb("nmr", [P, B])
        xT_ps, in_ps, g_ps = ps("xT_ps", [P, 2, G, T]), ps("in_ps", [P, G, T]), ps("g_ps", [P, G, T])
        z_ps, y_ps = ps("z_ps", [P, 2, 512]), ps("y_ps", [P, 2, 512])

        half_set, ln_ready, pow_ready, steps = sem("half_set"), sem("ln_ready"), sem("pow_ready"), sem("steps")
        xn_ready, xT_done, kv_ready, r_ready, ret_ready = (sem("xn_ready"), sem("xT_done"), sem("kv_ready"),
                                                           sem("r_ready"), sem("ret_ready"))
        in_done, in_ready, g_done, gate_ready, gi_ready, rest_ready = (
            sem("in_done"), sem("in_ready"), sem("g_done"), sem("gate_ready"), sem("gi_ready"), sem("rest_ready"))
        ms_ready, z_done, s_ready = sem("ms_ready"), sem("z_done"), sem("s_ready")
        sT_ready, xb_ready, y_done, x_done = sem("sT_ready"), sem("xb_ready"), sem("y_done"), sem("x_done")
        NG = B // G

        def cols(t, g):
            return t[:, :, bass.ds(G * g, G)].rearrange("p t b -> p b t")

        with nc.Block() as block:

            @block.gpsimd
            def _(pool):
                pool.memset(lnv[:, 5, :], -0.5).then_inc(half_set, 1)
                pool.wait_ge(half_set, 1)
                pool.wait_ge(ln_ready, 1)
                nc.gpsimd.tensor_tensor(rstd[:], lnv[:, 4, :], lnv[:, 5, :], ALU.pow).then_inc(pow_ready, 1)

                def step(g, u, last=None):
                    wait(pool, r_ready, G * (g - 1))
                    c = m["ctxT"][:, bass.ds(G * g, G), :]
                    nc.gpsimd.tensor_tensor(kv[:, u], c, c, ALU.mult).then_inc(kv_ready, 1)
                    pool.wait_ge(gate_ready, g + 1)
                    nc.gpsimd.tensor_tensor(gi[:], cols(gate, g), cols(inp, g), ALU.mult).then_inc(gi_ready, 1)
                    pool.wait_ge(gi_ready, g + 1)
                    nc.gpsimd.tensor_tensor(cols(rest, g), cols(inp, g), gi[:], ALU.subtract).then_inc(rest_ready, 1)

                over_batches(pool, step, NG)

            @block.vector
            def _(dve):
                layernorm_stats(nc, dve, m, lnv, rstd, nmr, steps, ln_ready, pow_ready)

                def normalise(g, u):
                    wait(dve, xT_done, g - 1)
                    for i in range(G):
                        last = dve.tensor_scalar(xn[:, u, i, :], m["x"][:, G * g + i, :], rstd[:, bass.ds(G * g + i, 1)],
                                                 nmr[:, bass.ds(G * g + i, 1)], ALU.mult, ALU.add)
                    last.then_inc(xn_ready, 1)

                normalise(0, 0)

                def step(g, u, last=None):
                    if not (isinstance(g, int) and g == last):
                        normalise(g + 1, 1 - u)
                    dve.wait_ge(kv_ready, g + 1)
                    for i in range(G):
                        dve.tensor_tensor_scan(r[:, u, i, :], m["col"]["decay"].broadcast_to([P, T]), kv[:, u, i, :],
                                               0.0, ALU.mult, ALU.add).then_inc(r_ready, 1)
                    dve.wait_ge(r_ready, G * (g + 1))
                    dve.wait_ge(xT_done, g + 1)
                    wait(dve, in_done, g - 1)
                    dve.tensor_tensor(ret[:, u], xT_ps[:, u], r[:, u], ALU.mult).then_inc(ret_ready, 1)

                over_batches(dve, step, NG)

            @block.tensor
            def _(pe):
                def turn(g, u):
                    pe.wait_ge(xn_ready, g + 1)
                    wait(pe, ret_ready, g - 1)
                    for i in range(G):
                        last = pe.transpose(xT_ps[:, u, i, :], xn[:, u, i, :], m["mat"]["ident"])
                    last.then_inc(xT_done, 1)

                pe.wait_ge(m["weights_in"], m["weights_count"])
                turn(0, 0)

                def step(g, u, last=None):
                    if not (isinstance(g, int) and g == last):
                        turn(g + 1, 1 - u)
                    pe.wait_ge(ret_ready, g + 1)
                    wait(pe, in_ready, g)
                    pe.matmul(in_ps[:], m["mat"]["r_wi"], ret[:, u], start=True, stop=True).then_inc(in_done, 1)
                    pe.wait_ge(in_ready, g + 1)
                    wait(pe, gate_ready, g)
                    pe.matmul(g_ps[:], m["mat"]["r_wg"], cols(inp, g), start=True, stop=True).then_inc(g_done, 1)

                over_batches(pe, step, NG)

            @block.scalar
            def _(act):
                act.preload_act_table(ACT.Sigmoid)

                def step(g, u, last=None):
                    act.wait_ge(in_done, g + 1)
                    act.activation(cols(inp, g), in_ps[:], ACT.Identity, bias=m["col"]["r_bi"]).then_inc(in_ready, 1)
                    act.wait_ge(g_done, g + 1)
                    act.activation(cols(gate, g), g_ps[:], ACT.Sigmoid, bias=m["col"]["r_bg"]).then_inc(gate_ready, 1)

                over_batches(act, step, NG)

        with nc.Block() as block:

            @block.tensor
            def _(pe):
                def step(t, u, last=None):
                    wait(pe, s_ready, t - 1)
                    pe.matmul(z_ps[:, u, 0:B], m["mat"]["r_bm"], inp[:, t, :], start=True, stop=False)
                    first = isinstance(t, int) and t == 0
                    z = pe.matmul(z_ps[:, u, 0:B], m["mat"]["r_a"], rest[:, t, :], start=False, stop=first)
                    if not first:
                        pe.wait_ge(ms_ready, t)
                        z = pe.matmul(z_ps[:, u, 0:B], m["mat"]["r_a"], ms[:, u, :], start=False, stop=True)
                    z.then_inc(z_done, 1)

                over_batches(pe, step, T)

            @block.scalar
            def _(act):
                act.preload_act_table(ACT.Tanh)

                def step(t, u, last=None):
                    act.wait_ge(z_done, t + 1)
                    act.activation(state[:, t, :], z_ps[:, u, 0:B], ACT.Tanh).then_inc(s_ready, 1)

                over_batches(act, step, T)

            @block.vector
            def _(dve):
                def step(t, u, last=None):
                    if isinstance(t, int) and t == 0:
                        return
                    dve.wait_ge(s_ready, t)
                    dve.tensor_tensor(ms[:, u, :], gate[:, t, :], state[:, t - 1, :], ALU.mult).then_inc(ms_ready, 1)

                over_batches(dve, step, T)

        with nc.Block() as block:

            @block.gpsimd
            def _(pool):
                def step(b, u, last=None):
                    wait(pool, x_done, b - 1)
                    nc.gpsimd.tensor_tensor(xb[:, u, :], m["x"][:, b, :], m["row"]["r_bo"], ALU.add).then_inc(xb_ready, 1)

                over_batches(pool, step)

            @block.scalar
            def _(act):
                def step(b, u, last=None):
                    wait(act, y_done, b - 1)
                    act.activation(sT[:, u, :], state[:, :, b], ACT.Copy).then_inc(sT_ready, 1)

                over_batches(act, step)

            @block.tensor
            def _(pe):
                def step(b, u, last=None):
                    pe.wait_ge(sT_ready, b + 1)
                    wait(pe, x_done, b - 1)
                    pe.matmul(y_ps[:, u, 0:D], sT[:, u, :], m["mat"]["r_wo"], start=True, stop=True).then_inc(y_done, 1)

                over_batches(pe, step)

            @block.vector
            def _(dve):
                def step(b, u, last=None):
                    dve.wait_ge(y_done, b + 1)
                    dve.wait_ge(xb_ready, b + 1)
                    dve.tensor_tensor(m["x"][:, b, :], y_ps[:, u, 0:D], xb[:, u, :], ALU.add).then_inc(x_done, 1)
                    dve.wait_ge(x_done, b + 1)
                    dve.bn_stats(m["stats"][:, b, :], m["x"][:, b, :])

                over_batches(dve, step)

        sem.clear()


def softmax_experts(nc, dve, act_ready, exp_ready, c, lg, tmp, rows):
    n = lg.shape[1]
    wide = [rows, n, E]
    c(dve.tensor_reduce(tmp, lg, AX.X, ALU.max))
    c(dve.tensor_tensor(lg, lg, tmp.unsqueeze(2).broadcast_to(wide), ALU.subtract))
    dve.sem_inc(act_ready, 1)
    dve.wait_ge(exp_ready, 1)
    c(dve.tensor_reduce(tmp, lg, AX.X, ALU.add))
    c(dve.reciprocal(tmp, tmp))
    c(dve.tensor_tensor(lg, lg, tmp.unsqueeze(2).broadcast_to(wide), ALU.mult))


def top_two_mixture(nc, m):
    G = 4
    NG = B // G
    F = 2
    with ExitStack() as ctx:
        def sb(n, shape, dt=F32):
            return ctx.enter_context(nc.sbuf_tensor(f"m_{n}", shape, dt))

        def ps(n, shape):
            return ctx.enter_context(nc.psum_tensor(f"m_{n}", shape, F32))

        sem = Semaphores(nc, ctx, "m")

        lg = m["logits"]
        wgt = sb("wgt", [P, B, E])
        pick = sb("pick", [P, B, E])
        left = sb("left", [P, B, E])
        t1, t2, t3 = sb("t1", [P, B]), sb("t2", [P, B]), sb("t3", [P, B])
        wT = sb("wT", [P, 2, P])
        h = sb("h", [P, 2, F, G * P])
        turn_ps = ps("turn_ps", [P, 512])
        h_ps, z_ps = ps("h_ps", [P, 2, G * P]), ps("z_ps", [P, 2, G, D])
        b_ps = ps("b_ps", [P, 2, 512])
        steps, act_ready, exp_ready, w_ready, wT_done, wT_ready = (sem("steps"), sem("act_ready"), sem("exp_ready"),
                                                                   sem("w_ready"), sem("wT_done"), sem("wT_ready"))
        b_done, b_added, h_done, h_ready, z_done, z_added, x_done = (
            sem("b_done"), sem("b_added"), sem("h_done"), sem("h_ready"), sem("z_done"), sem("z_added"), sem("x_done"))

        with nc.Block() as block:

            @block.scalar
            def _(act):
                act.wait_ge(act_ready, 1)
                act.activation(lg[:], lg[:], ACT.Exp).then_inc(exp_ready, 1)

            @block.vector
            def _(dve):
                c = Chain(dve, steps)
                softmax_experts(nc, dve, act_ready, exp_ready, c, lg[:], t1[:], P)
                wide = [P, B, E]

                def choose(src, top):
                    c(dve.tensor_reduce(top[:], src[:], AX.X, ALU.max))
                    c(dve.tensor_tensor(pick[:], src[:], top[:].unsqueeze(2).broadcast_to(wide), ALU.is_equal))
                    c(dve.tensor_tensor(pick[:], pick[:], m["down"][:].unsqueeze(1).broadcast_to(wide), ALU.mult))
                    c(dve.tensor_reduce(t3[:], pick[:], AX.X, ALU.max))
                    c(dve.tensor_tensor(pick[:], pick[:], t3[:].unsqueeze(2).broadcast_to(wide), ALU.is_equal))

                choose(lg, t1)
                c(dve.tensor_tensor(wgt[:], pick[:], t1[:].unsqueeze(2).broadcast_to(wide), ALU.mult))
                c(dve.scalar_tensor_tensor(left[:].rearrange("p b e -> p (b e)"), pick[:].rearrange("p b e -> p (b e)"), -4.0,
                                           lg[:].rearrange("p b e -> p (b e)"), ALU.mult, ALU.add))
                choose(left, t2)
                c(dve.tensor_tensor(pick[:], pick[:], t2[:].unsqueeze(2).broadcast_to(wide), ALU.mult))
                c(dve.tensor_tensor(wgt[:], wgt[:], pick[:], ALU.add))
                c(dve.tensor_tensor(t1[:], t1[:], t2[:], ALU.add))
                c(dve.tensor_scalar(t1[:], t1[:], 1e-8, None, ALU.add))
                c(dve.reciprocal(t1[:], t1[:]))
                c(dve.tensor_scalar(t1[:], t1[:], 0.3, None, ALU.mult))
                dve.tensor_tensor(wgt[:], wgt[:], t1[:].unsqueeze(2).broadcast_to(wide), ALU.mult).then_inc(w_ready, 1)
                dve.wait_ge(wT_done, 1)
                dve.tensor_copy(wT[:], turn_ps[:, 0:2 * P].rearrange("p (h t) -> p h t", h=2)).then_inc(wT_ready, 1)

            @block.tensor
            def _(pe):
                pe.wait_ge(w_ready, 1)
                for half in range(2):
                    last = pe.transpose(turn_ps[:, half * P:(half + 1) * P],
                                        wgt[:, 16 * half:16 * half + 16, :].rearrange("p b e -> p (b e)"), m["mat"]["ident"])
                last.then_inc(wT_done, 1)

        with nc.Block() as block:

            @block.tensor
            def _(pe):
                pe.wait_ge(m["m_in"], 48)
                for half in range(2):
                    def bias(b, u, last=None):
                        wait(pe, b_added, b + 16 * half - 1)
                        pe.matmul(b_ps[:, u, 0:D], wT[:, half, :], m["m_b2"][:, b, :], start=True, stop=True)\
                            .then_inc(b_done, 1)

                    over_batches(pe, bias, 16)

                def up(g, e):
                    n = E * g + e
                    for f in range(F):
                        wait(pe, h_ready, F * (n - 1) + f + 1)
                        pe.matmul(h_ps[:, f, :], m["m_w1"][:, e, f * P:(f + 1) * P], m["big"][:, bass.ds(G * g, G), :],
                                  start=True, stop=True).then_inc(h_done, 1)

                def down(g, e):
                    n = E * g + e
                    pe.wait_ge(h_ready, F * (n + 1))
                    wait(pe, z_added, n - 1)
                    for i in range(G):
                        for f in range(F):
                            last = pe.matmul(z_ps[:, e % 2, i, :], h[:, e % 2, f, i * P:(i + 1) * P], m["m_w2"][:, e, f, :],
                                             start=(f == 0), stop=(f == F - 1))
                    last.then_inc(z_done, 1)

                def group(g, u, last=None):
                    up(g, 0)
                    for e in range(1, E):
                        up(g, e)
                        down(g, e - 1)
                    down(g, E - 1)

                over_batches(pe, group, NG)

            @block.scalar
            def _(act):
                act.preload_act_table(ACT.Gelu)

                def group(g, u, last=None):
                    for e in range(E):
                        n = E * g + e
                        for f in range(F):
                            act.wait_ge(h_done, F * n + f + 1)
                            wait(act, z_done, n - 1)
                            act.activation(h[:, e % 2, f, :], h_ps[:, f, :], ACT.Gelu,
                                           bias=m["col"][f"m_b1_{F * e + f}"]).then_inc(h_ready, 1)

                over_batches(act, group, NG)

            @block.vector
            def _(dve):
                for half in range(2):
                    def bias(b, u, last=None):
                        dve.wait_ge(b_done, b + 16 * half + 1)
                        x = m["x"][:, b + 16 * half, :]
                        dve.tensor_tensor(x, x, b_ps[:, u, 0:D], ALU.add).then_inc(b_added, 1)

                    over_batches(dve, bias, 16)
                dve.wait_ge(b_added, B)

                def group(g, u, last=None):
                    for e in range(E):
                        n = E * g + e
                        dve.wait_ge(z_done, n + 1)
                        wait(dve, z_added, n)
                        for i in range(G):
                            x = m["x"][:, G * g + i, :]
                            w = wgt[:, G * g + i, e:e + 1]
                            last_op = dve.scalar_tensor_tensor(x, z_ps[:, e % 2, i, :], w, x, ALU.mult, ALU.add)
                        last_op.then_inc(z_added, 1)
                    dve.wait_ge(z_added, E * (g + 1))
                    for i in range(G):
                        dve.bn_stats(m["stats"][:, G * g + i, :], m["x"][:, G * g + i, :])

                over_batches(dve, group, NG)

        sem.clear()




def expert_choice(nc, m):
    G, NG, K, F = 4, 8, 32, 4
    with ExitStack() as ctx:
        def sb(n, shape, dt=F32):
            return ctx.enter_context(nc.sbuf_tensor(f"e_{n}", shape, dt))

        sem = Semaphores(nc, ctx, "e")

        lg = m["logits"]
        lnv, rstd, nmr = sb("lnv", [P, 6, B]), sb("rstd", [P, B]), sb("nmr", [P, B])
        xn = sb("xn", [P, 2, G, D])
        rank = sb("rank", [P, B, E])
        half_set, ln_ready, pow_ready, steps = sem("half_set"), sem("ln_ready"), sem("pow_ready"), sem("steps")

        with ExitStack() as inner:
            xnT = inner.enter_context(nc.sbuf_tensor("e_xnT", [P, 2, P], F32))
            xT_ps = inner.enter_context(nc.psum_tensor("e_xT_ps", [P, 2, 512], F32))
            lg_ps = inner.enter_context(nc.psum_tensor("e_lg_ps", [P, 2, 512], F32))
            xn_ready, xT_done, xnT_ready, lg_done, lg_ready = (sem("r_xn_ready"), sem("r_xT_done"), sem("r_xnT_ready"),
                                                               sem("r_lg_done"), sem("r_lg_ready"))
            with nc.Block() as block:

                @block.gpsimd
                def _(pool):
                    pool.memset(lnv[:, 5, :], -0.5).then_inc(half_set, 1)
                    pool.wait_ge(half_set, 1)
                    pool.wait_ge(ln_ready, 1)
                    nc.gpsimd.tensor_tensor(rstd[:], lnv[:, 4, :], lnv[:, 5, :], ALU.pow).then_inc(pow_ready, 1)

                @block.vector
                def _(dve):
                    layernorm_stats(nc, dve, m, lnv, rstd, nmr, steps, ln_ready, pow_ready)

                    def normalise(b, u):
                        wait(dve, xT_done, b - 1)
                        dve.tensor_scalar(xn[:, u, 0, :], m["x"][:, b, :], rstd[:, bass.ds(b, 1)], nmr[:, bass.ds(b, 1)],
                                          ALU.mult, ALU.add).then_inc(xn_ready, 1)

                    normalise(0, 0)

                    def step(b, u, last=None):
                        if not (isinstance(b, int) and b == last):
                            normalise(b + 1, 1 - u)
                        dve.wait_ge(lg_done, b + 1)
                        dve.tensor_copy(lg[:, b, :], lg_ps[:, u, 0:E]).then_inc(lg_ready, 1)

                    over_batches(dve, step)

                @block.scalar
                def _(act):
                    def step(b, u, last=None):
                        act.wait_ge(xT_done, b + 1)
                        wait(act, lg_done, b - 1)
                        act.activation(xnT[:, u, :], xT_ps[:, u, 0:P], ACT.Copy).then_inc(xnT_ready, 1)

                    over_batches(act, step)

                @block.tensor
                def _(pe):
                    def turn(b, u):
                        pe.wait_ge(xn_ready, b + 1)
                        wait(pe, xnT_ready, b - 1)
                        pe.transpose(xT_ps[:, u, 0:P], xn[:, u, 0, :], m["mat"]["ident"]).then_inc(xT_done, 1)

                    turn(0, 0)

                    def step(b, u, last=None):
                        if not (isinstance(b, int) and b == last):
                            turn(b + 1, 1 - u)
                        pe.wait_ge(xnT_ready, b + 1)
                        wait(pe, lg_ready, b - 1)
                        pe.matmul(lg_ps[:, u, 0:E], xnT[:, u, :], m["gate_w"][:], start=True, stop=True).then_inc(lg_done, 1)

                    over_batches(pe, step)

        with ExitStack() as inner:
            def ib(n, shape):
                return inner.enter_context(nc.sbuf_tensor(f"e_{n}", shape, F32))

            t1 = ib("t1", [P, B])
            pT, left, took = ib("pT", [P, 2, P]), ib("left", [P, 2, P]), ib("took", [P, 2, P])
            top = ib("top", [P, 2, 8])
            tk = ib("tk", [P, 2, P])
            pT_ps = inner.enter_context(nc.psum_tensor("e_pT_ps", [P, 512], F32))
            tk_ps = inner.enter_context(nc.psum_tensor("e_tk_ps", [P, 512], F32))
            rk_ps = inner.enter_context(nc.psum_tensor("e_rk_ps", [P, 512], F32))
            c_steps, act_ready, exp_ready, p_ready = sem("c_steps"), sem("act_ready"), sem("exp_ready"), sem("p_ready")
            pT_done, took_ready, tk_done, tk_ready, rk_done = (sem("pT_done"), sem("took_ready"), sem("tk_done"),
                                                               sem("tk_ready"), sem("rk_done"))
            with nc.Block() as block:

                @block.scalar
                def _(act):
                    act.wait_ge(act_ready, 1)
                    act.activation(lg[:], lg[:], ACT.Exp).then_inc(exp_ready, 1)

                @block.vector
                def _(dve):
                    c = Chain(dve, c_steps)
                    softmax_experts(nc, dve, act_ready, exp_ready, c, lg[:], t1[:], P)
                    dve.sem_inc(p_ready, 1)
                    dve.wait_ge(pT_done, 1)
                    c(dve.tensor_copy(pT[:], pT_ps[:, 0:2 * P].rearrange("p (h t) -> p h t", h=2)))
                    src = pT
                    for _ in range(K // 8):
                        for half in range(2):
                            c(dve.max(top[:, half, :], src[:, half, :]))
                            c(dve.match_replace(left[:, half, :], top[:, half, :], src[:, half, :], -1.0))
                        src = left
                    dve.tensor_scalar(took[:], left[:], 0.0, None, ALU.is_lt).then_inc(took_ready, 1)
                    dve.wait_ge(tk_done, 1)
                    dve.tensor_copy(tk[:], tk_ps[:, 0:2 * P].rearrange("p (h t) -> p h t", h=2)).then_inc(tk_ready, 1)
                    dve.wait_ge(rk_done, 1)
                    dve.tensor_tensor(rank[:].rearrange("p b e -> p (b e)"), rk_ps[:, 0:2 * P],
                                      tk[:].rearrange("p h t -> p (h t)"), ALU.mult)

                @block.tensor
                def _(pe):
                    pe.wait_ge(p_ready, 1)
                    for half in range(2):
                        last = pe.transpose(pT_ps[:, half * P:(half + 1) * P],
                                            lg[:, 16 * half:16 * half + 16, :].rearrange("p b e -> p (b e)"), m["mat"]["ident"])
                    last.then_inc(pT_done, 1)
                    pe.wait_ge(took_ready, 1)
                    for half in range(2):
                        last = pe.transpose(tk_ps[:, half * P:(half + 1) * P], took[:, half, :], m["mat"]["ident"])
                    last.then_inc(tk_done, 1)
                    pe.wait_ge(tk_ready, 1)
                    pe.matmul(rk_ps[:, 0:2 * P], m["mat"]["tri"], tk[:].rearrange("p h t -> p (h t)"), start=True, stop=True)\
                        .then_inc(rk_done, 1)

        oh = sb("oh", [P, 2, G, E, K])
        ohw = sb("ohw", [P, 2, E, G, K])
        xe = sb("xe", [P, 2, E, G, K])
        owT = sb("owT", [P, 2, E, P])
        h = sb("h", [P, 2, F, P])
        z = sb("z", [P, E, D])
        yb = sb("yb", [P, 2, D], BF16)
        g_ps = ctx.enter_context(nc.psum_tensor("e_g_ps", [P, 512], F32))
        h_ps = ctx.enter_context(nc.psum_tensor("e_h_ps", [P, 2, F, P], F32))
        z_ps = ctx.enter_context(nc.psum_tensor("e_z_ps", [P, 512], F32))
        y_ps = ctx.enter_context(nc.psum_tensor("e_y_ps", [P, G, 512], F32))
        xn_ready, oh_ready, ohw_ready = sem("xn_ready"), sem("oh_ready"), sem("ohw_ready")
        gx_done, gx_ready, gw_done, gw_ready = sem("gx_done"), sem("gx_ready"), sem("gw_done"), sem("gw_ready")
        h_done, h_ready, z_done, z_ready, y_done, y_read, x_done = (
            sem("h_done"), sem("h_ready"), sem("z_done"), sem("z_ready"), sem("y_done"), sem("y_read"), sem("x_done"))

        with nc.Block() as block:

            @block.gpsimd
            def _(pool):
                def step(g, u, last=None):
                    wait(pool, gw_done, 2 * (g - 1))
                    for i in range(G):
                        pool.wait_ge(oh_ready, G * g + i + 1)
                        nc.gpsimd.tensor_tensor(ohw[:, u, :, i, :], oh[:, u, i],
                                                lg[:, G * g + i, :].unsqueeze(2).broadcast_to([P, E, K]), ALU.mult)\
                            .then_inc(ohw_ready, 1)

                over_batches(pool, step, NG)

            @block.vector
            def _(dve):
                def ready(g, u):
                    wait(dve, gx_done, 2 * (g - 1))
                    wait(dve, ohw_ready, G * (g - 1))
                    for i in range(G):
                        dve.tensor_scalar(xn[:, u, i, :], m["x"][:, G * g + i, :], rstd[:, bass.ds(G * g + i, 1)],
                                          nmr[:, bass.ds(G * g + i, 1)], ALU.mult, ALU.add).then_inc(xn_ready, 1)
                        dve.tensor_tensor(oh[:, u, i], m["iota"][:].unsqueeze(1).broadcast_to([P, E, K]),
                                          rank[:, G * g + i, :].unsqueeze(2).broadcast_to([P, E, K]), ALU.is_equal)\
                            .then_inc(oh_ready, 1)

                def keep_weights(g, u):
                    for half in range(2):
                        dve.wait_ge(gw_done, 2 * g + half + 1)
                        dve.tensor_copy(owT[:, u, 4 * half:4 * half + 4, :], g_ps[:].rearrange("p (e t) -> p e t", e=4))\
                            .then_inc(gw_ready, 1)

                def keep_z(g, e):
                    dve.wait_ge(z_done, E * g + e + 1)
                    if e == 0:
                        wait(dve, y_done, g)
                    dve.tensor_copy(z[:, e, :], z_ps[:, 0:D]).then_inc(z_ready, 1)

                ready(0, 0)
                keep_weights(0, 0)

                def step(g, u, last=None):
                    more = not (isinstance(g, int) and g == last)
                    if more:
                        ready(g + 1, 1 - u)
                    for e in range(E):
                        keep_z(g, e)
                        if e == 5 and more:
                            keep_weights(g + 1, 1 - u)
                    dve.wait_ge(y_done, g + 1)
                    for i in range(G):
                        if i >= 2:
                            dve.wait_ge(x_done, G * g + i - 1)
                        else:
                            wait(dve, x_done, G * g + i - 1)
                        dve.tensor_copy(yb[:, i % 2, :], y_ps[:, i, 0:D]).then_inc(y_read, 1)
                        dve.wait_ge(y_read, G * g + i + 1)
                        x = m["x"][:, G * g + i, :]
                        dve.tensor_tensor(x, x, yb[:, i % 2, :], ALU.add).then_inc(x_done, 1)
                    dve.wait_ge(x_done, G * (g + 1))
                    for i in range(G):
                        dve.bn_stats(m["stats"][:, G * g + i, :], m["x"][:, G * g + i, :])

                over_batches(dve, step, NG)

            @block.scalar
            def _(act):
                act.preload_act_table(ACT.Gelu_apprx_tanh)

                def keep_tokens(g, u):
                    for half in range(2):
                        act.wait_ge(gx_done, 2 * g + half + 1)
                        if half == 0:
                            wait(act, h_done, E * (g - 1))
                        act.activation(xe[:, u, :, 2 * half:2 * half + 2, :],
                                       g_ps[:].rearrange("p (i e k) -> p e i k", i=2, e=E), ACT.Copy).then_inc(gx_ready, 1)

                keep_tokens(0, 0)

                def step(g, u, last=None):
                    more = not (isinstance(g, int) and g == last)
                    for e in range(E):
                        n = E * g + e
                        act.wait_ge(h_done, n + 1)
                        wait(act, z_done, n - 1)
                        act.activation(h[:, e % 2], h_ps[:, e % 2], ACT.Gelu_apprx_tanh).then_inc(h_ready, 1)
                        if e == 3 and more:
                            keep_tokens(g + 1, 1 - u)

                over_batches(act, step, NG)

            @block.tensor
            def _(pe):
                pe.wait_ge(m["weights_in"], m["weights_count"])

                def gather(g, u):
                    for half in range(2):
                        if half == 0:
                            wait(pe, gw_ready, 2 * g)
                        else:
                            pe.wait_ge(gx_ready, 2 * g + 1)
                        for j in range(2):
                            i = 2 * half + j
                            pe.wait_ge(xn_ready, G * g + i + 1)
                            pe.wait_ge(oh_ready, G * g + i + 1)
                            last = pe.matmul(g_ps[:, j * 256:(j + 1) * 256], xn[:, u, i, :],
                                             oh[:, u, i].rearrange("p e k -> p (e k)"), start=True, stop=True)
                        last.then_inc(gx_done, 1)

                def turn_weights(g, u):
                    pe.wait_ge(ohw_ready, G * (g + 1))
                    for half in range(2):
                        if half == 0:
                            pe.wait_ge(gx_ready, 2 * g + 2)
                        else:
                            pe.wait_ge(gw_ready, 2 * g + 1)
                        for j in range(4):
                            last = pe.transpose(g_ps[:, j * P:(j + 1) * P],
                                                ohw[:, u, 4 * half + j].rearrange("p i k -> p (i k)"), m["mat"]["ident"])
                        last.then_inc(gw_done, 1)

                def up(g, u, e):
                    n = E * g + e
                    if e == 0:
                        pe.wait_ge(gx_ready, 2 * (g + 1))
                    wait(pe, h_ready, n - 1)
                    for f in range(F):
                        last = pe.matmul(h_ps[:, e % 2, f, :], m["e_w1"][:, e, f * P:(f + 1) * P],
                                         xe[:, u, e].rearrange("p i k -> p (i k)"), start=True, stop=True)
                    last.then_inc(h_done, 1)

                def down(g, e):
                    n = E * g + e
                    pe.wait_ge(h_ready, n + 1)
                    wait(pe, z_ready, n)
                    for f in range(F):
                        last = pe.matmul(z_ps[:, 0:D], h[:, e % 2, f, :], m["e_w2"][:, e, f, :],
                                         start=(f == 0), stop=(f == F - 1))
                    last.then_inc(z_done, 1)

                def scatter(g, u):
                    pe.wait_ge(z_ready, E * (g + 1))
                    pe.wait_ge(gw_ready, 2 * (g + 1))
                    wait(pe, y_read, G * g)
                    for e in range(E):
                        for i in range(G):
                            r = slice(K * i, K * i + K)
                            last = pe.matmul(y_ps[:, i, 0:D], owT[r, u, e, :], z[r, e, :], start=(e == 0), stop=(e == E - 1))
                    last.then_inc(y_done, 1)

                gather(0, 0)
                turn_weights(0, 0)

                def step(g, u, last=None):
                    more = not (isinstance(g, int) and g == last)
                    up(g, u, 0)
                    for e in range(1, E):
                        up(g, u, e)
                        down(g, e - 1)
                        if e == 4 and more:
                            gather(g + 1, 1 - u)
                        if e == 6 and more:
                            turn_weights(g + 1, 1 - u)
                    down(g, E - 1)
                    scatter(g, u)

                over_batches(pe, step, NG)

        sem.clear()


def hashed_mixture(nc, m):
    G, NG = 4, 8
    with ExitStack() as ctx:
        def sb(n, shape, dt=F32):
            return ctx.enter_context(nc.sbuf_tensor(f"s_{n}", shape, dt))

        def ps(n, shape):
            return ctx.enter_context(nc.psum_tensor(f"s_{n}", shape, F32))

        sem = Semaphores(nc, ctx, "s")

        lnv, rstd, nmr = sb("lnv", [P, 6, B]), sb("rstd", [P, B]), sb("nmr", [P, B])
        xn = sb("xn", [P, 2, G, D])
        xT = sb("xT", [P, 2, 8, 64])
        av = sb("av", [P, 512])
        sg = sb("sg", [P, 512])
        gt = sb("gt", [P, 512])
        hs = sb("hs", [P, 2, 512])
        hr = sb("hr", [P, 2, 8, 64])
        yT = sb("yT", [P, 64, 8])
        x_ps, a_ps, y_ps, t_ps = ps("x_ps", [P, G, P]), ps("a_ps", [P, 4, 512]), ps("y_ps", [P, 512]), ps("t_ps", [P, G, P])
        half_set, ln_ready, pow_ready, steps = sem("half_set"), sem("ln_ready"), sem("pow_ready"), sem("steps")
        av_ready = sem("av_ready")
        xn_ready, x_turned, xT_ready = sem("xn_ready"), sem("x_turned"), sem("xT_ready")
        gate_done, up_done, sg_ready, gt_ready, hs_ready = (sem("gate_done"), sem("up_done"), sem("sg_ready"),
                                                            sem("gt_ready"), sem("hs_ready"))
        r_done, hr_ready = sem("r_done"), sem("hr_ready")
        y_done, yT_ready, y_turned, x_done = sem("y_done"), sem("yT_ready"), sem("y_turned"), sem("x_done")

        with nc.Block() as block:

            @block.gpsimd
            def _(pool):
                pool.memset(lnv[:, 5, :], -0.5).then_inc(half_set, 1)
                pool.wait_ge(half_set, 1)
                pool.wait_ge(ln_ready, 1)
                nc.gpsimd.tensor_tensor(rstd[:], lnv[:, 4, :], lnv[:, 5, :], ALU.pow).then_inc(pow_ready, 1)

            @block.vector
            def _(dve):
                layernorm_stats(nc, dve, m, lnv, rstd, nmr, steps, ln_ready, pow_ready)

                def normalise(g, u):
                    wait(dve, x_turned, g - 1)
                    for i in range(G):
                        last = dve.tensor_scalar(xn[:, u, i, :], m["x"][:, G * g + i, :], rstd[:, bass.ds(G * g + i, 1)],
                                                 nmr[:, bass.ds(G * g + i, 1)], ALU.mult, ALU.add)
                    last.then_inc(xn_ready, 1)

                normalise(0, 0)

                def step(g, u, last=None):
                    if not (isinstance(g, int) and g == last):
                        normalise(g + 1, 1 - u)
                    for k in range(2):
                        dve.wait_ge(sg_ready, 2 * g + k + 1)
                        wait(dve, hs_ready, 2 * g + k)
                        dve.scalar_tensor_tensor(gt[:], sg[:], 1.0, av[:], ALU.add, ALU.mult)\
                            .then_inc(gt_ready, 1)
                        dve.wait_ge(gt_ready, 2 * g + k + 1)
                        dve.wait_ge(up_done, 2 * g + k + 1)
                        wait(dve, y_done, g)
                        dve.scalar_tensor_tensor(hs[:, k, :], a_ps[:, 1, :], m["col"][f"sb3_{k}"], gt[:], ALU.add, ALU.mult)\
                            .then_inc(hs_ready, 1)
                    for i in range(G):
                        if i == 0:
                            dve.wait_ge(y_turned, g + 1)
                        x = m["x"][:, G * g + i, :]
                        last_op = dve.scalar_tensor_tensor(x, t_ps[:, i, :], 0.25, x, ALU.mult, ALU.add)
                    last_op.then_inc(x_done, 1)
                    dve.wait_ge(x_done, g + 1)
                    for i in range(G):
                        dve.bn_stats(m["stats"][:, G * g + i, :], m["x"][:, G * g + i, :])

                over_batches(dve, step, NG)

            @block.scalar
            def _(act):
                act.preload_act_table(ACT.Gelu)

                def x_keep(g, u):
                    act.wait_ge(x_turned, g + 1)
                    wait(act, r_done, 2 * (g - 1))
                    act.activation(xT[:, u].rearrange("p r q -> p q r"), x_ps[:].rearrange("p i t -> p (i t)")
                                   .rearrange("p (q r) -> p q r", r=8), ACT.Copy).then_inc(xT_ready, 1)

                x_keep(0, 0)

                def step(g, u, last=None):
                    for k in range(2):
                        act.wait_ge(gate_done, 2 * g + k + 1)
                        wait(act, gt_ready, 2 * g + k)
                        act.activation(av[:], a_ps[:, 0, :], ACT.Identity, bias=m["col"][f"sb1_{k}"]).then_inc(av_ready, 1)
                        act.wait_ge(av_ready, 2 * g + k + 1)
                        act.activation(sg[:], av[:], ACT.Tanh, scale=0.5).then_inc(sg_ready, 1)
                    for k in range(2):
                        act.wait_ge(r_done, 2 * g + k + 1)
                        wait(act, y_done, g)
                        act.activation(hr[:, k].rearrange("p r q -> p (r q)"), a_ps[:, 2 + k, :], ACT.Gelu)\
                            .then_inc(hr_ready, 1)
                    if not (isinstance(g, int) and g == last):
                        x_keep(g + 1, 1 - u)
                    act.wait_ge(y_done, g + 1)
                    wait(act, y_turned, g)
                    act.activation(yT[:].rearrange("p q r -> p r q"), y_ps[:].rearrange("p (r q) -> p r q", r=8), ACT.Copy)\
                        .then_inc(yT_ready, 1)

                over_batches(act, step, NG)

            @block.tensor
            def _(pe):
                pe.wait_ge(m["weights_in"], m["weights_count"])

                def turn(g, u):
                    pe.wait_ge(xn_ready, g + 1)
                    wait(pe, xT_ready, g)
                    for i in range(G):
                        last = pe.transpose(x_ps[:, i, :], xn[:, u, i, :], m["mat"]["ident"])
                    last.then_inc(x_turned, 1)

                turn(0, 0)

                def step(g, u, last=None):
                    xin = xT[:, u].rearrange("p r q -> p (r q)")
                    pe.wait_ge(xT_ready, g + 1)
                    for k in range(2):
                        wait(pe, av_ready, 2 * g + k)
                        pe.matmul(a_ps[:, 0, :], m["s_w1"][:, k, :], xin, start=True, stop=True).then_inc(gate_done, 1)
                        wait(pe, hs_ready, 2 * g + k)
                        pe.matmul(a_ps[:, 1, :], m["s_w3"][:, k, :], xin, start=True, stop=True).then_inc(up_done, 1)
                    for k in range(2):
                        wait(pe, hr_ready, 2 * (g - 1) + k + 1)
                        pe.matmul(a_ps[:, 2 + k, :], m["s_b1"][:], m["s_hot"][0:E, k, :], start=True, stop=False,
                                  skip_group_check=True)
                        for r in range(8):
                            last_op = pe.matmul(a_ps[:, 2 + k, 64 * r:64 * r + 64], m["s_up"][:, HASHED[k][r], :], xT[:, u, r, :],
                                                start=False, stop=(r == 7), skip_group_check=True)
                        last_op.then_inc(r_done, 1)
                    if not (isinstance(g, int) and g == last):
                        turn(g + 1, 1 - u)
                    wait(pe, yT_ready, g)
                    pe.matmul(y_ps[:], m["s_b2"][:], m["s_hot"][:, 2, :], start=True, stop=False, skip_group_check=True)
                    for k in range(2):
                        pe.wait_ge(hs_ready, 2 * g + k + 1)
                        pe.matmul(y_ps[:], m["s_w2"][:, k, :], hs[:, k, :], start=False, stop=False, skip_group_check=True)
                    for k in range(2):
                        pe.wait_ge(hr_ready, 2 * g + k + 1)
                        for r in range(8):
                            last_op = pe.matmul(y_ps[:, 64 * r:64 * r + 64], m["s_down"][:, HASHED[k][r], :], hr[:, k, r, :],
                                                start=False, stop=(k == 1 and r == 7), skip_group_check=True)
                    last_op.then_inc(y_done, 1)
                    pe.wait_ge(yT_ready, g + 1)
                    wait(pe, x_done, g)
                    y = yT[:].rearrange("p q r -> p (q r)")
                    for i in range(G):
                        last_op = pe.transpose(t_ps[:, i, :], y[:, i * P:(i + 1) * P], m["mat"]["ident"])
                    last_op.then_inc(y_turned, 1)

                over_batches(pe, step, NG)

        sem.clear()


def zones(nc, m, a, out):
    TOP, F = 3, 4
    with ExitStack() as ctx:
        def sb(n, shape, dt=F32):
            return ctx.enter_context(nc.sbuf_tensor(f"z_{n}", shape, dt))

        def ps(n, shape):
            return ctx.enter_context(nc.psum_tensor(f"zp_{n}", shape, F32))

        sem = Semaphores(nc, ctx, "z")

        lnv, rstd, nmr = sb("lnv", [P, 6, B]), sb("rstd", [P, B]), sb("nmr", [P, B])
        xn = sb("xn", [P, 2, D])
        xT = sb("xT", [P, 2, P])
        meanT = sb("meanT", [P, B])
        hid, hidT = sb("hid", [B, 32]), sb("hidT", [32, B])
        lg, t1 = sb("lg", [B, 1, E]), sb("t1", [B, 1])
        top, idx, wt = sb("top", [B, 8]), sb("idx", [B, 8], U32), sb("wt", [B, 3])
        idx_row, w_row = sb("idx_row", [1, B * TOP], U32), sb("w_row", [1, B * TOP])
        w_all = sb("w_all", [P, B * TOP])
        h, hT = sb("h", [P, 2, 512]), sb("hT", [P, 2, F, P])
        o = sb("o", [P, 2, D])
        x_ps, p_ps, h_ps, t_ps, z_ps = (ps("x_ps", [P, 2, 512]), ps("p_ps", [P, 512]), ps("h_ps", [P, 2, 512]),
                                        ps("t_ps", [P, F, P]), ps("z_ps", [P, 2, 512]))
        half_set, ln_ready, pow_ready, steps = sem("half_set"), sem("ln_ready"), sem("pow_ready"), sem("steps")
        xn_ready, x_turned, xT_ready, x_sum = sem("xn_ready"), sem("x_turned"), sem("xT_ready"), sem("x_sum")
        mean_done = sem("mean_done")

        with nc.Block() as block:

            @block.gpsimd
            def _(pool):
                pool.memset(lnv[:, 5, :], -0.5).then_inc(half_set, 1)
                pool.wait_ge(half_set, 1)
                pool.wait_ge(ln_ready, 1)
                nc.gpsimd.tensor_tensor(rstd[:], lnv[:, 4, :], lnv[:, 5, :], ALU.pow).then_inc(pow_ready, 1)

                def step(b, u, last=None):
                    pool.wait_ge(xn_ready, b + 1)
                    nc.gpsimd.tensor_tensor(m["x"][:, b, :], m["x"][:, b, :], xn[:, u, :], ALU.add).then_inc(x_sum, 1)

                over_batches(pool, step)

            @block.vector
            def _(dve):
                layernorm_stats(nc, dve, m, lnv, rstd, nmr, steps, ln_ready, pow_ready)

                def step(b, u, last=None):
                    wait(dve, x_turned, b - 1)
                    wait(dve, x_sum, b - 1)
                    dve.tensor_scalar(xn[:, u, :], m["x"][:, b, :], rstd[:, bass.ds(b, 1)], nmr[:, bass.ds(b, 1)],
                                      ALU.mult, ALU.add).then_inc(xn_ready, 1)

                over_batches(dve, step)
                dve.wait_ge(x_turned, B)
                dve.tensor_copy(meanT[:], p_ps[:, 0:B])

            @block.scalar
            def _(act):
                def step(b, u, last=None):
                    act.wait_ge(x_turned, b + 1)
                    act.activation(m["big"][:, b, :], x_ps[:, u, 0:P], ACT.Copy).then_inc(xT_ready, 1)

                over_batches(act, step)

            @block.tensor
            def _(pe):
                def step(b, u, last=None):
                    pe.wait_ge(xn_ready, b + 1)
                    wait(pe, xT_ready, b - 1)
                    pe.matmul(p_ps[:, bass.ds(b, 1)], xn[:, u, :], m["mean"][:], start=True, stop=True)
                    pe.transpose(x_ps[:, u, 0:P], xn[:, u, :], m["mat"]["ident"]).then_inc(x_turned, 1)

                over_batches(pe, step)

        c_steps, h1_done, h1_ready, hT_done, hT_ready, l_done = (sem("c_steps"), sem("h1_done"), sem("h1_ready"),
                                                                 sem("hT_done"), sem("hT_ready"), sem("l_done"))
        tanh_ready, act_ready, exp_ready, pick_ready, row_in, w_done = (sem("tanh_ready"), sem("act_ready"), sem("exp_ready"),
                                                                        sem("pick_ready"), sem("row_in"), sem("w_done"))
        with nc.Block() as block:

            @block.tensor
            def _(pe):
                pe.matmul(p_ps[0:B, 64:96], meanT[:], m["z_w1"][:], start=True, stop=True).then_inc(h1_done, 1)
                pe.wait_ge(tanh_ready, 1)
                pe.matmul(p_ps[0:B, 128:160], hid[:], m["mat"]["ident"][0:B, 0:B], start=True, stop=True).then_inc(hT_done, 1)
                pe.wait_ge(hT_ready, 1)
                pe.matmul(p_ps[0:B, 192:192 + E], hidT[:], m["z_w2"][:], start=True, stop=True).then_inc(l_done, 1)
                pe.wait_ge(row_in, 32)
                pe.matmul(x_ps[:, 0, 0:B * TOP], m["ones"][:], w_row[:], start=True, stop=True).then_inc(w_done, 1)

            @block.scalar
            def _(act):
                act.wait_ge(h1_ready, 1)
                act.activation(hid[:], hid[:], ACT.Tanh).then_inc(tanh_ready, 1)
                act.wait_ge(act_ready, 1)
                act.activation(lg[:], lg[:], ACT.Exp).then_inc(exp_ready, 1)

            @block.vector
            def _(dve):
                c = Chain(dve, c_steps)
                dve.wait_ge(h1_done, 1)
                dve.tensor_tensor(hid[:], p_ps[0:B, 64:96], m["row"]["z_b1"][0:B, 0:32], ALU.add).then_inc(h1_ready, 1)
                dve.wait_ge(hT_done, 1)
                dve.tensor_copy(hidT[:], p_ps[0:B, 128:160]).then_inc(hT_ready, 1)
                dve.wait_ge(l_done, 1)
                c(dve.tensor_tensor(lg[:, 0, :], p_ps[0:B, 192:192 + E], m["row"]["z_b2"][0:B, 0:E], ALU.add))
                softmax_experts(nc, dve, act_ready, exp_ready, c, lg[:], t1[:], B)
                c(dve.max(top[:], lg[:, 0, :]))
                c(dve.max_index(idx[:], top[:], lg[:, 0, :]))
                c(dve.tensor_reduce(t1[:], top[:, 0:TOP], AX.X, ALU.add))
                c(dve.reciprocal(t1[:], t1[:]))
                dve.tensor_scalar(wt[:], top[:, 0:TOP], t1[:, 0:1], None, ALU.mult).then_inc(pick_ready, 1)
                dve.wait_ge(w_done, 1)
                dve.tensor_copy(w_all[:], x_ps[:, 0, 0:B * TOP])

            @block.sync
            def _(sp):
                sp.wait_ge(pick_ready, 1)
                sp.dma_start(idx_row[0:1, :].rearrange("p (b k) -> p b k", k=TOP), idx[:, 0:TOP]).then_inc(row_in, 16)
                sp.dma_start(w_row[0:1, :].rearrange("p (b k) -> p b k", k=TOP), wt[:]).then_inc(row_in, 16)
                sp.wait_ge(row_in, 32)

        xs_ready, h_done, h_ready, t_done, t_ready, z_done, o_ready = (
            sem("xs_ready"), sem("h_done"), sem("h_ready"), sem("t_done"), sem("t_ready"), sem("z_done"), sem("o_ready"))
        stored = [sem("stored0"), sem("stored1")]
        with nc.Block() as block:

            @block.gpsimd
            def _(pool):
                def step(b, u, last=None):
                    wait(pool, h_done, TOP * (b - 1))
                    nc.gpsimd.tensor_copy(xT[:, u, :], m["big"][:, b, :]).then_inc(xs_ready, 1)

                over_batches(pool, step)

            @block.tensor
            def _(pe):
                pe.wait_ge(m["z_in"], 32)

                def up(b, u, k, q):
                    n = TOP * b + k
                    if k == 0:
                        pe.wait_ge(xs_ready, b + 1)
                    wait(pe, h_ready, n - 1)
                    zone = pe.value_load(idx_row[0:1, bass.ds(n, 1)], min_val=0, max_val=E - 1)
                    pe.matmul(h_ps[:, q % 2, :], xT[:, u, :], m["z_wa"][:, bass.ds(zone * 512, 512)], start=True, stop=True)\
                        .then_inc(h_done, 1)
                    return zone

                def turn(b, k, q):
                    n = TOP * b + k
                    pe.wait_ge(h_ready, n + 1)
                    wait(pe, t_ready, n)
                    for f in range(F):
                        last = pe.transpose(t_ps[:, f, :], h[:, q % 2, f * P:(f + 1) * P], m["mat"]["ident"])
                    last.then_inc(t_done, 1)

                def down(b, u, k, q, zone):
                    n = TOP * b + k
                    pe.wait_ge(t_ready, n + 1)
                    if k == 0:
                        wait(pe, o_ready, b - 1)
                    for f in range(F):
                        last = pe.matmul(z_ps[:, u, 0:D], hT[:, q % 2, f, :], m["z_wb"][:, bass.ds(zone, 1), f * P:(f + 1) * P],
                                         start=(k == 0 and f == 0), stop=(k == TOP - 1 and f == F - 1))
                    if k == TOP - 1:
                        last.then_inc(z_done, 1)

                def step(b, u, last=None):
                    at = [TOP * u + k for k in range(TOP)]
                    e0 = up(b, u, 0, at[0])
                    e1 = up(b, u, 1, at[1])
                    turn(b, 0, at[0])
                    down(b, u, 0, at[0], e0)
                    e2 = up(b, u, 2, at[2])
                    turn(b, 1, at[1])
                    down(b, u, 1, at[1], e1)
                    turn(b, 2, at[2])
                    down(b, u, 2, at[2], e2)

                over_batches(pe, step)

            @block.scalar
            def _(act):
                act.preload_act_table(ACT.Gelu_apprx_tanh)

                def step(b, u, last=None):
                    for k in range(TOP):
                        n, q = TOP * b + k, (TOP * u + k) % 2
                        act.wait_ge(h_done, n + 1)
                        wait(act, t_done, n - 1)
                        act.activation(h[:, q, :], h_ps[:, q, :], ACT.Gelu_apprx_tanh).then_inc(h_ready, 1)

                over_batches(act, step)

            @block.vector
            def _(dve):
                def step(b, u, last=None):
                    for k in range(TOP):
                        n, q = TOP * b + k, (TOP * u + k) % 2
                        dve.wait_ge(t_done, n + 1)
                        if k == 2:
                            wait(dve, z_done, b)
                        dve.tensor_scalar(hT[:, q], t_ps[:], w_all[:, bass.ds(n, 1)], None, ALU.mult).then_inc(t_ready, 1)
                    dve.wait_ge(z_done, b + 1)
                    wait(dve, stored[u], 8 * (b - u))
                    dve.tensor_tensor(o[:, u, :], m["x"][:, b, :], z_ps[:, u, 0:D], ALU.add).then_inc(o_ready, 1)

                over_batches(dve, step)

            @block.sync
            def _(sp):
                def step(b, u, last=None):
                    sp.wait_ge(o_ready, b + 1)
                    sp.dma_start(out[:, b, :], o[:, u, :]).then_inc(stored[u], 16)

                over_batches(sp, step)
                for u in range(2):
                    sp.wait_ge(stored[u], 8 * B)

        sem.clear()




def load(nc, m, a):
    with ExitStack() as ctx:
        sem = Semaphores(nc, ctx, "load")

        x_in, c_in, w_in = sem("x_in"), sem("c_in"), sem("w_in")
        steps, lam_ready, lam_exp = sem("steps"), sem("lam_ready"), sem("lam_exp")
        lq = ctx.enter_context(nc.sbuf_tensor("lq", [P, 4, 4], F32))
        lp = ctx.enter_context(nc.sbuf_tensor("lp", [P, 2, 4], F32))
        ls = ctx.enter_context(nc.sbuf_tensor("ls", [P, 2], F32))
        small = [("cols", a["cols"]), ("router_w", a["router_w"]), ("gate_w", a["gate_w"]), ("z_w1", a["z_w1"]),
                 ("z_w2", a["z_w2"]), ("down", a["down"]), ("iota", a["iota"]), ("maskq", a["maskq"]), ("maskk", a["maskk"]),
                 ("s_b1", a["s_b1"]), ("s_b2", a["s_b2"]), ("s_hot", a["s_hot"])]
        with nc.Block() as block:

            @block.sync
            def _(sp):
                for i in range(4):
                    sp.dma_start(m["x"][:, 8 * i:8 * i + 8, :], a["x"][:, 8 * i:8 * i + 8, :]).then_inc(x_in, 16)
                sp.dma_start(m["mats"][:], a["mats"]).then_inc(w_in, 16)
                for name, src in small:
                    sp.dma_start(m[name][:], src).then_inc(w_in, 16)
                for i, (s, (q, k)) in enumerate(m["sel"].items()):
                    sp.dma_start(q[:], a[s + "_q"]).then_inc(w_in, 16)
                    sp.dma_start(k[:], a[s + "_k"]).then_inc(w_in, 16)

            @block.scalar
            def _(act):
                act.dma_start(m["ctxT"][:], a["ctxT"]).then_inc(c_in, 16)
                act.dma_start(m["rows"][:], a["rows"].partition_broadcast(P)).then_inc(w_in, 16)
                act.dma_start(lq[:], a["lams"].partition_broadcast(P)).then_inc(c_in, 16)
                for name in ("e_w1", "e_w2", "s_w1", "s_w2", "s_w3", "s_up", "s_down"):
                    act.dma_start(m[name][:], a[name]).then_inc(m["weights_in"], 16)
                act.wait_ge(lam_ready, 1)
                act.activation(ls[:], ls[:], ACT.Exp).then_inc(lam_exp, 1)

            @block.vector
            def _(dve):
                dve.wait_ge(x_in, 64)
                with dve.Fori(0, B) as b:
                    dve.bn_stats(m["stats"][:, b, :], m["x"][:, b, :])
                dve.memset(m["onesb"][:], 1.0)
                dve.memset(m["mean"][:], 1.0 / P)
                dve.memset(m["ones"][:], 1.0)
                dve.wait_ge(c_in, 32)
                c = Chain(dve, steps)
                c(dve.tensor_tensor(lp[:], lq[:, 0:4:2, :], lq[:, 1:4:2, :], ALU.mult))
                c(dve.tensor_reduce(ls[:], lp[:], AX.X, ALU.add))
                dve.sem_inc(lam_ready, 1)
                dve.wait_ge(lam_exp, 1)
                dve.scalar_tensor_tensor(m["lam"][:], ls[:, 0:1], LAMBDA_INIT, ls[:, 1:2], ALU.add, ALU.subtract)
                dve.wait_ge(w_in, 16 * (2 + len(small) + 2 * len(m["sel"])))
                dve.tensor_copy(m["identb"][:], m["mat"]["ident"])
                dve.tensor_scalar(m["negident"][:], m["mat"]["ident"], -1.0, None, ALU.mult)

        sem.clear()


def program(nc, a, out):
    with ExitStack() as ctx:
        def sb(n, shape, dt=F32):
            return ctx.enter_context(nc.sbuf_tensor(n, shape, dt))

        m = {}
        m["x"] = sb("x_all", [P, B, D])
        m["ctxT"] = sb("ctxT", [P, B, P])
        m["big"] = sb("big", [P, B, P])
        m["stats"] = sb("stats", [P, B, 6])
        m["mats"] = sb("mats", [P, len(MATS), P])
        m["cols"] = sb("cols", [P, len(COLS)])
        m["rows"] = sb("rows", [P, len(ROWS), P])
        m["mat"] = {n: m["mats"][:, i, :] for i, n in enumerate(MATS)}
        m["col"] = {n: m["cols"][:, i:i + 1] for i, n in enumerate(COLS)}
        m["row"] = {n: m["rows"][:, i, :] for i, n in enumerate(ROWS)}
        m["sel"] = {"sel8": (sb("sel8_q", [P, 2, 4, P], F16), sb("sel8_k", [P, 2, 4, P], F16)),
                    "sel4": (sb("sel4_q", [P, 2, 4, P], F16), sb("sel4_k", [P, 2, 4, P], F16)),
                    "sel4x2": (sb("sel4x2_q", [P, 2, 8, P], F16), sb("sel4x2_k", [P, 2, 8, P], F16))}
        m.update({"sel8": m["sel"]["sel8"], "sel4": m["sel"]["sel4"], "sel4x2": m["sel"]["sel4x2"]})
        m["maskq"] = sb("maskq", [P, B, P], U8)
        m["maskk"] = sb("maskk", [P, B, P], U8)
        m["identb"], m["negident"], m["onesb"] = (sb("identb", [P, P], BF16), sb("negident", [P, P], BF16),
                                                  sb("onesb", [P, P], BF16))
        m["mean"], m["ones"], m["lam"] = sb("mean", [P, 1]), sb("ones", [1, P]), sb("lam", [P, 1])
        m["router_w"], m["gate_w"] = sb("router_w", [P, E]), sb("gate_w", [P, E])
        m["z_w1"], m["z_w2"] = sb("z_w1", [P, 32]), sb("z_w2", [32, E])
        m["down"], m["iota"] = sb("down", [P, E]), sb("iota", [P, 32])
        m["s_b1"], m["s_b2"], m["s_hot"] = sb("s_b1", [E, P]), sb("s_b2", [E + 1, P]), sb("s_hot", [E + 1, 3, 512])
        m["logits"] = sb("logits", [P, B, E])
        m["weights_in"] = ctx.enter_context(nc.semaphore("weights_in"))
        m["weights_count"] = 16 * 7
        m["m_in"], m["z_in"] = (ctx.enter_context(nc.semaphore("m_in")), ctx.enter_context(nc.semaphore("z_in")))
        m["pool"] = sb("pool", [P, 3, 4096])
        m["e_w1"] = m["pool"][:, 0].rearrange("p (e f) -> p e f", e=E)
        m["e_w2"] = m["pool"][:, 1].rearrange("p (e c d) -> p e c d", e=E, c=4)
        m["z_wa"] = m["pool"][:, 0]
        m["z_wb"] = m["pool"][:, 1].rearrange("p (e n) -> p e n", e=E)
        m["m_w1"] = m["pool"][:, 0, 0:2048].rearrange("p (e f) -> p e f", e=E)
        m["m_w2"] = m["pool"][:, 0, 2048:4096].rearrange("p (e c d) -> p e c d", e=E, c=2)
        m["m_b2"] = m["pool"][:, 1, 0:2048].rearrange("p (b d) -> p b d", b=16)
        m["s_w1"], m["s_w3"], m["s_w2"] = sb("s_w1", [P, 2, P]), sb("s_w3", [P, 2, P]), sb("s_w2", [P, 2, P])
        m["s_up"], m["s_down"] = sb("s_up", [P, E, P]), sb("s_down", [P, E, P])

        load(nc, m, a)
        attention(nc, m, "a0", 16, 8, 8, 8 ** -0.5, False, False, False, "x", "sel8")
        expert_choice(nc, m)
        recurrence(nc, m)
        attention(nc, m, "a1", 16, 4, 4, 0.5, True, False, False, "moe", "sel4",
                  [(m["m_w1"], a["m_w1"]), (m["m_w2"], a["m_w2"]), (m["m_b2"], a["m_b2"])], m["m_in"])
        top_two_mixture(nc, m)
        attention(nc, m, "a2", 16, 8, 8, 8 ** -0.5, False, True, False, "x", "sel8")
        hashed_mixture(nc, m)
        attention(nc, m, "a3", 32, 4, 8, 0.5, False, False, True, "x", "sel4x2",
                  [(m["z_wa"], a["z_wa"]), (m["z_wb"], a["z_wb"])], m["z_in"])
        zones(nc, m, a, out)



def lay_out(i):
    f = np.float32

    def t(n):
        return np.ascontiguousarray(np.asarray(i[n]).T)

    def g(n):
        return np.asarray(i[n])

    def spread(w, n=4, by=8):
        w = w.reshape(-1, H, n)
        o = np.zeros((w.shape[0], H, by), f)
        o[:, :, :n] = w
        return o.reshape(-1, H * by)

    def wide(w):
        o = np.zeros((P, P), f)
        o[:w.shape[0], :w.shape[1]] = w
        return o

    def row(v):
        o = np.zeros(P, f)
        o[:v.size] = v.reshape(-1)
        return o

    ip, ib = g("L3_xattn_in_proj_weight"), g("L3_xattn_in_proj_bias")
    mats = {"a0_q": t("L0_xattn_w_q"), "a0_k": t("L0_xattn_w_k"), "a0_v": t("L0_xattn_w_v"), "a0_o": t("L0_xattn_w_o"),
            "r_wi": t("L1_xattn_Wi"), "r_wg": t("L1_xattn_Wg"), "r_a": t("L1_xattn_A"), "r_bm": t("L1_xattn_Bm"),
            "r_wo": t("L1_xattn_Wo"), "a1_q": g("L1_ffn_q_w"), "a1_k": spread(g("L1_ffn_k_w")),
            "a1_v": wide(g("L1_ffn_v_w")), "a1_o": g("L1_ffn_o_w"), "a2_q": g("L2_xattn_Wq"), "a2_k": g("L2_xattn_Wk"),
            "a2_v": g("L2_xattn_Wv"), "a2_o": g("L2_xattn_Wo"), "a3_q": ip[:P].T, "a3_k": ip[P:2 * P].T,
            "a3_v": ip[2 * P:].T, "a3_o": t("L3_xattn_out_proj_weight"), "ident": np.eye(P, dtype=f),
            "tri": np.triu(np.ones((P, P), f))}
    b1 = g("L1_ffn_b1").reshape(-1, P)
    cols = {"a0_q": g("L0_xattn_b_q"), "a0_k": g("L0_xattn_b_k"), "a1_q": g("L1_ffn_q_b"),
            "a1_k": spread(g("L1_ffn_k_b")[None])[0], "a1_o": g("L1_ffn_o_b"), "a2_q": g("L2_xattn_bq"),
            "a2_k": g("L2_xattn_bk"), "a3_q": ib[:P], "a3_k": ib[P:2 * P], "r_bi": g("L1_xattn_bi"), "r_bg": g("L1_xattn_bg"),
            "decay": np.repeat(g("L1_xattn_decay").reshape(H), D // H), "sb1_0": g("L2_ffn_sb1")[:P],
            "sb1_1": g("L2_ffn_sb1")[P:], "sb3_0": g("L2_ffn_sb3")[:P], "sb3_1": g("L2_ffn_sb3")[P:]}
    cols.update({f"m_b1_{k}": b1[k] for k in range(16)})
    rows = {"a0_v": g("L0_xattn_b_v"), "a0_o": g("L0_xattn_b_o"), "a1_v": row(g("L1_ffn_v_b")), "a2_v": g("L2_xattn_bv"),
            "a2_o": g("L2_xattn_bo"), "a3_v": ib[2 * P:], "a3_o": g("L3_xattn_out_proj_bias"), "r_bo": g("L1_xattn_bo"),
            "router_b": row(g("L1_ffn_router_b")), "z_b1": row(g("L3_ffn_b1")), "z_b2": row(g("L3_ffn_b2"))}

    def select(nblk, hd, parts, rows_of=None):
        o = np.zeros((P, 2, nblk, P), np.float16)
        for blk in range(nblk):
            for grp in range(4):
                src = (4 * blk + grp) * (P // (4 * nblk))
                for s, part in enumerate(parts):
                    for d in range(hd):
                        o[src + d, part, blk, 32 * grp + s * hd + d] = 1
        return o

    mask = g("mask_Bx1xSxS2_bk0").reshape(B, P, P)
    b2 = g("L1_ffn_b2")
    m_b2 = np.zeros((16, E, 16, P), f)
    for k in range(16):
        m_b2[k, :, k] = b2
    hot = np.zeros((E + 1, 3, 8, 64), f)
    for r in range(8):
        for k in range(2):
            hot[HASHED[k][r], k, r] = 1
            hot[HASHED[k][r], 2, r] += 1
    hot[E, 2] = 2
    w2 = g("L0_ffn_w2").reshape(E, 4, P, D)
    return {
        "x": g("x").transpose(1, 0, 2), "ctxT": g("ctx_1024").transpose(2, 0, 1),
        "mats": np.stack([mats[n] for n in MATS], 1), "cols": np.stack([cols[n] for n in COLS], 1),
        "rows": np.stack([rows[n] for n in ROWS], 0),
        "sel8_q": select(4, 8, (0, 1, 0)), "sel8_k": select(4, 8, (0, 0, 1)),
        "sel4_q": select(4, 4, (0, 1, 0)), "sel4_k": select(4, 4, (0, 0, 1)),
        "sel4x2_q": select(8, 4, (0, 1, 0)), "sel4x2_k": select(8, 4, (0, 0, 1)),
        "maskq": mask.transpose(1, 0, 2), "maskk": mask.transpose(2, 0, 1),
        "router_w": g("L1_ffn_router_w"), "gate_w": g("L0_ffn_gate_w"), "z_w1": g("L3_ffn_W1"), "z_w2": g("L3_ffn_W2"),
        "down": np.tile(np.arange(E, 0, -1, dtype=f), (P, 1)), "iota": np.tile(np.arange(1, 33, dtype=f), (P, 1)),
        "s_b1": g("L2_ffn_b1"), "s_b2": np.concatenate([g("L2_ffn_b2"), g("L2_ffn_sb2")[None]], 0),
        "s_hot": hot.reshape(E + 1, 3, 512),
        "lams": np.stack([g("L3_xattn_lambda_q1"), g("L3_xattn_lambda_k1"), g("L3_xattn_lambda_q2"),
                          g("L3_xattn_lambda_k2")]),
        "e_w1": g("L0_ffn_w1").transpose(1, 0, 2), "e_w2": w2.transpose(2, 0, 1, 3),
        "m_w1": g("L1_ffn_w1").transpose(1, 0, 2), "m_w2": g("L1_ffn_w2").reshape(E, 2, P, D).transpose(2, 0, 1, 3),
        "m_b2": m_b2.reshape(P, 16, P),
        "s_w1": g("L2_ffn_sw1").reshape(P, 2, P), "s_w3": g("L2_ffn_sw3").reshape(P, 2, P),
        "s_w2": g("L2_ffn_sw2").reshape(2, P, P).transpose(1, 0, 2),
        "s_up": g("L2_ffn_w1").transpose(1, 0, 2), "s_down": g("L2_ffn_w2").transpose(1, 0, 2),
        "z_wa": g("L3_ffn_Wa").transpose(1, 0, 2).reshape(P, 4096),
        "z_wb": g("L3_ffn_Wb").reshape(E, 4, P, D).transpose(2, 0, 1, 3).reshape(P, E, 512),
    }


def kernel(**inputs):
    import concourse.bacc as bacc
    from concourse.bass_utils import run_bass_kernel_spmd

    nc = bacc.Bacc("TRN2", target_bir_lowering=False, num_devices=1)
    arrays = {f"in_{n}": np.ascontiguousarray(v) for n, v in lay_out(inputs).items()}
    a = {n[3:]: nc.dram_tensor(n, v.shape, mybir.dt.from_np(v.dtype), kind="ExternalInput").ap() for n, v in arrays.items()}
    out = nc.dram_tensor("out", (P, B, D), F32, kind="ExternalOutput").ap()
    program(nc, a, out)
    r = run_bass_kernel_spmd(nc, [arrays], core_ids=[0])
    return np.ascontiguousarray(r.results[0]["out"].transpose(1, 0, 2))
```

```python
from contextlib import ExitStack

import numpy as np
import concourse.bass as bass
from concourse import mybir
from concourse.alu_op_type import AluOpType as ALU

F32 = mybir.dt.float32
F16 = mybir.dt.float16
BF16 = mybir.dt.bfloat16
U32 = mybir.dt.uint32
I32 = mybir.dt.int32
U8 = mybir.dt.uint8
ACT = mybir.ActivationFunctionType
AX = mybir.AxisListType

P = 128
B = 32
D = 128
H = 16
E = 8
EPS = 1e-5
NEG = -1.0e9
LAMBDA_INIT = 0.2
HASHED = [[(11 * r + k * 7919) % 8 for r in range(8)] for k in range(2)]

MATS = ["a0_q", "a0_k", "a0_v", "a0_o", "r_wi", "r_wg", "r_a", "r_bm", "r_wo", "a1_q", "a1_k", "a1_v", "a1_o",
        "a2_q", "a2_k", "a2_v", "a2_o", "a3_q", "a3_k", "a3_v", "a3_o", "ident", "tri"]
COLS = ["a0_q", "a0_k", "a1_q", "a1_k", "a1_o", "a2_q", "a2_k", "a3_q", "a3_k", "r_bi", "r_bg", "decay",
        "sb1_0", "sb1_1", "sb3_0", "sb3_1"] + [f"m_b1_{i}" for i in range(16)]
ROWS = ["a0_v", "a0_o", "a1_v", "a2_v", "a2_o", "a3_v", "a3_o", "r_bo", "router_b", "z_b1", "z_b2"]


class Chain:

    def __init__(self, eng, sem, at=0):
        self.eng, self.sem, self.at, self.n = eng, sem, at, 0

    def link(self, ins):
        ins.then_inc(self.sem, 1)
        self.n += 1
        self.eng.wait_ge(self.sem, self.at + self.n)

    def __call__(self, ins):
        self.link(ins)


class Semaphores:

    def __init__(self, nc, ctx, name):
        self.nc, self.ctx, self.name, self.taken = nc, ctx, name, []

    def __call__(self, n):
        self.taken.append(self.ctx.enter_context(self.nc.semaphore(f"{self.name}_{n}")))
        return self.taken[-1]

    def clear(self):
        with self.nc.Block() as block:

            @block.gpsimd
            def _(pool):
                for s in self.taken:
                    pool.sem_clear(s)


def wait(eng, sem, value):
    if isinstance(value, int) and value < 1:
        return
    eng.wait_ge(sem, value)


def over_batches(eng, step, n=B):
    step(0, 0)
    step(1, 1)
    with eng.Fori(1, n // 2 - 1) as i:
        for u in range(2):
            step(2 * i + u, u)
    step(n - 2, 0, n - 1)
    step(n - 1, 1, n - 1)


def attention(nc, m, name, nsub, hd, vd, scale, own, masked, differs, ends, sel, ahead=(), ahead_in=None):
    nblk = nsub // 4
    NH = nblk // 4
    NQ = nblk
    NE = NQ // 2
    R = 3 * hd
    V1 = vd + 1
    VW = H * vd
    with ExitStack() as ctx:
        def sb(n, shape, dt=F32):
            return ctx.enter_context(nc.sbuf_tensor(f"{name}_{n}", shape, dt))

        def ps(n, shape, dt=F32):
            return ctx.enter_context(nc.psum_tensor(f"{name}_{n}", shape, dt))

        sem = Semaphores(nc, ctx, name)

        selq, selk = m[sel]
        xn = sb("xn", [P, 2, D])
        xb = sb("xb", [P, 2, D])
        xnT = sb("xnT", [P, 2, P])
        src = xnT if own else sb("ctxs", [P, 2, P])
        hi = sb("hi", [P, 2, 2, P], F16)
        lo = sb("lo", [P, 2, 2, P], F16)
        qst = sb("qst", [P, 2, nblk, P], F16)
        kst = sb("kst", [P, 2, nblk, P], F16)
        v32 = sb("v32", [P, H, vd])
        vhi = sb("vhi", [P, 2, H, V1], F16)
        vlo = sb("vlo", [P, 2, H, vd], F16)
        zero = sb("zero", [P, H, vd])
        mx = sb("mx", [P, 2, 4], F16)
        eight = sb("eight", [P, 1])
        pr = sb("pr", [P, 2, 4, P])
        phi = sb("phi", [P, 4, 4, P], F16)
        plo = sb("plo", [P, 4, 4, P], F16)
        rec = sb("rec", [P, nsub])
        on = sb("on", [P, 2, D])
        on2 = sb("on2", [P, D])
        oT = sb("oT", [P, 2, P])
        lnv = sb("lnv", [P, 6, B])
        rstd = sb("rstd", [P, B])
        nmr = sb("nmr", [P, B])
        qm = sb("qm", [P, 2, P]) if masked else None
        nbq = sb("nbq", [P, 2, P], BF16) if masked else None
        nbk = sb("nbk", [P, 2, P], BF16) if masked else None
        keepb = sb("keepb", [P, 2, P], BF16) if masked else None
        anyq = sb("anyq", [P, 2]) if masked else None
        anyb = sb("anyb", [P, 2, P]) if masked else None
        mT = sb("mT", [P, 2, P]) if ends == "moe" else None

        s_ps = ps("s", [P, 2, 4, P])
        st_ps = ps("st", [P, 2, 4, P])
        stack_ps = ps("stack", [P, 4, P])
        q_ps = ps("q", [P, 4, P])
        k_ps = ps("k", [P, 4, P])
        o_ps = ps("o", [P, 512])
        o_h = o_ps[:, 0:nsub * V1].rearrange("p (h c) -> p h c", c=V1)

        ln_ready, pow_ready = sem("ln_ready"), sem("pow_ready")
        xn_ready, xT_done, xnT_ready = sem("xn_ready"), sem("xT_done"), sem("xnT_ready")
        src_ready, xb_ready = sem("src_ready"), sem("xb_ready")
        kv_done, q_done = sem("kv_done"), sem("q_done")
        khi, klo, qhi, qlo = sem("khi"), sem("klo"), sem("qhi"), sem("qlo")
        v32_ready, vhi_ready, vlo_ready = sem("v32_ready"), sem("vhi_ready"), sem("vlo_ready")
        kstack, qstack, kst_ready, qst_ready = sem("kstack"), sem("qstack"), sem("kst_ready"), sem("qst_ready")
        s_done, mx_ready, st_done, pv_done = sem("s_done"), sem("mx_ready"), sem("st_done"), sem("pv_done")
        pr_ready, phi_ready, even_lo, odd_lo = sem("pr_ready"), sem("phi_ready"), sem("even_lo"), sem("odd_lo")
        on_done, oT_done, oT_ready, y_done, x_done = (sem("on_done"), sem("oT_done"), sem("oT_ready"),
                                                      sem("y_done"), sem("x_done"))
        steps, ones_set = sem("steps"), sem("ones_set")
        keep_ready, cnt_done, any_ready, mask_steps, nbk_ready, qm_ready = (
            sem("keep_ready"), sem("cnt_done"), sem("any_ready"), sem("mask_steps"), sem("nbk_ready"), sem("qm_ready"))
        mT_ready, lg_done, lg_ready, mT_kept, x_sum = (sem("mT_ready"), sem("lg_done"), sem("lg_ready"),
                                                       sem("mT_kept"), sem("x_sum"))

        def there(b, d):
            return not isinstance(b, int) or 0 <= b + d < B

        def wait_low(eng, b, j, back=0):
            wait(eng, odd_lo if j % 2 else even_lo, NE * b + j // 2 + 1 - back)

        def low_part(eng, ops, b, j):
            n = NQ * b + j
            eng.wait_ge(pr_ready, n + 1)
            eng.wait_ge(phi_ready, n + 1)
            wait(eng, pv_done, n - 3)
            ops.tensor_tensor(plo[:, j % 4], pr[:, j % 2], phi[:, j % 4], ALU.subtract)\
                .then_inc(odd_lo if j % 2 else even_lo, 1)

        with nc.Block() as block:

            @block.sync
            def _(sp):
                if ahead:
                    sp.wait_ge(m["weights_in"], m["weights_count"])
                for to, frm in ahead:
                    sp.dma_start(to, frm).then_inc(ahead_in, 16)

            @block.gpsimd
            def _(pool):
                pool.memset(vhi[:], 1.0).then_inc(ones_set, 1)
                pool.memset(on[:], 0.0).then_inc(ones_set, 1)
                pool.memset(eight[:], 8.0).then_inc(ones_set, 1)
                pool.memset(zero[:], 0.0).then_inc(ones_set, 1)
                pool.memset(lnv[:, 5, :], -0.5).then_inc(ones_set, 1)
                pool.wait_ge(ones_set, 5)

                def source(b, u):
                    if own:
                        pool.wait_ge(xn_ready, b + 1)
                        nc.gpsimd.tensor_tensor(m["x"][:, b, :], m["x"][:, b, :], xn[:, u, :], ALU.add).then_inc(x_sum, 1)
                    else:
                        wait(pool, kv_done, b - 1)
                        nc.gpsimd.tensor_copy(src[:, u, :], m["ctxT"][:, b, :]).then_inc(src_ready, 1)

                def split_v(b, u):
                    pool.wait_ge(v32_ready, b + 1)
                    wait(pool, pv_done, NQ * (b - 1))
                    nc.gpsimd.tensor_tensor(vhi[:, u, :, 0:vd], v32[:], zero[:], ALU.add).then_inc(vhi_ready, 1)
                    pool.wait_ge(vhi_ready, b + 1)
                    nc.gpsimd.tensor_tensor(vlo[:, u], v32[:], vhi[:, u, :, 0:vd], ALU.subtract).then_inc(vlo_ready, 1)

                def to_mixture(b, u):
                    pool.wait_ge(mT_ready, b + 1)
                    nc.gpsimd.tensor_copy(m["big"][:, b, :], mT[:, u, :]).then_inc(mT_kept, 1)

                def x_and_bias(b, u):
                    wait(pool, x_done, b - 1)
                    nc.gpsimd.tensor_tensor(xb[:, u, :], m["x"][:, b, :], m["row"][f"{name}_o"], ALU.add)\
                        .then_inc(xb_ready, 1)

                if not own:
                    source(0, 0)
                pool.wait_ge(ln_ready, 1)
                nc.gpsimd.tensor_tensor(rstd[:], lnv[:, 4, :], lnv[:, 5, :], ALU.pow).then_inc(pow_ready, 1)
                if own:
                    source(0, 0)
                split_v(0, 0)
                source(1, 1)

                def step(b, u, last=None):
                    if there(b, -1):
                        low_part(pool, nc.gpsimd, b - 1, NQ - 1)
                    if own and there(b, -2):
                        to_mixture(b - 2, u)
                    if there(b, 1):
                        split_v(b + 1, 1 - u)
                    low_part(pool, nc.gpsimd, b, 1)
                    if there(b, 2):
                        source(b + 2, u)
                    for j in range(3, NQ - 1, 2):
                        low_part(pool, nc.gpsimd, b, j)
                    if not own:
                        x_and_bias(b, u)

                over_batches(pool, step)
                low_part(pool, nc.gpsimd, B - 1, NQ - 1)
                if own:
                    to_mixture(B - 2, 0)
                    to_mixture(B - 1, 1)

            @block.vector
            def _(dve):
                layernorm_stats(nc, dve, m, lnv, rstd, nmr, steps, ln_ready, pow_ready)
                LN = LN_STEPS
                per = 5 if differs else 1

                def normalise(b, u):
                    wait(dve, xT_done, b - 1)
                    if own:
                        wait(dve, x_sum, b - 1)
                    dve.tensor_scalar(xn[:, u, :], m["x"][:, b, :], rstd[:, bass.ds(b, 1)], nmr[:, bass.ds(b, 1)],
                                      ALU.mult, ALU.add).then_inc(xn_ready, 1)

                def mask_keep(b, u):
                    wait(dve, cnt_done, b - 1)
                    dve.tensor_copy(keepb[:, u, :], m["maskk"][:, b, :]).then_inc(keep_ready, 1)

                def mask_any(b, u):
                    dve.wait_ge(cnt_done, b + 1)
                    dve.wait_ge(xnT_ready, b + 1)
                    dve.tensor_scalar(anyb[:, u, :], q_ps[:, 2, :], 1.0, None, ALU.min).then_inc(any_ready, 1)

                def mask_rows(b, u):
                    wait(dve, s_done, NQ * (b - 1))
                    wait(dve, st_done, NQ * (b - 1))
                    dve.wait_ge(any_ready, b + 1)
                    dve.tensor_reduce(anyq[:, u:u + 1], m["maskq"][:, b, :], AX.X, ALU.max).then_inc(mask_steps, 1)
                    dve.tensor_scalar(nbq[:, u, :], m["maskq"][:, b, :], -1.0, -NEG, ALU.add, ALU.mult).then_inc(mask_steps, 1)
                    dve.scalar_tensor_tensor(nbk[:, u, :], keepb[:, u, :], -1.0, anyb[:, u, :], ALU.add, ALU.mult)\
                        .then_inc(mask_steps, 1)
                    dve.wait_ge(mask_steps, 3 * b + 3)
                    dve.tensor_scalar(nbq[:, u, :], nbq[:, u, :], anyq[:, u:u + 1], None, ALU.mult).then_inc(nbk_ready, 1)
                    dve.tensor_scalar(nbk[:, u, :], nbk[:, u, :], -NEG, None, ALU.mult).then_inc(nbk_ready, 1)

                def k_low(b, u):
                    dve.wait_ge(khi, b + 1)
                    wait(dve, kstack, NH * (b - 1))
                    dve.scalar_tensor_tensor(lo[:, u, 1, :], k_ps[:, 0, :], m["col"][f"{name}_k"], hi[:, u, 1, :],
                                             ALU.add, ALU.subtract).then_inc(klo, 1)

                def v_bias(b, u):
                    dve.wait_ge(khi, b + 1)
                    wait(dve, vlo_ready, b)
                    dve.tensor_tensor(v32[:], k_ps[:, 1, 0:VW].rearrange("p (h c) -> p h c", c=vd),
                                      m["row"][f"{name}_v"][:, 0:VW].rearrange("p (h c) -> p h c", c=vd), ALU.add)\
                        .then_inc(v32_ready, 1)

                def q_masked(b, u):
                    dve.wait_ge(q_done, b + 1)
                    dve.wait_ge(any_ready, b + 1)
                    wait(dve, qhi, b - 1)
                    dve.scalar_tensor_tensor(qm[:, u, :], q_ps[:, 1, :], m["col"][f"{name}_q"], anyb[:, u, :],
                                             ALU.add, ALU.mult).then_inc(qm_ready, 1)

                def q_low(b, u):
                    dve.wait_ge(qhi, b + 1)
                    wait(dve, qstack, NH * (b - 1))
                    if masked:
                        dve.wait_ge(qm_ready, b + 1)
                        dve.tensor_tensor(lo[:, u, 0, :], qm[:, u, :], hi[:, u, 0, :], ALU.subtract).then_inc(qlo, 1)
                    else:
                        dve.scalar_tensor_tensor(lo[:, u, 0, :], q_ps[:, 1, :], m["col"][f"{name}_q"], hi[:, u, 0, :],
                                                 ALU.add, ALU.subtract).then_inc(qlo, 1)

                def q_keep(b, u, half):
                    dve.wait_ge(qstack, NH * b + half + 1)
                    wait(dve, st_done, NQ * (b - 1))
                    dve.tensor_copy(qst[:, u, 4 * half:4 * half + 4, :], stack_ps[:]).then_inc(qst_ready, 1)

                def maximum(b, j):
                    n = NQ * b + j
                    dve.wait_ge(s_done, n + 1)
                    wait(dve, st_done, n - 1)
                    dve.tensor_reduce(mx[:, j % 2, :], s_ps[:, j % 2], AX.X, ALU.max).then_inc(mx_ready, 1)

                def divide(b, u):
                    dve.wait_ge(pv_done, NQ * (b + 1))
                    c = Chain(dve, steps, LN + per * b)
                    c(dve.reciprocal(rec[:], o_h[:, :, vd]))
                    out = on[:, u, 0:VW].rearrange("p (h c) -> p h c", c=vd)
                    if differs:
                        o4 = o_h.rearrange("p (h s) c -> p h s c", s=2)
                        r4 = rec[:].rearrange("p (h s) -> p h s", s=2)
                        c(dve.tensor_scalar(rec[:], rec[:], 1.0 - LAMBDA_INIT, None, ALU.mult))
                        c(dve.tensor_tensor(r4[:, :, 1], r4[:, :, 1], m["lam"][:, 0:1].broadcast_to([P, H]), ALU.mult))
                        c(dve.tensor_tensor(on2[:].rearrange("p (h c) -> p h c", c=vd), o4[:, :, 1, 0:vd],
                                            r4[:, :, 1].unsqueeze(2).broadcast_to([P, H, vd]), ALU.mult))
                        c(dve.tensor_tensor(out, o4[:, :, 0, 0:vd], r4[:, :, 0].unsqueeze(2).broadcast_to([P, H, vd]), ALU.mult))
                        dve.scalar_tensor_tensor(on[:, u, :], on2[:], -1.0, on[:, u, :], ALU.mult, ALU.add).then_inc(on_done, 1)
                    else:
                        dve.tensor_tensor(out, o_h[:, :, 0:vd], rec[:].unsqueeze(2).broadcast_to([P, H, vd]), ALU.mult)\
                            .then_inc(on_done, 1)

                def finish(b, u):
                    if own:
                        dve.wait_ge(lg_done, b + 1)
                        dve.tensor_tensor(m["logits"][:, b, :], k_ps[:, 0, 0:E], m["row"]["router_b"][:, 0:E], ALU.add)\
                            .then_inc(lg_ready, 1)
                        return
                    dve.wait_ge(y_done, b + 1)
                    dve.wait_ge(xb_ready, b + 1)
                    dve.tensor_tensor(m["x"][:, b, :], k_ps[:, 3, :], xb[:, u, :], ALU.add).then_inc(x_done, 1)

                def statistics(b):
                    dve.wait_ge(x_done, b + 1)
                    dve.bn_stats(m["stats"][:, b, :], m["x"][:, b, :])

                dve.wait_ge(ones_set, 5)
                normalise(0, 0)
                if masked:
                    mask_keep(0, 0)
                    mask_any(0, 0)
                k_low(0, 0)
                v_bias(0, 0)
                if masked:
                    q_masked(0, 0)
                q_low(0, 0)
                normalise(1, 1)
                if masked:
                    mask_rows(0, 0)
                    mask_keep(1, 1)
                for half in range(NH):
                    q_keep(0, 0, half)
                maximum(0, 0)

                def step(b, u, last=None):
                    maximum(b, 1)
                    if there(b, -2):
                        finish(b - 2, u)
                    if masked and there(b, 1):
                        mask_any(b + 1, 1 - u)
                    if there(b, 1):
                        k_low(b + 1, 1 - u)
                        v_bias(b + 1, 1 - u)
                        if masked:
                            q_masked(b + 1, 1 - u)
                    maximum(b, 2)
                    if there(b, 1):
                        q_low(b + 1, 1 - u)
                    low_part(dve, nc.vector, b, 0)
                    if there(b, -1):
                        divide(b - 1, 1 - u)
                    maximum(b, 3)
                    if NQ == 4 and there(b, 1):
                        q_keep(b + 1, 1 - u, 0)
                    if there(b, 2):
                        normalise(b + 2, u)
                        if masked:
                            mask_keep(b + 2, u)
                    if masked and there(b, 1):
                        mask_rows(b + 1, 1 - u)
                    for j in range(4, NQ):
                        maximum(b, j)
                        if there(b, 1) and j in (5, 6):
                            q_keep(b + 1, 1 - u, j - 5)
                        if j % 2 == 0:
                            low_part(dve, nc.vector, b, j - 2)
                    if there(b, 1):
                        maximum(b + 1, 0)
                    low_part(dve, nc.vector, b, NQ - 2)
                    if not own and there(b, -2):
                        statistics(b - 2)

                over_batches(dve, step)
                finish(B - 2, 0)
                divide(B - 1, 1)
                finish(B - 1, 1)
                if not own:
                    statistics(B - 2)
                    statistics(B - 1)

            @block.scalar
            def _(act):
                act.preload_act_table(ACT.Exp)
                act.wait_ge(ones_set, 5)

                def x_keep(b, u):
                    act.wait_ge(xT_done, b + 1)
                    wait(act, q_done, b - 1)
                    if own:
                        wait(act, kv_done, b - 1)
                    act.activation(xnT[:, u, :], q_ps[:, 0, :], ACT.Copy).then_inc(xnT_ready, 1)

                def k_high(b, u):
                    act.wait_ge(kv_done, b + 1)
                    wait(act, kstack, NH * (b - 1))
                    act.activation(hi[:, u, 1, :], k_ps[:, 0, :], ACT.Identity, bias=m["col"][f"{name}_k"]).then_inc(khi, 1)

                def q_high(b, u):
                    wait(act, qstack, NH * (b - 1))
                    if masked:
                        act.wait_ge(qm_ready, b + 1)
                        act.activation(hi[:, u, 0, :], qm[:, u, :], ACT.Copy).then_inc(qhi, 1)
                        return
                    act.wait_ge(q_done, b + 1)
                    act.activation(hi[:, u, 0, :], q_ps[:, 1, :], ACT.Identity, bias=m["col"][f"{name}_q"]).then_inc(qhi, 1)

                def k_keep(b, u, half):
                    act.wait_ge(kstack, NH * b + half + 1)
                    wait(act, st_done, NQ * (b - 1))
                    act.activation(kst[:, u, 4 * half:4 * half + 4, :], stack_ps[:], ACT.Copy).then_inc(kst_ready, 1)

                def exp(b, j):
                    n = NQ * b + j
                    act.wait_ge(st_done, n + 1)
                    wait(act, pv_done, n - 3)
                    act.activation(phi[:, j % 4], st_ps[:, j % 2], ACT.Exp, bias=eight[:], scale=scale).then_inc(phi_ready, 1)
                    wait_low(act, b, j, 1)
                    act.activation(pr[:, j % 2], st_ps[:, j % 2], ACT.Exp, bias=eight[:], scale=scale).then_inc(pr_ready, 1)

                def o_keep(b, u):
                    act.wait_ge(oT_done, b + 1)
                    act.activation(oT[0:VW, u, :], k_ps[0:VW, 2, :], ACT.Copy).then_inc(oT_ready, 1)

                def m_keep(b, u):
                    act.wait_ge(y_done, b + 1)
                    wait(act, mT_kept, b)
                    act.activation(mT[:, u, :], k_ps[:, 3, :], ACT.Identity, bias=m["col"]["a1_o"]).then_inc(mT_ready, 1)

                x_keep(0, 0)
                k_high(0, 0)
                q_high(0, 0)
                for half in range(NH):
                    k_keep(0, 0, half)
                x_keep(1, 1)

                def step(b, u, last=None):
                    exp(b, 0)
                    if there(b, 1):
                        k_high(b + 1, 1 - u)
                        if not masked:
                            q_high(b + 1, 1 - u)
                    exp(b, 1)
                    if there(b, 1):
                        if masked:
                            q_high(b + 1, 1 - u)
                        k_keep(b + 1, 1 - u, 0)
                    exp(b, 2)
                    if there(b, -1):
                        o_keep(b - 1, 1 - u)
                    if NH == 2 and there(b, 1):
                        k_keep(b + 1, 1 - u, 1)
                    if own and there(b, -1):
                        m_keep(b - 1, 1 - u)
                    for j in range(3, NQ):
                        exp(b, j)
                    if there(b, 2):
                        x_keep(b + 2, u)

                over_batches(act, step)
                o_keep(B - 1, 1)
                if own:
                    m_keep(B - 1, 1)

            @block.tensor
            def _(pe):
                def x_turn(b, u):
                    pe.wait_ge(xn_ready, b + 1)
                    wait(pe, qlo, b)
                    if masked:
                        pe.wait_ge(keep_ready, b + 1)
                        pe.matmul(q_ps[:, 2, :], m["onesb"][:], keepb[:, u, :], start=True, stop=True).then_inc(cnt_done, 1)
                    pe.transpose(q_ps[:, 0, :], xn[:, u, :], m["mat"]["ident"]).then_inc(xT_done, 1)

                def k_dense(b, u):
                    pe.wait_ge(xnT_ready if own else src_ready, b + 1)
                    wait(pe, klo, b)
                    wait(pe, v32_ready, b)
                    wait(pe, lg_ready if own else x_done, b - 2)
                    pe.matmul(k_ps[:, 0, :], m["mat"][f"{name}_k"], src[:, u, :], start=True, stop=True)
                    pe.matmul(k_ps[:, 1, 0:VW], src[:, u, :], m["mat"][f"{name}_v"][:, 0:VW], start=True, stop=True)\
                        .then_inc(kv_done, 1)

                def q_dense(b, u):
                    pe.wait_ge(xnT_ready, b + 1)
                    if masked:
                        pe.wait_ge(any_ready, b + 1)
                    pe.matmul(q_ps[:, 1, :], m["mat"][f"{name}_q"], xnT[:, u, :], start=True, stop=True).then_inc(q_done, 1)

                def stack(b, u, which, half):
                    pe.wait_ge(klo if which else qlo, b + 1)
                    if which:
                        wait(pe, qst_ready, NH * b)
                        wait(pe, kst_ready, NH * b + half)
                    else:
                        pe.wait_ge(kst_ready, NH * (b + 1))
                        wait(pe, qst_ready, NH * b + half)
                    w = selk if which else selq
                    for blk in range(4):
                        c = 4 * half + blk
                        pe.matmul(stack_ps[:, blk, :], w[:, 0, c, :], hi[:, u, which, :], start=True, stop=False)
                        last = pe.matmul(stack_ps[:, blk, :], w[:, 1, c, :], lo[:, u, which, :], start=False, stop=True)
                    last.then_inc(kstack if which else qstack, 1)

                def heads(j):
                    return (j % 4, 4 * (j // 4)) if nblk == 4 else (j // 2, 4 * (j % 2))

                def head(g, blk):
                    return 4 * blk + g

                def scores(b, u, j):
                    n = NQ * b + j
                    if j == 0:
                        pe.wait_ge(kst_ready, NH * (b + 1))
                        pe.wait_ge(qst_ready, NH * (b + 1))
                        if masked:
                            pe.wait_ge(nbk_ready, 2 * (b + 1))
                    wait(pe, mx_ready, n - 1)
                    g, b0 = heads(j)
                    r = slice(32 * g, 32 * g + R)
                    if masked:
                        for i in range(4):
                            pe.matmul(s_ps[:, j % 2, i, :], m["identb"][:], nbq[:, u, :], start=(i == 0), stop=False,
                                      skip_group_check=True)
                    for i in range(4):
                        last = pe.matmul(s_ps[:, j % 2, i, :], qst[r, u, b0 + i, :], kst[r, u, b0 + i, :],
                                         start=not masked, stop=True, skip_group_check=masked)
                    last.then_inc(s_done, 1)

                def scores_by_key(b, u, j):
                    n = NQ * b + j
                    pe.wait_ge(mx_ready, n + 1)
                    wait(pe, pr_ready, n - 1)
                    g, b0 = heads(j)
                    r = slice(32 * g, 32 * g + R)
                    for i in range(4):
                        pe.matmul(st_ps[:, j % 2, i, :], mx[:, j % 2, i:i + 1].broadcast_to([P, P]), m["negident"][:],
                                  start=(i == 0), stop=False, skip_group_check=True)
                        if masked:
                            pe.matmul(st_ps[:, j % 2, i, :], m["identb"][:], nbk[:, u, :], start=False, stop=False,
                                      skip_group_check=True)
                    for i in range(4):
                        last = pe.matmul(st_ps[:, j % 2, i, :], kst[r, u, b0 + i, :], qst[r, u, b0 + i, :],
                                         start=False, stop=True, skip_group_check=True)
                    last.then_inc(st_done, 1)

                def values(b, u, j):
                    n = NQ * b + j
                    if j == 0:
                        pe.wait_ge(vlo_ready, b + 1)
                        wait(pe, on_done, b)
                    pe.wait_ge(phi_ready, n + 1)
                    wait_low(pe, b, j)
                    g, b0 = heads(j)
                    for i in range(4):
                        h = head(g, b0 + i)
                        v = h // 2 if differs else h
                        pe.matmul(o_h[:, h, :], phi[:, j % 4, i, :], vhi[:, u, v, :], start=True, stop=False,
                                  skip_group_check=True)
                        pe.matmul(o_h[:, h, 0:vd], phi[:, j % 4, i, :], vlo[:, u, v, :], start=False, stop=False,
                                  skip_group_check=True)
                        last = pe.matmul(o_h[:, h, :], plo[:, j % 4, i, :], vhi[:, u, v, :], start=False, stop=True,
                                         skip_group_check=True)
                    last.then_inc(pv_done, 1)

                def o_turn(b, u):
                    pe.wait_ge(on_done, b + 1)
                    ahead_of = min(b + 3, B) if isinstance(b, int) else b + 3
                    pe.wait_ge(klo, ahead_of)
                    pe.wait_ge(v32_ready, ahead_of)
                    pe.transpose(k_ps[:, 2, :], on[:, u, :], m["mat"]["ident"]).then_inc(oT_done, 1)

                def project(b, u):
                    pe.wait_ge(oT_ready, b + 1)
                    if own:
                        pe.matmul(k_ps[:, 3, :], m["mat"]["a1_o"][0:VW, :], oT[0:VW, u, :], start=True, stop=True)\
                            .then_inc(y_done, 1)
                    else:
                        pe.matmul(k_ps[:, 3, :], oT[:, u, :], m["mat"][f"{name}_o"], start=True, stop=True).then_inc(y_done, 1)

                def route(b, u):
                    pe.wait_ge(mT_ready, b + 1)
                    pe.matmul(k_ps[:, 0, 0:E], mT[:, u, :], m["router_w"][:], start=True, stop=True).then_inc(lg_done, 1)

                x_turn(0, 0)
                k_dense(0, 0)
                q_dense(0, 0)
                for which in (1, 0):
                    for half in range(NH):
                        stack(0, 0, which, half)
                x_turn(1, 1)
                scores(0, 0, 0)

                def step(b, u, last=None):
                    for j in range(NQ):
                        if j < NQ - 1:
                            scores(b, u, j + 1)
                        elif there(b, 1):
                            scores(b + 1, 1 - u, 0)
                        if there(b, -1) and j == 3:
                            project(b - 1, 1 - u)
                        if there(b, 1) and NH == 1 and j == 2:
                            stack(b + 1, 1 - u, 0, 0)
                        if there(b, 1) and NH == 2 and j in (4, 5):
                            stack(b + 1, 1 - u, 0, j - 4)
                        scores_by_key(b, u, j)
                        if there(b, -1) and j == 2:
                            o_turn(b - 1, 1 - u)
                        if j > 1:
                            values(b, u, j - 2)
                        elif there(b, -1):
                            values(b - 1, 1 - u, NQ - 2 + j)
                        if there(b, 1) and j == 0:
                            k_dense(b + 1, 1 - u)
                            q_dense(b + 1, 1 - u)
                        if there(b, 1) and (j == 1 or (NH == 2 and j == 2)):
                            stack(b + 1, 1 - u, 1, j - 1)
                        if own and there(b, -1) and j == 3:
                            route(b - 1, 1 - u)
                        if there(b, 2) and j == NQ - 1:
                            x_turn(b + 2, u)

                over_batches(pe, step)
                values(B - 1, 1, NQ - 2)
                values(B - 1, 1, NQ - 1)
                o_turn(B - 1, 1)
                project(B - 1, 1)
                if own:
                    route(B - 1, 1)

        sem.clear()


LN_STEPS = 7


def layernorm_stats(nc, dve, m, lnv, rstd, nmr, steps, ln_ready, pow_ready):
    st = m["stats"]
    c = Chain(dve, steps)
    c(dve.tensor_tensor(lnv[:, 0, :], st[:, :, 1], st[:, :, 4], ALU.add))
    c(dve.tensor_tensor(lnv[:, 1, :], st[:, :, 1], st[:, :, 4], ALU.subtract))
    c(dve.tensor_tensor(lnv[:, 2, :], st[:, :, 2], st[:, :, 5], ALU.add))
    c(dve.tensor_tensor(lnv[:, 3, :], lnv[:, 1, :], lnv[:, 1, :], ALU.mult))
    c(dve.tensor_scalar(lnv[:, 2, :], lnv[:, 2, :], 1.0 / D, EPS, ALU.mult, ALU.add))
    c(dve.scalar_tensor_tensor(lnv[:, 4, :], lnv[:, 3, :], 0.25, lnv[:, 2, :], ALU.mult, ALU.add))
    dve.sem_inc(ln_ready, 1)
    dve.wait_ge(pow_ready, 1)
    c(dve.scalar_tensor_tensor(nmr[:], lnv[:, 0, :], -0.5, rstd[:], ALU.mult, ALU.mult))


def recurrence(nc, m):
    T = P
    with ExitStack() as ctx:
        def sb(n, shape, dt=F32):
            return ctx.enter_context(nc.sbuf_tensor(f"r_{n}", shape, dt))

        def ps(n, shape):
            return ctx.enter_context(nc.psum_tensor(f"r_{n}", shape, F32))

        sem = Semaphores(nc, ctx, "r")

        inp, gate, rest = (m["pool"][:, i].rearrange("p (t b) -> p t b", b=B) for i in range(3))
        state = m["big"][:].rearrange("p b t -> p (b t)").rearrange("p (t b) -> p t b", b=B)
        G = 4
        xn = sb("xn", [P, 2, G, D])
        kv = sb("kv", [P, 2, G, T])
        r = sb("r", [P, 2, G, T])
        ret = sb("ret", [P, 2, G, T])
        gi = sb("gi", [P, G, T])
        ms = sb("ms", [P, 2, B])
        sT = sb("sT", [P, 2, T])
        xb = sb("xb", [P, 2, D])
        lnv, rstd, nmr = sb("lnv", [P, 6, B]), sb("rstd", [P, B]), sb("nmr", [P, B])
        xT_ps, in_ps, g_ps = ps("xT_ps", [P, 2, G, T]), ps("in_ps", [P, G, T]), ps("g_ps", [P, G, T])
        z_ps, y_ps = ps("z_ps", [P, 2, 512]), ps("y_ps", [P, 2, 512])

        half_set, ln_ready, pow_ready, steps = sem("half_set"), sem("ln_ready"), sem("pow_ready"), sem("steps")
        xn_ready, xT_done, kv_ready, r_ready, ret_ready = (sem("xn_ready"), sem("xT_done"), sem("kv_ready"),
                                                           sem("r_ready"), sem("ret_ready"))
        in_done, in_ready, g_done, gate_ready, gi_ready, rest_ready = (
            sem("in_done"), sem("in_ready"), sem("g_done"), sem("gate_ready"), sem("gi_ready"), sem("rest_ready"))
        ms_ready, z_done, s_ready = sem("ms_ready"), sem("z_done"), sem("s_ready")
        sT_ready, xb_ready, y_done, x_done = sem("sT_ready"), sem("xb_ready"), sem("y_done"), sem("x_done")
        NG = B // G

        def cols(t, g):
            return t[:, :, bass.ds(G * g, G)].rearrange("p t b -> p b t")

        with nc.Block() as block:

            @block.gpsimd
            def _(pool):
                pool.memset(lnv[:, 5, :], -0.5).then_inc(half_set, 1)
                pool.wait_ge(half_set, 1)
                pool.wait_ge(ln_ready, 1)
                nc.gpsimd.tensor_tensor(rstd[:], lnv[:, 4, :], lnv[:, 5, :], ALU.pow).then_inc(pow_ready, 1)

                def step(g, u, last=None):
                    wait(pool, r_ready, G * (g - 1))
                    c = m["ctxT"][:, bass.ds(G * g, G), :]
                    nc.gpsimd.tensor_tensor(kv[:, u], c, c, ALU.mult).then_inc(kv_ready, 1)
                    pool.wait_ge(gate_ready, g + 1)
                    nc.gpsimd.tensor_tensor(gi[:], cols(gate, g), cols(inp, g), ALU.mult).then_inc(gi_ready, 1)
                    pool.wait_ge(gi_ready, g + 1)
                    nc.gpsimd.tensor_tensor(cols(rest, g), cols(inp, g), gi[:], ALU.subtract).then_inc(rest_ready, 1)

                over_batches(pool, step, NG)

            @block.vector
            def _(dve):
                layernorm_stats(nc, dve, m, lnv, rstd, nmr, steps, ln_ready, pow_ready)

                def normalise(g, u):
                    wait(dve, xT_done, g - 1)
                    for i in range(G):
                        last = dve.tensor_scalar(xn[:, u, i, :], m["x"][:, G * g + i, :], rstd[:, bass.ds(G * g + i, 1)],
                                                 nmr[:, bass.ds(G * g + i, 1)], ALU.mult, ALU.add)
                    last.then_inc(xn_ready, 1)

                normalise(0, 0)

                def step(g, u, last=None):
                    if not (isinstance(g, int) and g == last):
                        normalise(g + 1, 1 - u)
                    dve.wait_ge(kv_ready, g + 1)
                    for i in range(G):
                        dve.tensor_tensor_scan(r[:, u, i, :], m["col"]["decay"].broadcast_to([P, T]), kv[:, u, i, :],
                                               0.0, ALU.mult, ALU.add).then_inc(r_ready, 1)
                    dve.wait_ge(r_ready, G * (g + 1))
                    dve.wait_ge(xT_done, g + 1)
                    wait(dve, in_done, g - 1)
                    dve.tensor_tensor(ret[:, u], xT_ps[:, u], r[:, u], ALU.mult).then_inc(ret_ready, 1)

                over_batches(dve, step, NG)

            @block.tensor
            def _(pe):
                def turn(g, u):
                    pe.wait_ge(xn_ready, g + 1)
                    wait(pe, ret_ready, g - 1)
                    for i in range(G):
                        last = pe.transpose(xT_ps[:, u, i, :], xn[:, u, i, :], m["mat"]["ident"])
                    last.then_inc(xT_done, 1)

                pe.wait_ge(m["weights_in"], m["weights_count"])
                turn(0, 0)

                def step(g, u, last=None):
                    if not (isinstance(g, int) and g == last):
                        turn(g + 1, 1 - u)
                    pe.wait_ge(ret_ready, g + 1)
                    wait(pe, in_ready, g)
                    pe.matmul(in_ps[:], m["mat"]["r_wi"], ret[:, u], start=True, stop=True).then_inc(in_done, 1)
                    pe.wait_ge(in_ready, g + 1)
                    wait(pe, gate_ready, g)
                    pe.matmul(g_ps[:], m["mat"]["r_wg"], cols(inp, g), start=True, stop=True).then_inc(g_done, 1)

                over_batches(pe, step, NG)

            @block.scalar
            def _(act):
                act.preload_act_table(ACT.Sigmoid)

                def step(g, u, last=None):
                    act.wait_ge(in_done, g + 1)
                    act.activation(cols(inp, g), in_ps[:], ACT.Identity, bias=m["col"]["r_bi"]).then_inc(in_ready, 1)
                    act.wait_ge(g_done, g + 1)
                    act.activation(cols(gate, g), g_ps[:], ACT.Sigmoid, bias=m["col"]["r_bg"]).then_inc(gate_ready, 1)

                over_batches(act, step, NG)

        with nc.Block() as block:

            @block.tensor
            def _(pe):
                def step(t, u, last=None):
                    wait(pe, s_ready, t - 1)
                    pe.matmul(z_ps[:, u, 0:B], m["mat"]["r_bm"], inp[:, t, :], start=True, stop=False)
                    first = isinstance(t, int) and t == 0
                    z = pe.matmul(z_ps[:, u, 0:B], m["mat"]["r_a"], rest[:, t, :], start=False, stop=first)
                    if not first:
                        pe.wait_ge(ms_ready, t)
                        z = pe.matmul(z_ps[:, u, 0:B], m["mat"]["r_a"], ms[:, u, :], start=False, stop=True)
                    z.then_inc(z_done, 1)

                over_batches(pe, step, T)

            @block.scalar
            def _(act):
                act.preload_act_table(ACT.Tanh)

                def step(t, u, last=None):
                    act.wait_ge(z_done, t + 1)
                    act.activation(state[:, t, :], z_ps[:, u, 0:B], ACT.Tanh).then_inc(s_ready, 1)

                over_batches(act, step, T)

            @block.vector
            def _(dve):
                def step(t, u, last=None):
                    if isinstance(t, int) and t == 0:
                        return
                    dve.wait_ge(s_ready, t)
                    dve.tensor_tensor(ms[:, u, :], gate[:, t, :], state[:, t - 1, :], ALU.mult).then_inc(ms_ready, 1)

                over_batches(dve, step, T)

        with nc.Block() as block:

            @block.gpsimd
            def _(pool):
                def step(b, u, last=None):
                    wait(pool, x_done, b - 1)
                    nc.gpsimd.tensor_tensor(xb[:, u, :], m["x"][:, b, :], m["row"]["r_bo"], ALU.add).then_inc(xb_ready, 1)

                over_batches(pool, step)

            @block.scalar
            def _(act):
                def step(b, u, last=None):
                    wait(act, y_done, b - 1)
                    act.activation(sT[:, u, :], state[:, :, b], ACT.Copy).then_inc(sT_ready, 1)

                over_batches(act, step)

            @block.tensor
            def _(pe):
                def step(b, u, last=None):
                    pe.wait_ge(sT_ready, b + 1)
                    wait(pe, x_done, b - 1)
                    pe.matmul(y_ps[:, u, 0:D], sT[:, u, :], m["mat"]["r_wo"], start=True, stop=True).then_inc(y_done, 1)

                over_batches(pe, step)

            @block.vector
            def _(dve):
                def step(b, u, last=None):
                    dve.wait_ge(y_done, b + 1)
                    dve.wait_ge(xb_ready, b + 1)
                    dve.tensor_tensor(m["x"][:, b, :], y_ps[:, u, 0:D], xb[:, u, :], ALU.add).then_inc(x_done, 1)
                    dve.wait_ge(x_done, b + 1)
                    dve.bn_stats(m["stats"][:, b, :], m["x"][:, b, :])

                over_batches(dve, step)

        sem.clear()


def softmax_experts(nc, dve, act_ready, exp_ready, c, lg, tmp, rows):
    n = lg.shape[1]
    wide = [rows, n, E]
    c(dve.tensor_reduce(tmp, lg, AX.X, ALU.max))
    c(dve.tensor_tensor(lg, lg, tmp.unsqueeze(2).broadcast_to(wide), ALU.subtract))
    dve.sem_inc(act_ready, 1)
    dve.wait_ge(exp_ready, 1)
    c(dve.tensor_reduce(tmp, lg, AX.X, ALU.add))
    c(dve.reciprocal(tmp, tmp))
    c(dve.tensor_tensor(lg, lg, tmp.unsqueeze(2).broadcast_to(wide), ALU.mult))


def top_two_mixture(nc, m):
    G = 4
    NG = B // G
    F = 2
    with ExitStack() as ctx:
        def sb(n, shape, dt=F32):
            return ctx.enter_context(nc.sbuf_tensor(f"m_{n}", shape, dt))

        def ps(n, shape):
            return ctx.enter_context(nc.psum_tensor(f"m_{n}", shape, F32))

        sem = Semaphores(nc, ctx, "m")

        lg = m["logits"]
        wgt = sb("wgt", [P, B, E])
        pick = sb("pick", [P, B, E])
        left = sb("left", [P, B, E])
        t1, t2, t3 = sb("t1", [P, B]), sb("t2", [P, B]), sb("t3", [P, B])
        wT = sb("wT", [P, 2, P])
        h = sb("h", [P, 2, F, G * P])
        turn_ps = ps("turn_ps", [P, 512])
        h_ps, z_ps = ps("h_ps", [P, 2, G * P]), ps("z_ps", [P, 2, G, D])
        b_ps = ps("b_ps", [P, 2, 512])
        steps, act_ready, exp_ready, w_ready, wT_done, wT_ready = (sem("steps"), sem("act_ready"), sem("exp_ready"),
                                                                   sem("w_ready"), sem("wT_done"), sem("wT_ready"))
        b_done, b_added, h_done, h_ready, z_done, z_added, x_done = (
            sem("b_done"), sem("b_added"), sem("h_done"), sem("h_ready"), sem("z_done"), sem("z_added"), sem("x_done"))

        with nc.Block() as block:

            @block.scalar
            def _(act):
                act.wait_ge(act_ready, 1)
                act.activation(lg[:], lg[:], ACT.Exp).then_inc(exp_ready, 1)

            @block.vector
            def _(dve):
                c = Chain(dve, steps)
                softmax_experts(nc, dve, act_ready, exp_ready, c, lg[:], t1[:], P)
                wide = [P, B, E]

                def choose(src, top):
                    c(dve.tensor_reduce(top[:], src[:], AX.X, ALU.max))
                    c(dve.tensor_tensor(pick[:], src[:], top[:].unsqueeze(2).broadcast_to(wide), ALU.is_equal))
                    c(dve.tensor_tensor(pick[:], pick[:], m["down"][:].unsqueeze(1).broadcast_to(wide), ALU.mult))
                    c(dve.tensor_reduce(t3[:], pick[:], AX.X, ALU.max))
                    c(dve.tensor_tensor(pick[:], pick[:], t3[:].unsqueeze(2).broadcast_to(wide), ALU.is_equal))

                choose(lg, t1)
                c(dve.tensor_tensor(wgt[:], pick[:], t1[:].unsqueeze(2).broadcast_to(wide), ALU.mult))
                c(dve.scalar_tensor_tensor(left[:].rearrange("p b e -> p (b e)"), pick[:].rearrange("p b e -> p (b e)"), -4.0,
                                           lg[:].rearrange("p b e -> p (b e)"), ALU.mult, ALU.add))
                choose(left, t2)
                c(dve.tensor_tensor(pick[:], pick[:], t2[:].unsqueeze(2).broadcast_to(wide), ALU.mult))
                c(dve.tensor_tensor(wgt[:], wgt[:], pick[:], ALU.add))
                c(dve.tensor_tensor(t1[:], t1[:], t2[:], ALU.add))
                c(dve.tensor_scalar(t1[:], t1[:], 1e-8, None, ALU.add))
                c(dve.reciprocal(t1[:], t1[:]))
                c(dve.tensor_scalar(t1[:], t1[:], 0.3, None, ALU.mult))
                dve.tensor_tensor(wgt[:], wgt[:], t1[:].unsqueeze(2).broadcast_to(wide), ALU.mult).then_inc(w_ready, 1)
                dve.wait_ge(wT_done, 1)
                dve.tensor_copy(wT[:], turn_ps[:, 0:2 * P].rearrange("p (h t) -> p h t", h=2)).then_inc(wT_ready, 1)

            @block.tensor
            def _(pe):
                pe.wait_ge(w_ready, 1)
                for half in range(2):
                    last = pe.transpose(turn_ps[:, half * P:(half + 1) * P],
                                        wgt[:, 16 * half:16 * half + 16, :].rearrange("p b e -> p (b e)"), m["mat"]["ident"])
                last.then_inc(wT_done, 1)

        with nc.Block() as block:

            @block.tensor
            def _(pe):
                pe.wait_ge(m["m_in"], 48)
                for half in range(2):
                    def bias(b, u, last=None):
                        wait(pe, b_added, b + 16 * half - 1)
                        pe.matmul(b_ps[:, u, 0:D], wT[:, half, :], m["m_b2"][:, b, :], start=True, stop=True)\
                            .then_inc(b_done, 1)

                    over_batches(pe, bias, 16)

                def up(g, e):
                    n = E * g + e
                    for f in range(F):
                        wait(pe, h_ready, F * (n - 1) + f + 1)
                        pe.matmul(h_ps[:, f, :], m["m_w1"][:, e, f * P:(f + 1) * P], m["big"][:, bass.ds(G * g, G), :],
                                  start=True, stop=True).then_inc(h_done, 1)

                def down(g, e):
                    n = E * g + e
                    pe.wait_ge(h_ready, F * (n + 1))
                    wait(pe, z_added, n - 1)
                    for i in range(G):
                        for f in range(F):
                            last = pe.matmul(z_ps[:, e % 2, i, :], h[:, e % 2, f, i * P:(i + 1) * P], m["m_w2"][:, e, f, :],
                                             start=(f == 0), stop=(f == F - 1))
                    last.then_inc(z_done, 1)

                def group(g, u, last=None):
                    up(g, 0)
                    for e in range(1, E):
                        up(g, e)
                        down(g, e - 1)
                    down(g, E - 1)

                over_batches(pe, group, NG)

            @block.scalar
            def _(act):
                act.preload_act_table(ACT.Gelu)

                def group(g, u, last=None):
                    for e in range(E):
                        n = E * g + e
                        for f in range(F):
                            act.wait_ge(h_done, F * n + f + 1)
                            wait(act, z_done, n - 1)
                            act.activation(h[:, e % 2, f, :], h_ps[:, f, :], ACT.Gelu,
                                           bias=m["col"][f"m_b1_{F * e + f}"]).then_inc(h_ready, 1)

                over_batches(act, group, NG)

            @block.vector
            def _(dve):
                for half in range(2):
                    def bias(b, u, last=None):
                        dve.wait_ge(b_done, b + 16 * half + 1)
                        x = m["x"][:, b + 16 * half, :]
                        dve.tensor_tensor(x, x, b_ps[:, u, 0:D], ALU.add).then_inc(b_added, 1)

                    over_batches(dve, bias, 16)
                dve.wait_ge(b_added, B)

                def group(g, u, last=None):
                    for e in range(E):
                        n = E * g + e
                        dve.wait_ge(z_done, n + 1)
                        wait(dve, z_added, n)
                        for i in range(G):
                            x = m["x"][:, G * g + i, :]
                            w = wgt[:, G * g + i, e:e + 1]
                            last_op = dve.scalar_tensor_tensor(x, z_ps[:, e % 2, i, :], w, x, ALU.mult, ALU.add)
                        last_op.then_inc(z_added, 1)
                    dve.wait_ge(z_added, E * (g + 1))
                    for i in range(G):
                        dve.bn_stats(m["stats"][:, G * g + i, :], m["x"][:, G * g + i, :])

                over_batches(dve, group, NG)

        sem.clear()




def expert_choice(nc, m):
    G, NG, K, F = 4, 8, 32, 4
    with ExitStack() as ctx:
        def sb(n, shape, dt=F32):
            return ctx.enter_context(nc.sbuf_tensor(f"e_{n}", shape, dt))

        sem = Semaphores(nc, ctx, "e")

        lg = m["logits"]
        lnv, rstd, nmr = sb("lnv", [P, 6, B]), sb("rstd", [P, B]), sb("nmr", [P, B])
        xn = sb("xn", [P, 2, G, D])
        rank = sb("rank", [P, B, E])
        half_set, ln_ready, pow_ready, steps = sem("half_set"), sem("ln_ready"), sem("pow_ready"), sem("steps")

        with ExitStack() as inner:
            xnT = inner.enter_context(nc.sbuf_tensor("e_xnT", [P, 2, P], F32))
            xT_ps = inner.enter_context(nc.psum_tensor("e_xT_ps", [P, 2, 512], F32))
            lg_ps = inner.enter_context(nc.psum_tensor("e_lg_ps", [P, 2, 512], F32))
            xn_ready, xT_done, xnT_ready, lg_done, lg_ready = (sem("r_xn_ready"), sem("r_xT_done"), sem("r_xnT_ready"),
                                                               sem("r_lg_done"), sem("r_lg_ready"))
            with nc.Block() as block:

                @block.gpsimd
                def _(pool):
                    pool.memset(lnv[:, 5, :], -0.5).then_inc(half_set, 1)
                    pool.wait_ge(half_set, 1)
                    pool.wait_ge(ln_ready, 1)
                    nc.gpsimd.tensor_tensor(rstd[:], lnv[:, 4, :], lnv[:, 5, :], ALU.pow).then_inc(pow_ready, 1)

                @block.vector
                def _(dve):
                    layernorm_stats(nc, dve, m, lnv, rstd, nmr, steps, ln_ready, pow_ready)

                    def normalise(b, u):
                        wait(dve, xT_done, b - 1)
                        dve.tensor_scalar(xn[:, u, 0, :], m["x"][:, b, :], rstd[:, bass.ds(b, 1)], nmr[:, bass.ds(b, 1)],
                                          ALU.mult, ALU.add).then_inc(xn_ready, 1)

                    normalise(0, 0)

                    def step(b, u, last=None):
                        if not (isinstance(b, int) and b == last):
                            normalise(b + 1, 1 - u)
                        dve.wait_ge(lg_done, b + 1)
                        dve.tensor_copy(lg[:, b, :], lg_ps[:, u, 0:E]).then_inc(lg_ready, 1)

                    over_batches(dve, step)

                @block.scalar
                def _(act):
                    def step(b, u, last=None):
                        act.wait_ge(xT_done, b + 1)
                        wait(act, lg_done, b - 1)
                        act.activation(xnT[:, u, :], xT_ps[:, u, 0:P], ACT.Copy).then_inc(xnT_ready, 1)

                    over_batches(act, step)

                @block.tensor
                def _(pe):
                    def turn(b, u):
                        pe.wait_ge(xn_ready, b + 1)
                        wait(pe, xnT_ready, b - 1)
                        pe.transpose(xT_ps[:, u, 0:P], xn[:, u, 0, :], m["mat"]["ident"]).then_inc(xT_done, 1)

                    turn(0, 0)

                    def step(b, u, last=None):
                        if not (isinstance(b, int) and b == last):
                            turn(b + 1, 1 - u)
                        pe.wait_ge(xnT_ready, b + 1)
                        wait(pe, lg_ready, b - 1)
                        pe.matmul(lg_ps[:, u, 0:E], xnT[:, u, :], m["gate_w"][:], start=True, stop=True).then_inc(lg_done, 1)

                    over_batches(pe, step)

        with ExitStack() as inner:
            def ib(n, shape):
                return inner.enter_context(nc.sbuf_tensor(f"e_{n}", shape, F32))

            t1 = ib("t1", [P, B])
            pT, left, took = ib("pT", [P, 2, P]), ib("left", [P, 2, P]), ib("took", [P, 2, P])
            top = ib("top", [P, 2, 8])
            tk = ib("tk", [P, 2, P])
            pT_ps = inner.enter_context(nc.psum_tensor("e_pT_ps", [P, 512], F32))
            tk_ps = inner.enter_context(nc.psum_tensor("e_tk_ps", [P, 512], F32))
            rk_ps = inner.enter_context(nc.psum_tensor("e_rk_ps", [P, 512], F32))
            c_steps, act_ready, exp_ready, p_ready = sem("c_steps"), sem("act_ready"), sem("exp_ready"), sem("p_ready")
            pT_done, took_ready, tk_done, tk_ready, rk_done = (sem("pT_done"), sem("took_ready"), sem("tk_done"),
                                                               sem("tk_ready"), sem("rk_done"))
            with nc.Block() as block:

                @block.scalar
                def _(act):
                    act.wait_ge(act_ready, 1)
                    act.activation(lg[:], lg[:], ACT.Exp).then_inc(exp_ready, 1)

                @block.vector
                def _(dve):
                    c = Chain(dve, c_steps)
                    softmax_experts(nc, dve, act_ready, exp_ready, c, lg[:], t1[:], P)
                    dve.sem_inc(p_ready, 1)
                    dve.wait_ge(pT_done, 1)
                    c(dve.tensor_copy(pT[:], pT_ps[:, 0:2 * P].rearrange("p (h t) -> p h t", h=2)))
                    src = pT
                    for _ in range(K // 8):
                        for half in range(2):
                            c(dve.max(top[:, half, :], src[:, half, :]))
                            c(dve.match_replace(left[:, half, :], top[:, half, :], src[:, half, :], -1.0))
                        src = left
                    dve.tensor_scalar(took[:], left[:], 0.0, None, ALU.is_lt).then_inc(took_ready, 1)
                    dve.wait_ge(tk_done, 1)
                    dve.tensor_copy(tk[:], tk_ps[:, 0:2 * P].rearrange("p (h t) -> p h t", h=2)).then_inc(tk_ready, 1)
                    dve.wait_ge(rk_done, 1)
                    dve.tensor_tensor(rank[:].rearrange("p b e -> p (b e)"), rk_ps[:, 0:2 * P],
                                      tk[:].rearrange("p h t -> p (h t)"), ALU.mult)

                @block.tensor
                def _(pe):
                    pe.wait_ge(p_ready, 1)
                    for half in range(2):
                        last = pe.transpose(pT_ps[:, half * P:(half + 1) * P],
                                            lg[:, 16 * half:16 * half + 16, :].rearrange("p b e -> p (b e)"), m["mat"]["ident"])
                    last.then_inc(pT_done, 1)
                    pe.wait_ge(took_ready, 1)
                    for half in range(2):
                        last = pe.transpose(tk_ps[:, half * P:(half + 1) * P], took[:, half, :], m["mat"]["ident"])
                    last.then_inc(tk_done, 1)
                    pe.wait_ge(tk_ready, 1)
                    pe.matmul(rk_ps[:, 0:2 * P], m["mat"]["tri"], tk[:].rearrange("p h t -> p (h t)"), start=True, stop=True)\
                        .then_inc(rk_done, 1)

        oh = sb("oh", [P, 2, G, E, K])
        ohw = sb("ohw", [P, 2, E, G, K])
        xe = sb("xe", [P, 2, E, G, K])
        owT = sb("owT", [P, 2, E, P])
        h = sb("h", [P, 2, F, P])
        z = sb("z", [P, E, D])
        yb = sb("yb", [P, 2, D], BF16)
        g_ps = ctx.enter_context(nc.psum_tensor("e_g_ps", [P, 512], F32))
        h_ps = ctx.enter_context(nc.psum_tensor("e_h_ps", [P, 2, F, P], F32))
        z_ps = ctx.enter_context(nc.psum_tensor("e_z_ps", [P, 512], F32))
        y_ps = ctx.enter_context(nc.psum_tensor("e_y_ps", [P, G, 512], F32))
        xn_ready, oh_ready, ohw_ready = sem("xn_ready"), sem("oh_ready"), sem("ohw_ready")
        gx_done, gx_ready, gw_done, gw_ready = sem("gx_done"), sem("gx_ready"), sem("gw_done"), sem("gw_ready")
        h_done, h_ready, z_done, z_ready, y_done, y_read, x_done = (
            sem("h_done"), sem("h_ready"), sem("z_done"), sem("z_ready"), sem("y_done"), sem("y_read"), sem("x_done"))

        with nc.Block() as block:

            @block.gpsimd
            def _(pool):
                def step(g, u, last=None):
                    wait(pool, gw_done, 2 * (g - 1))
                    for i in range(G):
                        pool.wait_ge(oh_ready, G * g + i + 1)
                        nc.gpsimd.tensor_tensor(ohw[:, u, :, i, :], oh[:, u, i],
                                                lg[:, G * g + i, :].unsqueeze(2).broadcast_to([P, E, K]), ALU.mult)\
                            .then_inc(ohw_ready, 1)

                over_batches(pool, step, NG)

            @block.vector
            def _(dve):
                def ready(g, u):
                    wait(dve, gx_done, 2 * (g - 1))
                    wait(dve, ohw_ready, G * (g - 1))
                    for i in range(G):
                        dve.tensor_scalar(xn[:, u, i, :], m["x"][:, G * g + i, :], rstd[:, bass.ds(G * g + i, 1)],
                                          nmr[:, bass.ds(G * g + i, 1)], ALU.mult, ALU.add).then_inc(xn_ready, 1)
                        dve.tensor_tensor(oh[:, u, i], m["iota"][:].unsqueeze(1).broadcast_to([P, E, K]),
                                          rank[:, G * g + i, :].unsqueeze(2).broadcast_to([P, E, K]), ALU.is_equal)\
                            .then_inc(oh_ready, 1)

                def keep_weights(g, u):
                    for half in range(2):
                        dve.wait_ge(gw_done, 2 * g + half + 1)
                        dve.tensor_copy(owT[:, u, 4 * half:4 * half + 4, :], g_ps[:].rearrange("p (e t) -> p e t", e=4))\
                            .then_inc(gw_ready, 1)

                def keep_z(g, e):
                    dve.wait_ge(z_done, E * g + e + 1)
                    if e == 0:
                        wait(dve, y_done, g)
                    dve.tensor_copy(z[:, e, :], z_ps[:, 0:D]).then_inc(z_ready, 1)

                ready(0, 0)
                keep_weights(0, 0)

                def step(g, u, last=None):
                    more = not (isinstance(g, int) and g == last)
                    if more:
                        ready(g + 1, 1 - u)
                    for e in range(E):
                        keep_z(g, e)
                        if e == 5 and more:
                            keep_weights(g + 1, 1 - u)
                    dve.wait_ge(y_done, g + 1)
                    for i in range(G):
                        if i >= 2:
                            dve.wait_ge(x_done, G * g + i - 1)
                        else:
                            wait(dve, x_done, G * g + i - 1)
                        dve.tensor_copy(yb[:, i % 2, :], y_ps[:, i, 0:D]).then_inc(y_read, 1)
                        dve.wait_ge(y_read, G * g + i + 1)
                        x = m["x"][:, G * g + i, :]
                        dve.tensor_tensor(x, x, yb[:, i % 2, :], ALU.add).then_inc(x_done, 1)
                    dve.wait_ge(x_done, G * (g + 1))
                    for i in range(G):
                        dve.bn_stats(m["stats"][:, G * g + i, :], m["x"][:, G * g + i, :])

                over_batches(dve, step, NG)

            @block.scalar
            def _(act):
                act.preload_act_table(ACT.Gelu_apprx_tanh)

                def keep_tokens(g, u):
                    for half in range(2):
                        act.wait_ge(gx_done, 2 * g + half + 1)
                        if half == 0:
                            wait(act, h_done, E * (g - 1))
                        act.activation(xe[:, u, :, 2 * half:2 * half + 2, :],
                                       g_ps[:].rearrange("p (i e k) -> p e i k", i=2, e=E), ACT.Copy).then_inc(gx_ready, 1)

                keep_tokens(0, 0)

                def step(g, u, last=None):
                    more = not (isinstance(g, int) and g == last)
                    for e in range(E):
                        n = E * g + e
                        act.wait_ge(h_done, n + 1)
                        wait(act, z_done, n - 1)
                        act.activation(h[:, e % 2], h_ps[:, e % 2], ACT.Gelu_apprx_tanh).then_inc(h_ready, 1)
                        if e == 3 and more:
                            keep_tokens(g + 1, 1 - u)

                over_batches(act, step, NG)

            @block.tensor
            def _(pe):
                pe.wait_ge(m["weights_in"], m["weights_count"])

                def gather(g, u):
                    for half in range(2):
                        if half == 0:
                            wait(pe, gw_ready, 2 * g)
                        else:
                            pe.wait_ge(gx_ready, 2 * g + 1)
                        for j in range(2):
                            i = 2 * half + j
                            pe.wait_ge(xn_ready, G * g + i + 1)
                            pe.wait_ge(oh_ready, G * g + i + 1)
                            last = pe.matmul(g_ps[:, j * 256:(j + 1) * 256], xn[:, u, i, :],
                                             oh[:, u, i].rearrange("p e k -> p (e k)"), start=True, stop=True)
                        last.then_inc(gx_done, 1)

                def turn_weights(g, u):
                    pe.wait_ge(ohw_ready, G * (g + 1))
                    for half in range(2):
                        if half == 0:
                            pe.wait_ge(gx_ready, 2 * g + 2)
                        else:
                            pe.wait_ge(gw_ready, 2 * g + 1)
                        for j in range(4):
                            last = pe.transpose(g_ps[:, j * P:(j + 1) * P],
                                                ohw[:, u, 4 * half + j].rearrange("p i k -> p (i k)"), m["mat"]["ident"])
                        last.then_inc(gw_done, 1)

                def up(g, u, e):
                    n = E * g + e
                    if e == 0:
                        pe.wait_ge(gx_ready, 2 * (g + 1))
                    wait(pe, h_ready, n - 1)
                    for f in range(F):
                        last = pe.matmul(h_ps[:, e % 2, f, :], m["e_w1"][:, e, f * P:(f + 1) * P],
                                         xe[:, u, e].rearrange("p i k -> p (i k)"), start=True, stop=True)
                    last.then_inc(h_done, 1)

                def down(g, e):
                    n = E * g + e
                    pe.wait_ge(h_ready, n + 1)
                    wait(pe, z_ready, n)
                    for f in range(F):
                        last = pe.matmul(z_ps[:, 0:D], h[:, e % 2, f, :], m["e_w2"][:, e, f, :],
                                         start=(f == 0), stop=(f == F - 1))
                    last.then_inc(z_done, 1)

                def scatter(g, u):
                    pe.wait_ge(z_ready, E * (g + 1))
                    pe.wait_ge(gw_ready, 2 * (g + 1))
                    wait(pe, y_read, G * g)
                    for e in range(E):
                        for i in range(G):
                            r = slice(K * i, K * i + K)
                            last = pe.matmul(y_ps[:, i, 0:D], owT[r, u, e, :], z[r, e, :], start=(e == 0), stop=(e == E - 1))
                    last.then_inc(y_done, 1)

                gather(0, 0)
                turn_weights(0, 0)

                def step(g, u, last=None):
                    more = not (isinstance(g, int) and g == last)
                    up(g, u, 0)
                    for e in range(1, E):
                        up(g, u, e)
                        down(g, e - 1)
                        if e == 4 and more:
                            gather(g + 1, 1 - u)
                        if e == 6 and more:
                            turn_weights(g + 1, 1 - u)
                    down(g, E - 1)
                    scatter(g, u)

                over_batches(pe, step, NG)

        sem.clear()


def hashed_mixture(nc, m):
    G, NG = 4, 8
    with ExitStack() as ctx:
        def sb(n, shape, dt=F32):
            return ctx.enter_context(nc.sbuf_tensor(f"s_{n}", shape, dt))

        def ps(n, shape):
            return ctx.enter_context(nc.psum_tensor(f"s_{n}", shape, F32))

        sem = Semaphores(nc, ctx, "s")

        lnv, rstd, nmr = sb("lnv", [P, 6, B]), sb("rstd", [P, B]), sb("nmr", [P, B])
        xn = sb("xn", [P, 2, G, D])
        xT = sb("xT", [P, 2, 8, 64])
        av = sb("av", [P, 512])
        sg = sb("sg", [P, 512])
        gt = sb("gt", [P, 512])
        hs = sb("hs", [P, 2, 512])
        hr = sb("hr", [P, 2, 8, 64])
        yT = sb("yT", [P, 64, 8])
        x_ps, a_ps, y_ps, t_ps = ps("x_ps", [P, G, P]), ps("a_ps", [P, 4, 512]), ps("y_ps", [P, 512]), ps("t_ps", [P, G, P])
        half_set, ln_ready, pow_ready, steps = sem("half_set"), sem("ln_ready"), sem("pow_ready"), sem("steps")
        av_ready = sem("av_ready")
        xn_ready, x_turned, xT_ready = sem("xn_ready"), sem("x_turned"), sem("xT_ready")
        gate_done, up_done, sg_ready, gt_ready, hs_ready = (sem("gate_done"), sem("up_done"), sem("sg_ready"),
                                                            sem("gt_ready"), sem("hs_ready"))
        r_done, hr_ready = sem("r_done"), sem("hr_ready")
        y_done, yT_ready, y_turned, x_done = sem("y_done"), sem("yT_ready"), sem("y_turned"), sem("x_done")

        with nc.Block() as block:

            @block.gpsimd
            def _(pool):
                pool.memset(lnv[:, 5, :], -0.5).then_inc(half_set, 1)
                pool.wait_ge(half_set, 1)
                pool.wait_ge(ln_ready, 1)
                nc.gpsimd.tensor_tensor(rstd[:], lnv[:, 4, :], lnv[:, 5, :], ALU.pow).then_inc(pow_ready, 1)

            @block.vector
            def _(dve):
                layernorm_stats(nc, dve, m, lnv, rstd, nmr, steps, ln_ready, pow_ready)

                def normalise(g, u):
                    wait(dve, x_turned, g - 1)
                    for i in range(G):
                        last = dve.tensor_scalar(xn[:, u, i, :], m["x"][:, G * g + i, :], rstd[:, bass.ds(G * g + i, 1)],
                                                 nmr[:, bass.ds(G * g + i, 1)], ALU.mult, ALU.add)
                    last.then_inc(xn_ready, 1)

                normalise(0, 0)

                def step(g, u, last=None):
                    if not (isinstance(g, int) and g == last):
                        normalise(g + 1, 1 - u)
                    for k in range(2):
                        dve.wait_ge(sg_ready, 2 * g + k + 1)
                        wait(dve, hs_ready, 2 * g + k)
                        dve.scalar_tensor_tensor(gt[:], sg[:], 1.0, av[:], ALU.add, ALU.mult)\
                            .then_inc(gt_ready, 1)
                        dve.wait_ge(gt_ready, 2 * g + k + 1)
                        dve.wait_ge(up_done, 2 * g + k + 1)
                        wait(dve, y_done, g)
                        dve.scalar_tensor_tensor(hs[:, k, :], a_ps[:, 1, :], m["col"][f"sb3_{k}"], gt[:], ALU.add, ALU.mult)\
                            .then_inc(hs_ready, 1)
                    for i in range(G):
                        if i == 0:
                            dve.wait_ge(y_turned, g + 1)
                        x = m["x"][:, G * g + i, :]
                        last_op = dve.scalar_tensor_tensor(x, t_ps[:, i, :], 0.25, x, ALU.mult, ALU.add)
                    last_op.then_inc(x_done, 1)
                    dve.wait_ge(x_done, g + 1)
                    for i in range(G):
                        dve.bn_stats(m["stats"][:, G * g + i, :], m["x"][:, G * g + i, :])

                over_batches(dve, step, NG)

            @block.scalar
            def _(act):
                act.preload_act_table(ACT.Gelu)

                def x_keep(g, u):
                    act.wait_ge(x_turned, g + 1)
                    wait(act, r_done, 2 * (g - 1))
                    act.activation(xT[:, u].rearrange("p r q -> p q r"), x_ps[:].rearrange("p i t -> p (i t)")
                                   .rearrange("p (q r) -> p q r", r=8), ACT.Copy).then_inc(xT_ready, 1)

                x_keep(0, 0)

                def step(g, u, last=None):
                    for k in range(2):
                        act.wait_ge(gate_done, 2 * g + k + 1)
                        wait(act, gt_ready, 2 * g + k)
                        act.activation(av[:], a_ps[:, 0, :], ACT.Identity, bias=m["col"][f"sb1_{k}"]).then_inc(av_ready, 1)
                        act.wait_ge(av_ready, 2 * g + k + 1)
                        act.activation(sg[:], av[:], ACT.Tanh, scale=0.5).then_inc(sg_ready, 1)
                    for k in range(2):
                        act.wait_ge(r_done, 2 * g + k + 1)
                        wait(act, y_done, g)
                        act.activation(hr[:, k].rearrange("p r q -> p (r q)"), a_ps[:, 2 + k, :], ACT.Gelu)\
                            .then_inc(hr_ready, 1)
                    if not (isinstance(g, int) and g == last):
                        x_keep(g + 1, 1 - u)
                    act.wait_ge(y_done, g + 1)
                    wait(act, y_turned, g)
                    act.activation(yT[:].rearrange("p q r -> p r q"), y_ps[:].rearrange("p (r q) -> p r q", r=8), ACT.Copy)\
                        .then_inc(yT_ready, 1)

                over_batches(act, step, NG)

            @block.tensor
            def _(pe):
                pe.wait_ge(m["weights_in"], m["weights_count"])

                def turn(g, u):
                    pe.wait_ge(xn_ready, g + 1)
                    wait(pe, xT_ready, g)
                    for i in range(G):
                        last = pe.transpose(x_ps[:, i, :], xn[:, u, i, :], m["mat"]["ident"])
                    last.then_inc(x_turned, 1)

                turn(0, 0)

                def step(g, u, last=None):
                    xin = xT[:, u].rearrange("p r q -> p (r q)")
                    pe.wait_ge(xT_ready, g + 1)
                    for k in range(2):
                        wait(pe, av_ready, 2 * g + k)
                        pe.matmul(a_ps[:, 0, :], m["s_w1"][:, k, :], xin, start=True, stop=True).then_inc(gate_done, 1)
                        wait(pe, hs_ready, 2 * g + k)
                        pe.matmul(a_ps[:, 1, :], m["s_w3"][:, k, :], xin, start=True, stop=True).then_inc(up_done, 1)
                    for k in range(2):
                        wait(pe, hr_ready, 2 * (g - 1) + k + 1)
                        pe.matmul(a_ps[:, 2 + k, :], m["s_b1"][:], m["s_hot"][0:E, k, :], start=True, stop=False,
                                  skip_group_check=True)
                        for r in range(8):
                            last_op = pe.matmul(a_ps[:, 2 + k, 64 * r:64 * r + 64], m["s_up"][:, HASHED[k][r], :], xT[:, u, r, :],
                                                start=False, stop=(r == 7), skip_group_check=True)
                        last_op.then_inc(r_done, 1)
                    if not (isinstance(g, int) and g == last):
                        turn(g + 1, 1 - u)
                    wait(pe, yT_ready, g)
                    pe.matmul(y_ps[:], m["s_b2"][:], m["s_hot"][:, 2, :], start=True, stop=False, skip_group_check=True)
                    for k in range(2):
                        pe.wait_ge(hs_ready, 2 * g + k + 1)
                        pe.matmul(y_ps[:], m["s_w2"][:, k, :], hs[:, k, :], start=False, stop=False, skip_group_check=True)
                    for k in range(2):
                        pe.wait_ge(hr_ready, 2 * g + k + 1)
                        for r in range(8):
                            last_op = pe.matmul(y_ps[:, 64 * r:64 * r + 64], m["s_down"][:, HASHED[k][r], :], hr[:, k, r, :],
                                                start=False, stop=(k == 1 and r == 7), skip_group_check=True)
                    last_op.then_inc(y_done, 1)
                    pe.wait_ge(yT_ready, g + 1)
                    wait(pe, x_done, g)
                    y = yT[:].rearrange("p q r -> p (q r)")
                    for i in range(G):
                        last_op = pe.transpose(t_ps[:, i, :], y[:, i * P:(i + 1) * P], m["mat"]["ident"])
                    last_op.then_inc(y_turned, 1)

                over_batches(pe, step, NG)

        sem.clear()


def zones(nc, m, a, out):
    TOP, F = 3, 4
    with ExitStack() as ctx:
        def sb(n, shape, dt=F32):
            return ctx.enter_context(nc.sbuf_tensor(f"z_{n}", shape, dt))

        def ps(n, shape):
            return ctx.enter_context(nc.psum_tensor(f"zp_{n}", shape, F32))

        sem = Semaphores(nc, ctx, "z")

        lnv, rstd, nmr = sb("lnv", [P, 6, B]), sb("rstd", [P, B]), sb("nmr", [P, B])
        xn = sb("xn", [P, 2, D])
        xT = sb("xT", [P, 2, P])
        meanT = sb("meanT", [P, B])
        hid, hidT = sb("hid", [B, 32]), sb("hidT", [32, B])
        lg, t1 = sb("lg", [B, 1, E]), sb("t1", [B, 1])
        top, idx, wt = sb("top", [B, 8]), sb("idx", [B, 8], U32), sb("wt", [B, 3])
        idx_row, w_row = sb("idx_row", [1, B * TOP], U32), sb("w_row", [1, B * TOP])
        w_all = sb("w_all", [P, B * TOP])
        h, hT = sb("h", [P, 2, 512]), sb("hT", [P, 2, F, P])
        o = sb("o", [P, 2, D])
        x_ps, p_ps, h_ps, t_ps, z_ps = (ps("x_ps", [P, 2, 512]), ps("p_ps", [P, 512]), ps("h_ps", [P, 2, 512]),
                                        ps("t_ps", [P, F, P]), ps("z_ps", [P, 2, 512]))
        half_set, ln_ready, pow_ready, steps = sem("half_set"), sem("ln_ready"), sem("pow_ready"), sem("steps")
        xn_ready, x_turned, xT_ready, x_sum = sem("xn_ready"), sem("x_turned"), sem("xT_ready"), sem("x_sum")
        mean_done = sem("mean_done")

        with nc.Block() as block:

            @block.gpsimd
            def _(pool):
                pool.memset(lnv[:, 5, :], -0.5).then_inc(half_set, 1)
                pool.wait_ge(half_set, 1)
                pool.wait_ge(ln_ready, 1)
                nc.gpsimd.tensor_tensor(rstd[:], lnv[:, 4, :], lnv[:, 5, :], ALU.pow).then_inc(pow_ready, 1)

                def step(b, u, last=None):
                    pool.wait_ge(xn_ready, b + 1)
                    nc.gpsimd.tensor_tensor(m["x"][:, b, :], m["x"][:, b, :], xn[:, u, :], ALU.add).then_inc(x_sum, 1)

                over_batches(pool, step)

            @block.vector
            def _(dve):
                layernorm_stats(nc, dve, m, lnv, rstd, nmr, steps, ln_ready, pow_ready)

                def step(b, u, last=None):
                    wait(dve, x_turned, b - 1)
                    wait(dve, x_sum, b - 1)
                    dve.tensor_scalar(xn[:, u, :], m["x"][:, b, :], rstd[:, bass.ds(b, 1)], nmr[:, bass.ds(b, 1)],
                                      ALU.mult, ALU.add).then_inc(xn_ready, 1)

                over_batches(dve, step)
                dve.wait_ge(x_turned, B)
                dve.tensor_copy(meanT[:], p_ps[:, 0:B])

            @block.scalar
            def _(act):
                def step(b, u, last=None):
                    act.wait_ge(x_turned, b + 1)
                    act.activation(m["big"][:, b, :], x_ps[:, u, 0:P], ACT.Copy).then_inc(xT_ready, 1)

                over_batches(act, step)

            @block.tensor
            def _(pe):
                def step(b, u, last=None):
                    pe.wait_ge(xn_ready, b + 1)
                    wait(pe, xT_ready, b - 1)
                    pe.matmul(p_ps[:, bass.ds(b, 1)], xn[:, u, :], m["mean"][:], start=True, stop=True)
                    pe.transpose(x_ps[:, u, 0:P], xn[:, u, :], m["mat"]["ident"]).then_inc(x_turned, 1)

                over_batches(pe, step)

        c_steps, h1_done, h1_ready, hT_done, hT_ready, l_done = (sem("c_steps"), sem("h1_done"), sem("h1_ready"),
                                                                 sem("hT_done"), sem("hT_ready"), sem("l_done"))
        tanh_ready, act_ready, exp_ready, pick_ready, row_in, w_done = (sem("tanh_ready"), sem("act_ready"), sem("exp_ready"),
                                                                        sem("pick_ready"), sem("row_in"), sem("w_done"))
        with nc.Block() as block:

            @block.tensor
            def _(pe):
                pe.matmul(p_ps[0:B, 64:96], meanT[:], m["z_w1"][:], start=True, stop=True).then_inc(h1_done, 1)
                pe.wait_ge(tanh_ready, 1)
                pe.matmul(p_ps[0:B, 128:160], hid[:], m["mat"]["ident"][0:B, 0:B], start=True, stop=True).then_inc(hT_done, 1)
                pe.wait_ge(hT_ready, 1)
                pe.matmul(p_ps[0:B, 192:192 + E], hidT[:], m["z_w2"][:], start=True, stop=True).then_inc(l_done, 1)
                pe.wait_ge(row_in, 32)
                pe.matmul(x_ps[:, 0, 0:B * TOP], m["ones"][:], w_row[:], start=True, stop=True).then_inc(w_done, 1)

            @block.scalar
            def _(act):
                act.wait_ge(h1_ready, 1)
                act.activation(hid[:], hid[:], ACT.Tanh).then_inc(tanh_ready, 1)
                act.wait_ge(act_ready, 1)
                act.activation(lg[:], lg[:], ACT.Exp).then_inc(exp_ready, 1)

            @block.vector
            def _(dve):
                c = Chain(dve, c_steps)
                dve.wait_ge(h1_done, 1)
                dve.tensor_tensor(hid[:], p_ps[0:B, 64:96], m["row"]["z_b1"][0:B, 0:32], ALU.add).then_inc(h1_ready, 1)
                dve.wait_ge(hT_done, 1)
                dve.tensor_copy(hidT[:], p_ps[0:B, 128:160]).then_inc(hT_ready, 1)
                dve.wait_ge(l_done, 1)
                c(dve.tensor_tensor(lg[:, 0, :], p_ps[0:B, 192:192 + E], m["row"]["z_b2"][0:B, 0:E], ALU.add))
                softmax_experts(nc, dve, act_ready, exp_ready, c, lg[:], t1[:], B)
                c(dve.max(top[:], lg[:, 0, :]))
                c(dve.max_index(idx[:], top[:], lg[:, 0, :]))
                c(dve.tensor_reduce(t1[:], top[:, 0:TOP], AX.X, ALU.add))
                c(dve.reciprocal(t1[:], t1[:]))
                dve.tensor_scalar(wt[:], top[:, 0:TOP], t1[:, 0:1], None, ALU.mult).then_inc(pick_ready, 1)
                dve.wait_ge(w_done, 1)
                dve.tensor_copy(w_all[:], x_ps[:, 0, 0:B * TOP])

            @block.sync
            def _(sp):
                sp.wait_ge(pick_ready, 1)
                sp.dma_start(idx_row[0:1, :].rearrange("p (b k) -> p b k", k=TOP), idx[:, 0:TOP]).then_inc(row_in, 16)
                sp.dma_start(w_row[0:1, :].rearrange("p (b k) -> p b k", k=TOP), wt[:]).then_inc(row_in, 16)
                sp.wait_ge(row_in, 32)

        xs_ready, h_done, h_ready, t_done, t_ready, z_done, o_ready = (
            sem("xs_ready"), sem("h_done"), sem("h_ready"), sem("t_done"), sem("t_ready"), sem("z_done"), sem("o_ready"))
        stored = [sem("stored0"), sem("stored1")]
        with nc.Block() as block:

            @block.gpsimd
            def _(pool):
                def step(b, u, last=None):
                    wait(pool, h_done, TOP * (b - 1))
                    nc.gpsimd.tensor_copy(xT[:, u, :], m["big"][:, b, :]).then_inc(xs_ready, 1)

                over_batches(pool, step)

            @block.tensor
            def _(pe):
                pe.wait_ge(m["z_in"], 32)

                def up(b, u, k, q):
                    n = TOP * b + k
                    if k == 0:
                        pe.wait_ge(xs_ready, b + 1)
                    wait(pe, h_ready, n - 1)
                    zone = pe.value_load(idx_row[0:1, bass.ds(n, 1)], min_val=0, max_val=E - 1)
                    pe.matmul(h_ps[:, q % 2, :], xT[:, u, :], m["z_wa"][:, bass.ds(zone * 512, 512)], start=True, stop=True)\
                        .then_inc(h_done, 1)
                    return zone

                def turn(b, k, q):
                    n = TOP * b + k
                    pe.wait_ge(h_ready, n + 1)
                    wait(pe, t_ready, n)
                    for f in range(F):
                        last = pe.transpose(t_ps[:, f, :], h[:, q % 2, f * P:(f + 1) * P], m["mat"]["ident"])
                    last.then_inc(t_done, 1)

                def down(b, u, k, q, zone):
                    n = TOP * b + k
                    pe.wait_ge(t_ready, n + 1)
                    if k == 0:
                        wait(pe, o_ready, b - 1)
                    for f in range(F):
                        last = pe.matmul(z_ps[:, u, 0:D], hT[:, q % 2, f, :], m["z_wb"][:, bass.ds(zone, 1), f * P:(f + 1) * P],
                                         start=(k == 0 and f == 0), stop=(k == TOP - 1 and f == F - 1))
                    if k == TOP - 1:
                        last.then_inc(z_done, 1)

                def step(b, u, last=None):
                    at = [TOP * u + k for k in range(TOP)]
                    e0 = up(b, u, 0, at[0])
                    e1 = up(b, u, 1, at[1])
                    turn(b, 0, at[0])
                    down(b, u, 0, at[0], e0)
                    e2 = up(b, u, 2, at[2])
                    turn(b, 1, at[1])
                    down(b, u, 1, at[1], e1)
                    turn(b, 2, at[2])
                    down(b, u, 2, at[2], e2)

                over_batches(pe, step)

            @block.scalar
            def _(act):
                act.preload_act_table(ACT.Gelu_apprx_tanh)

                def step(b, u, last=None):
                    for k in range(TOP):
                        n, q = TOP * b + k, (TOP * u + k) % 2
                        act.wait_ge(h_done, n + 1)
                        wait(act, t_done, n - 1)
                        act.activation(h[:, q, :], h_ps[:, q, :], ACT.Gelu_apprx_tanh).then_inc(h_ready, 1)

                over_batches(act, step)

            @block.vector
            def _(dve):
                def step(b, u, last=None):
                    for k in range(TOP):
                        n, q = TOP * b + k, (TOP * u + k) % 2
                        dve.wait_ge(t_done, n + 1)
                        if k == 2:
                            wait(dve, z_done, b)
                        dve.tensor_scalar(hT[:, q], t_ps[:], w_all[:, bass.ds(n, 1)], None, ALU.mult).then_inc(t_ready, 1)
                    dve.wait_ge(z_done, b + 1)
                    wait(dve, stored[u], 8 * (b - u))
                    dve.tensor_tensor(o[:, u, :], m["x"][:, b, :], z_ps[:, u, 0:D], ALU.add).then_inc(o_ready, 1)

                over_batches(dve, step)

            @block.sync
            def _(sp):
                def step(b, u, last=None):
                    sp.wait_ge(o_ready, b + 1)
                    sp.dma_start(out[:, b, :], o[:, u, :]).then_inc(stored[u], 16)

                over_batches(sp, step)
                for u in range(2):
                    sp.wait_ge(stored[u], 8 * B)

        sem.clear()




def load(nc, m, a):
    with ExitStack() as ctx:
        sem = Semaphores(nc, ctx, "load")

        x_in, c_in, w_in = sem("x_in"), sem("c_in"), sem("w_in")
        steps, lam_ready, lam_exp = sem("steps"), sem("lam_ready"), sem("lam_exp")
        lq = ctx.enter_context(nc.sbuf_tensor("lq", [P, 4, 4], F32))
        lp = ctx.enter_context(nc.sbuf_tensor("lp", [P, 2, 4], F32))
        ls = ctx.enter_context(nc.sbuf_tensor("ls", [P, 2], F32))
        small = [("cols", a["cols"]), ("router_w", a["router_w"]), ("gate_w", a["gate_w"]), ("z_w1", a["z_w1"]),
                 ("z_w2", a["z_w2"]), ("down", a["down"]), ("iota", a["iota"]), ("maskq", a["maskq"]), ("maskk", a["maskk"]),
                 ("s_b1", a["s_b1"]), ("s_b2", a["s_b2"]), ("s_hot", a["s_hot"])]
        with nc.Block() as block:

            @block.sync
            def _(sp):
                for i in range(4):
                    sp.dma_start(m["x"][:, 8 * i:8 * i + 8, :], a["x"][:, 8 * i:8 * i + 8, :]).then_inc(x_in, 16)
                sp.dma_start(m["mats"][:], a["mats"]).then_inc(w_in, 16)
                for name, src in small:
                    sp.dma_start(m[name][:], src).then_inc(w_in, 16)
                for i, (s, (q, k)) in enumerate(m["sel"].items()):
                    sp.dma_start(q[:], a[s + "_q"]).then_inc(w_in, 16)
                    sp.dma_start(k[:], a[s + "_k"]).then_inc(w_in, 16)

            @block.scalar
            def _(act):
                act.dma_start(m["ctxT"][:], a["ctxT"]).then_inc(c_in, 16)
                act.dma_start(m["rows"][:], a["rows"].partition_broadcast(P)).then_inc(w_in, 16)
                act.dma_start(lq[:], a["lams"].partition_broadcast(P)).then_inc(c_in, 16)
                for name in ("e_w1", "e_w2", "s_w1", "s_w2", "s_w3", "s_up", "s_down"):
                    act.dma_start(m[name][:], a[name]).then_inc(m["weights_in"], 16)
                act.wait_ge(lam_ready, 1)
                act.activation(ls[:], ls[:], ACT.Exp).then_inc(lam_exp, 1)

            @block.vector
            def _(dve):
                dve.wait_ge(x_in, 64)
                with dve.Fori(0, B) as b:
                    dve.bn_stats(m["stats"][:, b, :], m["x"][:, b, :])
                dve.memset(m["onesb"][:], 1.0)
                dve.memset(m["mean"][:], 1.0 / P)
                dve.memset(m["ones"][:], 1.0)
                dve.wait_ge(c_in, 32)
                c = Chain(dve, steps)
                c(dve.tensor_tensor(lp[:], lq[:, 0:4:2, :], lq[:, 1:4:2, :], ALU.mult))
                c(dve.tensor_reduce(ls[:], lp[:], AX.X, ALU.add))
                dve.sem_inc(lam_ready, 1)
                dve.wait_ge(lam_exp, 1)
                dve.scalar_tensor_tensor(m["lam"][:], ls[:, 0:1], LAMBDA_INIT, ls[:, 1:2], ALU.add, ALU.subtract)
                dve.wait_ge(w_in, 16 * (2 + len(small) + 2 * len(m["sel"])))
                dve.tensor_copy(m["identb"][:], m["mat"]["ident"])
                dve.tensor_scalar(m["negident"][:], m["mat"]["ident"], -1.0, None, ALU.mult)

        sem.clear()


def program(nc, a, out):
    with ExitStack() as ctx:
        def sb(n, shape, dt=F32):
            return ctx.enter_context(nc.sbuf_tensor(n, shape, dt))

        m = {}
        m["x"] = sb("x_all", [P, B, D])
        m["ctxT"] = sb("ctxT", [P, B, P])
        m["big"] = sb("big", [P, B, P])
        m["stats"] = sb("stats", [P, B, 6])
        m["mats"] = sb("mats", [P, len(MATS), P])
        m["cols"] = sb("cols", [P, len(COLS)])
        m["rows"] = sb("rows", [P, len(ROWS), P])
        m["mat"] = {n: m["mats"][:, i, :] for i, n in enumerate(MATS)}
        m["col"] = {n: m["cols"][:, i:i + 1] for i, n in enumerate(COLS)}
        m["row"] = {n: m["rows"][:, i, :] for i, n in enumerate(ROWS)}
        m["sel"] = {"sel8": (sb("sel8_q", [P, 2, 4, P], F16), sb("sel8_k", [P, 2, 4, P], F16)),
                    "sel4": (sb("sel4_q", [P, 2, 4, P], F16), sb("sel4_k", [P, 2, 4, P], F16)),
                    "sel4x2": (sb("sel4x2_q", [P, 2, 8, P], F16), sb("sel4x2_k", [P, 2, 8, P], F16))}
        m.update({"sel8": m["sel"]["sel8"], "sel4": m["sel"]["sel4"], "sel4x2": m["sel"]["sel4x2"]})
        m["maskq"] = sb("maskq", [P, B, P], U8)
        m["maskk"] = sb("maskk", [P, B, P], U8)
        m["identb"], m["negident"], m["onesb"] = (sb("identb", [P, P], BF16), sb("negident", [P, P], F16),
                                                  sb("onesb", [P, P], BF16))
        m["mean"], m["ones"], m["lam"] = sb("mean", [P, 1]), sb("ones", [1, P]), sb("lam", [P, 1])
        m["router_w"], m["gate_w"] = sb("router_w", [P, E]), sb("gate_w", [P, E])
        m["z_w1"], m["z_w2"] = sb("z_w1", [P, 32]), sb("z_w2", [32, E])
        m["down"], m["iota"] = sb("down", [P, E]), sb("iota", [P, 32])
        m["s_b1"], m["s_b2"], m["s_hot"] = sb("s_b1", [E, P]), sb("s_b2", [E + 1, P]), sb("s_hot", [E + 1, 3, 512])
        m["logits"] = sb("logits", [P, B, E])
        m["weights_in"] = ctx.enter_context(nc.semaphore("weights_in"))
        m["weights_count"] = 16 * 7
        m["m_in"], m["z_in"] = (ctx.enter_context(nc.semaphore("m_in")), ctx.enter_context(nc.semaphore("z_in")))
        m["pool"] = sb("pool", [P, 3, 4096])
        m["e_w1"] = m["pool"][:, 0].rearrange("p (e f) -> p e f", e=E)
        m["e_w2"] = m["pool"][:, 1].rearrange("p (e c d) -> p e c d", e=E, c=4)
        m["z_wa"] = m["pool"][:, 0]
        m["z_wb"] = m["pool"][:, 1].rearrange("p (e n) -> p e n", e=E)
        m["m_w1"] = m["pool"][:, 0, 0:2048].rearrange("p (e f) -> p e f", e=E)
        m["m_w2"] = m["pool"][:, 0, 2048:4096].rearrange("p (e c d) -> p e c d", e=E, c=2)
        m["m_b2"] = m["pool"][:, 1, 0:2048].rearrange("p (b d) -> p b d", b=16)
        m["s_w1"], m["s_w3"], m["s_w2"] = sb("s_w1", [P, 2, P]), sb("s_w3", [P, 2, P]), sb("s_w2", [P, 2, P])
        m["s_up"], m["s_down"] = sb("s_up", [P, E, P]), sb("s_down", [P, E, P])

        load(nc, m, a)
        attention(nc, m, "a0", 16, 8, 8, 8 ** -0.5, False, False, False, "x", "sel8")
        expert_choice(nc, m)
        recurrence(nc, m)
        attention(nc, m, "a1", 16, 4, 4, 0.5, True, False, False, "moe", "sel4",
                  [(m["m_w1"], a["m_w1"]), (m["m_w2"], a["m_w2"]), (m["m_b2"], a["m_b2"])], m["m_in"])
        top_two_mixture(nc, m)
        attention(nc, m, "a2", 16, 8, 8, 8 ** -0.5, False, True, False, "x", "sel8")
        hashed_mixture(nc, m)
        attention(nc, m, "a3", 32, 4, 8, 0.5, False, False, True, "x", "sel4x2",
                  [(m["z_wa"], a["z_wa"]), (m["z_wb"], a["z_wb"])], m["z_in"])
        zones(nc, m, a, out)



def lay_out(i):
    f = np.float32

    def t(n):
        return np.ascontiguousarray(np.asarray(i[n]).T)

    def g(n):
        return np.asarray(i[n])

    def spread(w, n=4, by=8):
        w = w.reshape(-1, H, n)
        o = np.zeros((w.shape[0], H, by), f)
        o[:, :, :n] = w
        return o.reshape(-1, H * by)

    def wide(w):
        o = np.zeros((P, P), f)
        o[:w.shape[0], :w.shape[1]] = w
        return o

    def row(v):
        o = np.zeros(P, f)
        o[:v.size] = v.reshape(-1)
        return o

    ip, ib = g("L3_xattn_in_proj_weight"), g("L3_xattn_in_proj_bias")
    mats = {"a0_q": t("L0_xattn_w_q"), "a0_k": t("L0_xattn_w_k"), "a0_v": t("L0_xattn_w_v"), "a0_o": t("L0_xattn_w_o"),
            "r_wi": t("L1_xattn_Wi"), "r_wg": t("L1_xattn_Wg"), "r_a": t("L1_xattn_A"), "r_bm": t("L1_xattn_Bm"),
            "r_wo": t("L1_xattn_Wo"), "a1_q": g("L1_ffn_q_w"), "a1_k": spread(g("L1_ffn_k_w")),
            "a1_v": wide(g("L1_ffn_v_w")), "a1_o": g("L1_ffn_o_w"), "a2_q": g("L2_xattn_Wq"), "a2_k": g("L2_xattn_Wk"),
            "a2_v": g("L2_xattn_Wv"), "a2_o": g("L2_xattn_Wo"), "a3_q": ip[:P].T, "a3_k": ip[P:2 * P].T,
            "a3_v": ip[2 * P:].T, "a3_o": t("L3_xattn_out_proj_weight"), "ident": np.eye(P, dtype=f),
            "tri": np.triu(np.ones((P, P), f))}
    b1 = g("L1_ffn_b1").reshape(-1, P)
    cols = {"a0_q": g("L0_xattn_b_q"), "a0_k": g("L0_xattn_b_k"), "a1_q": g("L1_ffn_q_b"),
            "a1_k": spread(g("L1_ffn_k_b")[None])[0], "a1_o": g("L1_ffn_o_b"), "a2_q": g("L2_xattn_bq"),
            "a2_k": g("L2_xattn_bk"), "a3_q": ib[:P], "a3_k": ib[P:2 * P], "r_bi": g("L1_xattn_bi"), "r_bg": g("L1_xattn_bg"),
            "decay": np.repeat(g("L1_xattn_decay").reshape(H), D // H), "sb1_0": g("L2_ffn_sb1")[:P],
            "sb1_1": g("L2_ffn_sb1")[P:], "sb3_0": g("L2_ffn_sb3")[:P], "sb3_1": g("L2_ffn_sb3")[P:]}
    cols.update({f"m_b1_{k}": b1[k] for k in range(16)})
    rows = {"a0_v": g("L0_xattn_b_v"), "a0_o": g("L0_xattn_b_o"), "a1_v": row(g("L1_ffn_v_b")), "a2_v": g("L2_xattn_bv"),
            "a2_o": g("L2_xattn_bo"), "a3_v": ib[2 * P:], "a3_o": g("L3_xattn_out_proj_bias"), "r_bo": g("L1_xattn_bo"),
            "router_b": row(g("L1_ffn_router_b")), "z_b1": row(g("L3_ffn_b1")), "z_b2": row(g("L3_ffn_b2"))}

    def select(nblk, hd, parts, rows_of=None):
        o = np.zeros((P, 2, nblk, P), np.float16)
        for blk in range(nblk):
            for grp in range(4):
                src = (4 * blk + grp) * (P // (4 * nblk))
                for s, part in enumerate(parts):
                    for d in range(hd):
                        o[src + d, part, blk, 32 * grp + s * hd + d] = 1
        return o

    mask = g("mask_Bx1xSxS2_bk0").reshape(B, P, P)
    b2 = g("L1_ffn_b2")
    m_b2 = np.zeros((16, E, 16, P), f)
    for k in range(16):
        m_b2[k, :, k] = b2
    hot = np.zeros((E + 1, 3, 8, 64), f)
    for r in range(8):
        for k in range(2):
            hot[HASHED[k][r], k, r] = 1
            hot[HASHED[k][r], 2, r] += 1
    hot[E, 2] = 2
    w2 = g("L0_ffn_w2").reshape(E, 4, P, D)
    return {
        "x": g("x").transpose(1, 0, 2), "ctxT": g("ctx_1024").transpose(2, 0, 1),
        "mats": np.stack([mats[n] for n in MATS], 1), "cols": np.stack([cols[n] for n in COLS], 1),
        "rows": np.stack([rows[n] for n in ROWS], 0),
        "sel8_q": select(4, 8, (0, 1, 0)), "sel8_k": select(4, 8, (0, 0, 1)),
        "sel4_q": select(4, 4, (0, 1, 0)), "sel4_k": select(4, 4, (0, 0, 1)),
        "sel4x2_q": select(8, 4, (0, 1, 0)), "sel4x2_k": select(8, 4, (0, 0, 1)),
        "maskq": mask.transpose(1, 0, 2), "maskk": mask.transpose(2, 0, 1),
        "router_w": g("L1_ffn_router_w"), "gate_w": g("L0_ffn_gate_w"), "z_w1": g("L3_ffn_W1"), "z_w2": g("L3_ffn_W2"),
        "down": np.tile(np.arange(E, 0, -1, dtype=f), (P, 1)), "iota": np.tile(np.arange(1, 33, dtype=f), (P, 1)),
        "s_b1": g("L2_ffn_b1"), "s_b2": np.concatenate([g("L2_ffn_b2"), g("L2_ffn_sb2")[None]], 0),
        "s_hot": hot.reshape(E + 1, 3, 512),
        "lams": np.stack([g("L3_xattn_lambda_q1"), g("L3_xattn_lambda_k1"), g("L3_xattn_lambda_q2"),
                          g("L3_xattn_lambda_k2")]),
        "e_w1": g("L0_ffn_w1").transpose(1, 0, 2), "e_w2": w2.transpose(2, 0, 1, 3),
        "m_w1": g("L1_ffn_w1").transpose(1, 0, 2), "m_w2": g("L1_ffn_w2").reshape(E, 2, P, D).transpose(2, 0, 1, 3),
        "m_b2": m_b2.reshape(P, 16, P),
        "s_w1": g("L2_ffn_sw1").reshape(P, 2, P), "s_w3": g("L2_ffn_sw3").reshape(P, 2, P),
        "s_w2": g("L2_ffn_sw2").reshape(2, P, P).transpose(1, 0, 2),
        "s_up": g("L2_ffn_w1").transpose(1, 0, 2), "s_down": g("L2_ffn_w2").transpose(1, 0, 2),
        "z_wa": g("L3_ffn_Wa").transpose(1, 0, 2).reshape(P, 4096),
        "z_wb": g("L3_ffn_Wb").reshape(E, 4, P, D).transpose(2, 0, 1, 3).reshape(P, E, 512),
    }


def kernel(**inputs):
    import concourse.bacc as bacc
    from concourse.bass_utils import run_bass_kernel_spmd

    nc = bacc.Bacc("TRN2", target_bir_lowering=False, num_devices=1)
    arrays = {f"in_{n}": np.ascontiguousarray(v) for n, v in lay_out(inputs).items()}
    a = {n[3:]: nc.dram_tensor(n, v.shape, mybir.dt.from_np(v.dtype), kind="ExternalInput").ap() for n, v in arrays.items()}
    out = nc.dram_tensor("out", (P, B, D), F32, kind="ExternalOutput").ap()
    program(nc, a, out)
    r = run_bass_kernel_spmd(nc, [arrays], core_ids=[0])
    return np.ascontiguousarray(r.results[0]["out"].transpose(1, 0, 2))
```

```python
from contextlib import ExitStack

import numpy as np
import concourse.bass as bass
from concourse import mybir
from concourse.alu_op_type import AluOpType as ALU

F32 = mybir.dt.float32
F16 = mybir.dt.float16
BF16 = mybir.dt.bfloat16
U32 = mybir.dt.uint32
I32 = mybir.dt.int32
U8 = mybir.dt.uint8
ACT = mybir.ActivationFunctionType
AX = mybir.AxisListType

P = 128
B = 32
D = 128
H = 16
E = 8
EPS = 1e-5
NEG = -1.0e9
LAMBDA_INIT = 0.2
HASHED = [[(11 * r + k * 7919) % 8 for r in range(8)] for k in range(2)]

MATS = ["a0_q", "a0_k", "a0_v", "a0_o", "r_wi", "r_wg", "r_a", "r_bm", "r_wo", "a1_q", "a1_k", "a1_v", "a1_o",
        "a2_q", "a2_k", "a2_v", "a2_o", "a3_q", "a3_k", "a3_v", "a3_o", "ident", "tri"]
COLS = ["a0_q", "a0_k", "a1_q", "a1_k", "a1_o", "a2_q", "a2_k", "a3_q", "a3_k", "r_bi", "r_bg", "decay",
        "sb1_0", "sb1_1", "sb3_0", "sb3_1"] + [f"m_b1_{i}" for i in range(16)]
ROWS = ["a0_v", "a0_o", "a1_v", "a2_v", "a2_o", "a3_v", "a3_o", "r_bo", "router_b", "z_b1", "z_b2"]


class Chain:

    def __init__(self, eng, sem, at=0):
        self.eng, self.sem, self.at, self.n = eng, sem, at, 0

    def link(self, ins):
        ins.then_inc(self.sem, 1)
        self.n += 1
        self.eng.wait_ge(self.sem, self.at + self.n)

    def __call__(self, ins):
        self.link(ins)


class Semaphores:

    def __init__(self, nc, ctx, name):
        self.nc, self.ctx, self.name, self.taken = nc, ctx, name, []

    def __call__(self, n):
        self.taken.append(self.ctx.enter_context(self.nc.semaphore(f"{self.name}_{n}")))
        return self.taken[-1]

    def clear(self):
        with self.nc.Block() as block:

            @block.gpsimd
            def _(pool):
                for s in self.taken:
                    pool.sem_clear(s)


def wait(eng, sem, value):
    if isinstance(value, int) and value < 1:
        return
    eng.wait_ge(sem, value)


def over_batches(eng, step, n=B):
    step(0, 0)
    step(1, 1)
    with eng.Fori(1, n // 2 - 1) as i:
        for u in range(2):
            step(2 * i + u, u)
    step(n - 2, 0, n - 1)
    step(n - 1, 1, n - 1)


def attention(nc, m, name, nsub, hd, vd, scale, own, masked, differs, ends, sel, ahead=(), ahead_in=None):
    nblk = nsub // 4
    NH = nblk // 4
    NQ = nblk
    POOL_LOW = [j for j in range(NQ) if j % 2 or j == NQ // 2]
    V1 = vd + 1
    VW = H * vd
    with ExitStack() as ctx:
        def sb(n, shape, dt=F32):
            return ctx.enter_context(nc.sbuf_tensor(f"{name}_{n}", shape, dt))

        def ps(n, shape, dt=F32):
            return ctx.enter_context(nc.psum_tensor(f"{name}_{n}", shape, dt))

        sem = Semaphores(nc, ctx, name)

        selq, selk = m[sel]
        xn = sb("xn", [P, 2, D])
        xb = sb("xb", [P, 2, D])
        xnT = sb("xnT", [P, 2, P])
        src = xnT if own else sb("ctxs", [P, 2, P])
        hi = sb("hi", [P, 2, 2, P], F16)
        lo = sb("lo", [P, 2, 2, P], F16)
        qall = sb("qall", [P, 4, P], F16)
        qst = sb("qst", [P, 2, 4, nblk, P], F16)
        kst = sb("kst", [P, 2, nblk, P], F16)
        v32 = sb("v32", [P, H, vd])
        vhi = sb("vhi", [P, 2, H, V1], F16)
        vlo = sb("vlo", [P, 2, H, vd], F16)
        zero = sb("zero", [P, H, vd])
        mx = sb("mx", [P, 2, 4], F16)
        eight = sb("eight", [P, 1])
        pr = sb("pr", [P, 2, 4, P])
        phi = sb("phi", [P, 4, 4, P], F16)
        plo = sb("plo", [P, 4, 4, P], F16)
        rec = sb("rec", [P, nsub])
        on = sb("on", [P, 2, D])
        on2 = sb("on2", [P, D])
        oT = sb("oT", [P, 2, P])
        lnv = sb("lnv", [P, 6, B])
        rstd = sb("rstd", [P, B])
        nmr = sb("nmr", [P, B])
        qm = sb("qm", [P, 2, P]) if masked else None
        nbq = sb("nbq", [P, 2, P], BF16) if masked else None
        nbk = sb("nbk", [P, 2, P], BF16) if masked else None
        keepb = sb("keepb", [P, 2, P], BF16) if masked else None
        anyq = sb("anyq", [P, 2]) if masked else None
        anyb = sb("anyb", [P, 2, P]) if masked else None
        mT = sb("mT", [P, 2, P]) if ends == "moe" else None

        s_ps = ps("s", [P, 2, 4, P])
        st_ps = ps("st", [P, 2, 4, P])
        stack_ps = ps("stack", [P, 4, P])
        in_ps = ps("in", [P, 4, P])
        out_ps = ps("out", [P, 4, P])
        o_ps = ps("o", [P, 512])
        o_h = o_ps[:, 0:nsub * V1].rearrange("p (h c) -> p h c", c=V1)

        ln_ready, pow_ready = sem("ln_ready"), sem("pow_ready")
        xn_ready, xT_done, xnT_ready = sem("xn_ready"), sem("xT_done"), sem("xnT_ready")
        src_ready, xb_ready = sem("src_ready"), sem("xb_ready")
        kv_done, q_done = sem("kv_done"), sem("q_done")
        khi, klo, qhi, qlo = sem("khi"), sem("klo"), sem("qhi"), sem("qlo")
        v32_ready, vhi_ready, vlo_ready = sem("v32_ready"), sem("vhi_ready"), sem("vlo_ready")
        kstack, qstack, kst_ready, qall_ready, qst_ready = (sem("kstack"), sem("qstack"), sem("kst_ready"),
                                                            sem("qall_ready"), sem("qst_ready"))
        s_done, mx_ready, st_done, pv_done = sem("s_done"), sem("mx_ready"), sem("st_done"), sem("pv_done")
        pr_ready, phi_ready = sem("pr_ready"), sem("phi_ready")
        plo_ready = [sem(f"plo_ready{j}") for j in range(NQ)]
        on_done, oT_done, oT_ready, y_done, x_done = (sem("on_done"), sem("oT_done"), sem("oT_ready"),
                                                      sem("y_done"), sem("x_done"))
        steps, ones_set = sem("steps"), sem("ones_set")
        keep_ready, cnt_done, any_ready, mask_steps, nbk_ready, qm_ready = (
            sem("keep_ready"), sem("cnt_done"), sem("any_ready"), sem("mask_steps"), sem("nbk_ready"), sem("qm_ready"))
        mT_ready, lg_done, lg_ready, mhi_ready, mT_kept, x_sum = (sem("mT_ready"), sem("lg_done"), sem("lg_ready"),
                                                                  sem("mhi_ready"), sem("mT_kept"), sem("x_sum"))

        def there(b, d):
            return not isinstance(b, int) or 0 <= b + d < B

        def low_part(eng, ops, b, j):
            n = NQ * b + j
            eng.wait_ge(pr_ready, n + 1)
            eng.wait_ge(phi_ready, n + 1)
            wait(eng, pv_done, n - 3)
            ops.tensor_tensor(plo[:, j % 4], pr[:, j % 2], phi[:, j % 4], ALU.subtract).then_inc(plo_ready[j], 1)

        with nc.Block() as block:

            @block.sync
            def _(sp):
                if ahead and ahead_in is not m["weights_in"]:
                    sp.wait_ge(m["weights_in"], m["weights_count"])
                for to, frm in ahead:
                    sp.dma_start(to, frm).then_inc(ahead_in, 16)

            @block.gpsimd
            def _(pool):
                pool.memset(vhi[:], 1.0).then_inc(ones_set, 1)
                pool.memset(on[:], 0.0).then_inc(ones_set, 1)
                pool.memset(qst[:], 0.0).then_inc(ones_set, 1)
                pool.memset(eight[:], 8.0).then_inc(ones_set, 1)
                pool.memset(zero[:], 0.0).then_inc(ones_set, 1)
                pool.memset(lnv[:, 5, :], -0.5).then_inc(ones_set, 1)
                pool.wait_ge(ones_set, 6)

                def source(b, u):
                    if own:
                        pool.wait_ge(xn_ready, b + 1)
                        nc.gpsimd.tensor_tensor(m["x"][:, b, :], m["x"][:, b, :], xn[:, u, :], ALU.add).then_inc(x_sum, 1)
                    else:
                        wait(pool, kv_done, b - 1)
                        nc.gpsimd.tensor_copy(src[:, u, :], m["ctxT"][:, b, :]).then_inc(src_ready, 1)

                def split_v(b, u):
                    pool.wait_ge(v32_ready, b + 1)
                    wait(pool, pv_done, NQ * (b - 1))
                    nc.gpsimd.tensor_tensor(vhi[:, u, :, 0:vd], v32[:], zero[:], ALU.add).then_inc(vhi_ready, 1)
                    pool.wait_ge(vhi_ready, b + 1)
                    nc.gpsimd.tensor_tensor(vlo[:, u], v32[:], vhi[:, u, :, 0:vd], ALU.subtract).then_inc(vlo_ready, 1)

                def to_mixture(b, u):
                    pool.wait_ge(mT_ready, b + 1)
                    nc.gpsimd.tensor_copy(m["y_parts"][:, 0, b, :], mT[:, u, :]).then_inc(mhi_ready, 1)
                    pool.wait_ge(mhi_ready, b + 1)
                    nc.gpsimd.tensor_tensor(m["y_parts"][:, 1, b, :], mT[:, u, :], m["y_parts"][:, 0, b, :], ALU.subtract)\
                        .then_inc(mT_kept, 1)

                def x_and_bias(b, u):
                    wait(pool, x_done, b - 1)
                    nc.gpsimd.tensor_tensor(xb[:, u, :], m["x"][:, b, :], m["row"][f"{name}_o"], ALU.add)\
                        .then_inc(xb_ready, 1)

                if not own:
                    source(0, 0)
                pool.wait_ge(ln_ready, 1)
                nc.gpsimd.tensor_tensor(rstd[:], lnv[:, 4, :], lnv[:, 5, :], ALU.pow).then_inc(pow_ready, 1)
                if own:
                    source(0, 0)
                split_v(0, 0)
                source(1, 1)

                def step(b, u, last=None):
                    if there(b, -1):
                        low_part(pool, nc.gpsimd, b - 1, NQ - 1)
                    if own and there(b, -2):
                        to_mixture(b - 2, u)
                    if there(b, 1):
                        split_v(b + 1, 1 - u)
                    if there(b, 2):
                        source(b + 2, u)
                    for j in POOL_LOW[:-1]:
                        low_part(pool, nc.gpsimd, b, j)
                    if not own:
                        x_and_bias(b, u)

                over_batches(pool, step)
                low_part(pool, nc.gpsimd, B - 1, NQ - 1)
                if own:
                    to_mixture(B - 2, 0)
                    to_mixture(B - 1, 1)

            @block.vector
            def _(dve):
                layernorm_stats(nc, dve, m, lnv, rstd, nmr, steps, ln_ready, pow_ready)
                LN = LN_STEPS
                per = 5 if differs else 1

                def normalise(b, u):
                    wait(dve, xT_done, b - 1)
                    if own:
                        wait(dve, x_sum, b - 1)
                    dve.tensor_scalar(xn[:, u, :], m["x"][:, b, :], rstd[:, bass.ds(b, 1)], nmr[:, bass.ds(b, 1)],
                                      ALU.mult, ALU.add).then_inc(xn_ready, 1)

                def mask_keep(b, u):
                    wait(dve, cnt_done, b - 1)
                    dve.tensor_copy(keepb[:, u, :], m["maskk"][:, b, :]).then_inc(keep_ready, 1)

                def mask_any(b, u):
                    dve.wait_ge(cnt_done, b + 1)
                    dve.wait_ge(xnT_ready, b + 1)
                    dve.tensor_scalar(anyb[:, u, :], in_ps[:, 1, :], 1.0, None, ALU.min).then_inc(any_ready, 1)

                def mask_rows(b, u):
                    wait(dve, s_done, NQ * (b - 1))
                    wait(dve, st_done, NQ * (b - 1))
                    dve.wait_ge(any_ready, b + 1)
                    dve.tensor_reduce(anyq[:, u:u + 1], m["maskq"][:, b, :], AX.X, ALU.max).then_inc(mask_steps, 1)
                    dve.tensor_scalar(nbq[:, u, :], m["maskq"][:, b, :], -1.0, -NEG, ALU.add, ALU.mult).then_inc(mask_steps, 1)
                    dve.scalar_tensor_tensor(nbk[:, u, :], keepb[:, u, :], -1.0, anyb[:, u, :], ALU.add, ALU.mult)\
                        .then_inc(mask_steps, 1)
                    dve.wait_ge(mask_steps, 3 * b + 3)
                    dve.tensor_scalar(nbq[:, u, :], nbq[:, u, :], anyq[:, u:u + 1], None, ALU.mult).then_inc(nbk_ready, 1)
                    dve.tensor_scalar(nbk[:, u, :], nbk[:, u, :], -NEG, None, ALU.mult).then_inc(nbk_ready, 1)

                def k_low(b, u):
                    dve.wait_ge(khi, b + 1)
                    if not masked:
                        dve.wait_ge(qhi, b + 1)
                    wait(dve, kstack, NH * (b - 1))
                    dve.scalar_tensor_tensor(lo[:, u, 1, :], in_ps[:, 2, :], m["col"][f"{name}_k"], hi[:, u, 1, :],
                                             ALU.add, ALU.subtract).then_inc(klo, 1)

                def v_bias(b, u):
                    dve.wait_ge(khi if masked else qhi, b + 1)
                    wait(dve, vlo_ready, b)
                    dve.tensor_tensor(v32[:], in_ps[:, 3, 0:VW].rearrange("p (h c) -> p h c", c=vd),
                                      m["row"][f"{name}_v"][:, 0:VW].rearrange("p (h c) -> p h c", c=vd), ALU.add)\
                        .then_inc(v32_ready, 1)

                def q_masked(b, u):
                    dve.wait_ge(khi, b + 1)
                    dve.wait_ge(any_ready, b + 1)
                    wait(dve, qhi, b - 1)
                    dve.scalar_tensor_tensor(qm[:, u, :], in_ps[:, 1, :], m["col"][f"{name}_q"], anyb[:, u, :],
                                             ALU.add, ALU.mult).then_inc(qm_ready, 1)

                def q_low(b, u):
                    dve.wait_ge(qhi, b + 1)
                    wait(dve, qstack, NH * (b - 1))
                    if masked:
                        dve.wait_ge(qm_ready, b + 1)
                        dve.tensor_tensor(lo[:, u, 0, :], qm[:, u, :], hi[:, u, 0, :], ALU.subtract).then_inc(qlo, 1)
                    else:
                        dve.scalar_tensor_tensor(lo[:, u, 0, :], in_ps[:, 1, :], m["col"][f"{name}_q"], hi[:, u, 0, :],
                                                 ALU.add, ALU.subtract).then_inc(qlo, 1)

                def q_spread(b, u, half, groups=range(4)):
                    dve.wait_ge(qall_ready, NH * b + half + 1)
                    wait(dve, st_done, NQ * (b - 1))
                    for g in groups:
                        r = slice(32 * g, 32 * g + 32)
                        dve.tensor_copy(qst[r, u, g, 4 * half:4 * half + 4, :], qall[r]).then_inc(qst_ready, 1)

                def maximum(b, j):
                    n = NQ * b + j
                    dve.wait_ge(s_done, n + 1)
                    wait(dve, st_done, n - 1)
                    dve.tensor_reduce(mx[:, j % 2, :], s_ps[:, j % 2], AX.X, ALU.max).then_inc(mx_ready, 1)

                def divide(b, u):
                    dve.wait_ge(pv_done, NQ * (b + 1))
                    c = Chain(dve, steps, LN + per * b)
                    c(dve.reciprocal(rec[:], o_h[:, :, vd]))
                    out = on[:, u, 0:VW].rearrange("p (h c) -> p h c", c=vd)
                    if differs:
                        o4 = o_h.rearrange("p (h s) c -> p h s c", s=2)
                        r4 = rec[:].rearrange("p (h s) -> p h s", s=2)
                        c(dve.tensor_scalar(rec[:], rec[:], 1.0 - LAMBDA_INIT, None, ALU.mult))
                        c(dve.tensor_tensor(r4[:, :, 1], r4[:, :, 1], m["lam"][:, 0:1].broadcast_to([P, H]), ALU.mult))
                        c(dve.tensor_tensor(on2[:].rearrange("p (h c) -> p h c", c=vd), o4[:, :, 1, 0:vd],
                                            r4[:, :, 1].unsqueeze(2).broadcast_to([P, H, vd]), ALU.mult))
                        c(dve.tensor_tensor(out, o4[:, :, 0, 0:vd], r4[:, :, 0].unsqueeze(2).broadcast_to([P, H, vd]), ALU.mult))
                        dve.scalar_tensor_tensor(on[:, u, :], on2[:], -1.0, on[:, u, :], ALU.mult, ALU.add).then_inc(on_done, 1)
                    else:
                        dve.tensor_tensor(out, o_h[:, :, 0:vd], rec[:].unsqueeze(2).broadcast_to([P, H, vd]), ALU.mult)\
                            .then_inc(on_done, 1)

                def finish(b, u):
                    if own:
                        dve.wait_ge(lg_done, b + 1)
                        dve.tensor_tensor(m["logits"][:, b, :], out_ps[:, 2, 0:E], m["row"]["router_b"][:, 0:E], ALU.add)\
                            .then_inc(lg_ready, 1)
                        return
                    dve.wait_ge(y_done, b + 1)
                    dve.wait_ge(xb_ready, b + 1)
                    dve.tensor_tensor(m["x"][:, b, :], out_ps[:, 1, :], xb[:, u, :], ALU.add).then_inc(x_done, 1)

                def statistics(b):
                    dve.wait_ge(x_done, b + 1)
                    dve.bn_stats(m["stats"][:, b, :], m["x"][:, b, :])

                dve.wait_ge(ones_set, 6)
                normalise(0, 0)
                if masked:
                    mask_keep(0, 0)
                    mask_any(0, 0)
                if masked:
                    q_masked(0, 0)
                k_low(0, 0)
                v_bias(0, 0)
                q_low(0, 0)
                normalise(1, 1)
                if masked:
                    mask_keep(1, 1)
                    mask_rows(0, 0)
                for half in range(NH):
                    q_spread(0, 0, half)
                if masked:
                    mask_any(1, 1)
                maximum(0, 0)

                def step(b, u, last=None):
                    if masked and there(b, 1):
                        q_masked(b + 1, 1 - u)
                    maximum(b, 1)
                    if there(b, 1):
                        k_low(b + 1, 1 - u)
                        v_bias(b + 1, 1 - u)
                        q_low(b + 1, 1 - u)
                    if there(b, -2):
                        finish(b - 2, u)
                    maximum(b, 2)
                    low_part(dve, nc.vector, b, 0)
                    if masked and there(b, 1):
                        mask_rows(b + 1, 1 - u)
                    if there(b, 2):
                        normalise(b + 2, u)
                        if masked:
                            mask_keep(b + 2, u)
                    if there(b, -1):
                        divide(b - 1, 1 - u)
                    maximum(b, 3)
                    if NQ == 4 and there(b, 1):
                        q_spread(b + 1, 1 - u, 0)
                    for j in range(4, NQ):
                        maximum(b, j)
                        if j - 2 not in POOL_LOW:
                            low_part(dve, nc.vector, b, j - 2)
                        if there(b, 1) and j != 6:
                            q_spread(b + 1, 1 - u, j // 6, (2, 3) if j == 5 else (0, 1))
                    if there(b, 1):
                        maximum(b + 1, 0)
                    if NQ - 2 not in POOL_LOW:
                        low_part(dve, nc.vector, b, NQ - 2)
                    if there(b, 1) and NH == 2:
                        q_spread(b + 1, 1 - u, 1, (2, 3))
                    if masked and there(b, 2):
                        mask_any(b + 2, u)
                    if not own and there(b, -2):
                        statistics(b - 2)

                over_batches(dve, step)
                finish(B - 2, 0)
                divide(B - 1, 1)
                finish(B - 1, 1)
                if not own:
                    statistics(B - 2)
                    statistics(B - 1)

            @block.scalar
            def _(act):
                act.preload_act_table(ACT.Exp)
                act.wait_ge(ones_set, 6)

                def x_keep(b, u):
                    act.wait_ge(xT_done, b + 1)
                    wait(act, q_done, b - 1)
                    wait(act, kv_done, b - 1)
                    act.activation(xnT[:, u, :], in_ps[:, 0, :], ACT.Copy).then_inc(xnT_ready, 1)

                def k_high(b, u):
                    act.wait_ge(kv_done, b + 1)
                    wait(act, kstack, NH * (b - 1))
                    act.activation(hi[:, u, 1, :], in_ps[:, 2, :], ACT.Identity, bias=m["col"][f"{name}_k"]).then_inc(khi, 1)

                def q_high(b, u):
                    wait(act, qstack, NH * (b - 1))
                    if masked:
                        act.wait_ge(qm_ready, b + 1)
                        act.activation(hi[:, u, 0, :], qm[:, u, :], ACT.Copy).then_inc(qhi, 1)
                        return
                    act.activation(hi[:, u, 0, :], in_ps[:, 1, :], ACT.Identity, bias=m["col"][f"{name}_q"]).then_inc(qhi, 1)

                def k_keep(b, u, half):
                    act.wait_ge(kstack, NH * b + half + 1)
                    wait(act, st_done, NQ * (b - 1))
                    act.activation(kst[:, u, 4 * half:4 * half + 4, :], stack_ps[:], ACT.Copy).then_inc(kst_ready, 1)

                def q_keep(b, half):
                    act.wait_ge(qstack, NH * b + half + 1)
                    wait(act, qst_ready, 4 * (NH * b + half))
                    act.activation(qall[:], stack_ps[:], ACT.Copy).then_inc(qall_ready, 1)

                def exp(b, j):
                    n = NQ * b + j
                    act.wait_ge(st_done, n + 1)
                    wait(act, pv_done, n - 3)
                    act.activation(phi[:, j % 4], st_ps[:, j % 2], ACT.Exp, bias=eight[:], scale=scale).then_inc(phi_ready, 1)
                    wait(act, plo_ready[(j - 2) % NQ], b + 1 if j >= 2 else b)
                    act.activation(pr[:, j % 2], st_ps[:, j % 2], ACT.Exp, bias=eight[:], scale=scale).then_inc(pr_ready, 1)

                def o_keep(b, u):
                    act.wait_ge(oT_done, b + 1)
                    act.activation(oT[0:VW, u, :], out_ps[0:VW, 0, :], ACT.Copy).then_inc(oT_ready, 1)

                def m_keep(b, u):
                    act.wait_ge(y_done, b + 1)
                    wait(act, mT_kept, b)
                    act.activation(mT[:, u, :], out_ps[:, 1, :], ACT.Identity, bias=m["col"]["a1_o"]).then_inc(mT_ready, 1)

                x_keep(0, 0)
                k_high(0, 0)
                q_high(0, 0)
                for half in range(NH):
                    k_keep(0, 0, half)
                for half in range(NH):
                    q_keep(0, half)
                x_keep(1, 1)

                def step(b, u, last=None):
                    if there(b, 1):
                        k_high(b + 1, 1 - u)
                        q_high(b + 1, 1 - u)
                    exp(b, 0)
                    for j in range(1, NQ):
                        if there(b, 1) and j <= NH:
                            k_keep(b + 1, 1 - u, j - 1)
                        if there(b, 1) and j in ((2,) if NH == 1 else (3, 5)):
                            q_keep(b + 1, int(j == 5))
                        if own and there(b, -1) and j == 3:
                            m_keep(b - 1, 1 - u)
                        if there(b, 2) and j == NQ - 1:
                            x_keep(b + 2, u)
                        exp(b, j)
                        if there(b, -1) and j == 2:
                            o_keep(b - 1, 1 - u)

                over_batches(act, step)
                o_keep(B - 1, 1)
                if own:
                    m_keep(B - 1, 1)

            @block.tensor
            def _(pe):
                def x_turn(b, u):
                    pe.wait_ge(xn_ready, b + 1)
                    wait(pe, klo, b)
                    wait(pe, v32_ready, b)
                    wait(pe, qlo, b)
                    if masked:
                        pe.wait_ge(keep_ready, b + 1)
                        pe.matmul(in_ps[:, 1, :], m["onesb"][:], keepb[:, u, :], start=True, stop=True).then_inc(cnt_done, 1)
                    pe.transpose(in_ps[:, 0, :], xn[:, u, :], m["mat"]["ident"]).then_inc(xT_done, 1)

                def dense(b, u):
                    pe.wait_ge(xnT_ready, b + 1)
                    if masked:
                        pe.wait_ge(any_ready, b + 1)
                    pe.matmul(in_ps[:, 1, :], m["mat"][f"{name}_q"], xnT[:, u, :], start=True, stop=True).then_inc(q_done, 1)
                    if not own:
                        pe.wait_ge(src_ready, b + 1)
                    pe.matmul(in_ps[:, 2, :], m["mat"][f"{name}_k"], src[:, u, :], start=True, stop=True)
                    pe.matmul(in_ps[:, 3, 0:VW], src[:, u, :], m["mat"][f"{name}_v"][:, 0:VW], start=True, stop=True)\
                        .then_inc(kv_done, 1)

                def stack(b, u, which, half):
                    pe.wait_ge(klo if which else qlo, b + 1)
                    if which:
                        wait(pe, qall_ready, NH * b)
                        wait(pe, kst_ready, NH * b + half)
                    else:
                        pe.wait_ge(kst_ready, NH * (b + 1))
                        wait(pe, qall_ready, NH * b + half)
                    w = selk if which else selq
                    for blk in range(4):
                        c = 4 * half + blk
                        pe.matmul(stack_ps[:, blk, :], w[:, 0, c, :], hi[:, u, int(which), :], start=True, stop=False)
                        last = pe.matmul(stack_ps[:, blk, :], w[:, 1, c, :], lo[:, u, int(which), :], start=False, stop=True)
                    last.then_inc(kstack if which else qstack, 1)

                def heads(j):
                    return (j % 4, 4 * (j // 4)) if nblk == 4 else (j // 2, 4 * (j % 2))

                def head(g, blk):
                    return 4 * blk + g

                def scores(b, u, j):
                    n = NQ * b + j
                    if j == 0:
                        pe.wait_ge(kst_ready, NH * (b + 1))
                        if masked:
                            pe.wait_ge(nbk_ready, 2 * (b + 1))
                    g, b0 = heads(j)
                    pe.wait_ge(qst_ready, 4 * b + g + 1 if NH == 1 else 8 * b + 4 * (b0 // 4) + g + 1)
                    wait(pe, mx_ready, n - 1)
                    if masked:
                        for i in range(4):
                            pe.matmul(s_ps[:, j % 2, i, :], m["identb"][:], nbq[:, u, :], start=(i == 0), stop=False,
                                      skip_group_check=True)
                    for i in range(4):
                        last = pe.matmul(s_ps[:, j % 2, i, :], qst[:, u, g, b0 + i, :], kst[:, u, b0 + i, :],
                                         start=not masked, stop=True, skip_group_check=masked)
                    last.then_inc(s_done, 1)

                def scores_by_key(b, u, j):
                    n = NQ * b + j
                    pe.wait_ge(mx_ready, n + 1)
                    wait(pe, pr_ready, n - 1)
                    g, b0 = heads(j)
                    for i in range(4):
                        pe.matmul(st_ps[:, j % 2, i, :], mx[:, j % 2, i:i + 1].broadcast_to([P, P]), m["negident"][:],
                                  start=(i == 0), stop=False, skip_group_check=True)
                        if masked:
                            pe.matmul(st_ps[:, j % 2, i, :], m["identb"][:], nbk[:, u, :], start=False, stop=False,
                                      skip_group_check=True)
                    for i in range(4):
                        last = pe.matmul(st_ps[:, j % 2, i, :], kst[:, u, b0 + i, :], qst[:, u, g, b0 + i, :],
                                         start=False, stop=True, skip_group_check=True)
                    last.then_inc(st_done, 1)

                def values(b, u, j):
                    n = NQ * b + j
                    if j == 0:
                        pe.wait_ge(vlo_ready, b + 1)
                        wait(pe, on_done, b)
                    pe.wait_ge(phi_ready, n + 1)
                    pe.wait_ge(plo_ready[j], b + 1)
                    g, b0 = heads(j)
                    for i in range(4):
                        h = head(g, b0 + i)
                        v = h // 2 if differs else h
                        pe.matmul(o_h[:, h, :], phi[:, j % 4, i, :], vhi[:, u, v, :], start=True, stop=False,
                                  skip_group_check=True)
                        pe.matmul(o_h[:, h, 0:vd], phi[:, j % 4, i, :], vlo[:, u, v, :], start=False, stop=False,
                                  skip_group_check=True)
                        last = pe.matmul(o_h[:, h, :], plo[:, j % 4, i, :], vhi[:, u, v, :], start=False, stop=True,
                                         skip_group_check=True)
                    last.then_inc(pv_done, 1)

                def o_turn(b, u):
                    pe.wait_ge(on_done, b + 1)
                    wait(pe, lg_ready if own else x_done, b)
                    pe.transpose(out_ps[:, 0, :], on[:, u, :], m["mat"]["ident"]).then_inc(oT_done, 1)

                def project(b, u):
                    pe.wait_ge(oT_ready, b + 1)
                    if own:
                        pe.matmul(out_ps[:, 1, :], m["mat"]["a1_o"][0:VW, :], oT[0:VW, u, :], start=True, stop=True)\
                            .then_inc(y_done, 1)
                    else:
                        pe.matmul(out_ps[:, 1, :], oT[:, u, :], m["mat"][f"{name}_o"], start=True, stop=True).then_inc(y_done, 1)

                def route(b, u):
                    pe.wait_ge(mT_ready, b + 1)
                    pe.matmul(out_ps[:, 2, 0:E], mT[:, u, :], m["router_w"][:], start=True, stop=True).then_inc(lg_done, 1)

                x_turn(0, 0)
                dense(0, 0)
                for which in (True, False):
                    for half in range(NH):
                        stack(0, 0, which, half)
                x_turn(1, 1)
                dense(1, 1)
                scores(0, 0, 0)

                def step(b, u, last=None):
                    for j in range(NQ):
                        if j < NQ - 1:
                            scores(b, u, j + 1)
                        elif there(b, 1):
                            scores(b + 1, 1 - u, 0)
                        if there(b, -1) and j == 3:
                            project(b - 1, 1 - u)
                        scores_by_key(b, u, j)
                        if there(b, -1) and j == 2:
                            o_turn(b - 1, 1 - u)
                        if j > 1:
                            values(b, u, j - 2)
                        elif there(b, -1):
                            values(b - 1, 1 - u, NQ - 2 + j)
                        if own and there(b, -1) and j == 3:
                            route(b - 1, 1 - u)
                        if there(b, 1) and j < 2 * NH:
                            stack(b + 1, 1 - u, j < NH, j % NH)
                        if there(b, 2) and j == NQ - 2:
                            x_turn(b + 2, u)
                        if there(b, 2) and j == NQ - 1:
                            dense(b + 2, u)

                over_batches(pe, step)
                values(B - 1, 1, NQ - 2)
                values(B - 1, 1, NQ - 1)
                o_turn(B - 1, 1)
                project(B - 1, 1)
                if own:
                    route(B - 1, 1)

        sem.clear()


LN_STEPS = 7


def layernorm_stats(nc, dve, m, lnv, rstd, nmr, steps, ln_ready, pow_ready):
    st = m["stats"]
    c = Chain(dve, steps)
    c(dve.tensor_tensor(lnv[:, 0, :], st[:, :, 1], st[:, :, 4], ALU.add))
    c(dve.tensor_tensor(lnv[:, 1, :], st[:, :, 1], st[:, :, 4], ALU.subtract))
    c(dve.tensor_tensor(lnv[:, 2, :], st[:, :, 2], st[:, :, 5], ALU.add))
    c(dve.tensor_tensor(lnv[:, 3, :], lnv[:, 1, :], lnv[:, 1, :], ALU.mult))
    c(dve.tensor_scalar(lnv[:, 2, :], lnv[:, 2, :], 1.0 / D, EPS, ALU.mult, ALU.add))
    c(dve.scalar_tensor_tensor(lnv[:, 4, :], lnv[:, 3, :], 0.25, lnv[:, 2, :], ALU.mult, ALU.add))
    dve.sem_inc(ln_ready, 1)
    dve.wait_ge(pow_ready, 1)
    c(dve.scalar_tensor_tensor(nmr[:], lnv[:, 0, :], -0.5, rstd[:], ALU.mult, ALU.mult))


def recurrence(nc, m):
    T = P
    C = 16
    with ExitStack() as ctx:
        def sb(n, shape, dt=F32):
            return ctx.enter_context(nc.sbuf_tensor(f"r_{n}", shape, dt))

        def ps(n, shape):
            return ctx.enter_context(nc.psum_tensor(f"r_{n}", shape, F32))

        sem = Semaphores(nc, ctx, "r")

        inp, gate, rest = (m["pool"][:, i].rearrange("p (t b) -> p t b", b=B) for i in range(3))
        state = m["big"][:].rearrange("p b t -> p (b t)").rearrange("p (t b) -> p t b", b=B)
        G = 4
        xn = sb("xn", [P, 2, G, D])
        kv = sb("kv", [P, 2, G, T])
        r = sb("r", [P, 2, G, T])
        ret = sb("ret", [P, 2, G, T])
        gi = sb("gi", [P, 2, G, T])
        ms = sb("ms", [P, 2, B])
        sT = sb("sT", [P, 2, G, T])
        lnv, rstd, nmr = sb("lnv", [P, 6, B]), sb("rstd", [P, B]), sb("nmr", [P, B])
        xT_ps, in_ps, g_ps = ps("xT_ps", [P, 2, G, T]), ps("in_ps", [P, G, T]), ps("g_ps", [P, G, T])
        z_ps = ps("z_ps", [P, 2, C, B])
        y_ps = xT_ps

        half_set, ln_ready, pow_ready, steps = sem("half_set"), sem("ln_ready"), sem("pow_ready"), sem("steps")
        xn_ready, xT_done, kv_ready, r_ready, ret_ready = (sem("xn_ready"), sem("xT_done"), sem("kv_ready"),
                                                           sem("r_ready"), sem("ret_ready"))
        in_done, in_ready, g_done, gate_ready, gi_ready, rest_ready = (
            sem("in_done"), sem("in_ready"), sem("g_done"), sem("gate_ready"), sem("gi_ready"), sem("rest_ready"))
        ms_ready, z_done, s_ready = sem("ms_ready"), sem("z_done"), sem("s_ready")
        sT_ready, xb_ready, y_done, x_done = sem("sT_ready"), sem("xb_ready"), sem("y_done"), sem("x_done")
        NG = B // G

        def cols(t, g):
            return t[:, :, bass.ds(G * g, G)].rearrange("p t b -> p b t")

        with nc.Block() as block:

            @block.gpsimd
            def _(pool):
                pool.memset(lnv[:, 5, :], -0.5).then_inc(half_set, 1)
                pool.wait_ge(half_set, 1)
                pool.wait_ge(ln_ready, 1)
                nc.gpsimd.tensor_tensor(rstd[:], lnv[:, 4, :], lnv[:, 5, :], ALU.pow).then_inc(pow_ready, 1)

                def square(g, u):
                    wait(pool, r_ready, G * (g - 1))
                    c = m["ctxT"][:, bass.ds(G * g, G), :]
                    nc.gpsimd.tensor_tensor(kv[:, u], c, c, ALU.mult).then_inc(kv_ready, 1)

                square(0, 0)
                square(1, 1)

                def step(g, u, last=None):
                    if not (isinstance(g, int) and g + 2 >= NG):
                        square(g + 2, u)
                    pool.wait_ge(gate_ready, g + 1)
                    wait(pool, rest_ready, g - 1)
                    nc.gpsimd.tensor_tensor(gi[:, u], cols(gate, g), cols(inp, g), ALU.mult).then_inc(gi_ready, 1)

                over_batches(pool, step, NG)

            @block.vector
            def _(dve):
                layernorm_stats(nc, dve, m, lnv, rstd, nmr, steps, ln_ready, pow_ready)

                def normalise(g, u):
                    wait(dve, xT_done, g - 1)
                    for i in range(G):
                        last = dve.tensor_scalar(xn[:, u, i, :], m["x"][:, G * g + i, :], rstd[:, bass.ds(G * g + i, 1)],
                                                 nmr[:, bass.ds(G * g + i, 1)], ALU.mult, ALU.add)
                    last.then_inc(xn_ready, 1)

                def rest_of(g, u):
                    dve.wait_ge(gi_ready, g + 1)
                    dve.tensor_tensor(cols(rest, g), cols(inp, g), gi[:, u], ALU.subtract).then_inc(rest_ready, 1)

                normalise(0, 0)
                normalise(1, 1)

                def step(g, u, last=None):
                    dve.wait_ge(kv_ready, g + 1)
                    for i in range(G):
                        dve.tensor_tensor_scan(r[:, u, i, :], m["col"]["decay"].broadcast_to([P, T]), kv[:, u, i, :],
                                               0.0, ALU.mult, ALU.add).then_inc(r_ready, 1)
                    dve.wait_ge(r_ready, G * (g + 1))
                    dve.wait_ge(xT_done, g + 1)
                    wait(dve, in_done, g - 1)
                    dve.tensor_tensor(ret[:, u], xT_ps[:, u], r[:, u], ALU.mult).then_inc(ret_ready, 1)
                    if not (isinstance(g, int) and g + 2 >= NG):
                        normalise(g + 2, u)
                    if not (isinstance(g, int) and g < 2):
                        rest_of(g - 2, u)

                over_batches(dve, step, NG)
                rest_of(NG - 2, 0)
                rest_of(NG - 1, 1)

            @block.tensor
            def _(pe):
                def turn(g, u):
                    pe.wait_ge(xn_ready, g + 1)
                    wait(pe, ret_ready, g - 1)
                    for i in range(G):
                        last = pe.transpose(xT_ps[:, u, i, :], xn[:, u, i, :], m["mat"]["ident"])
                    last.then_inc(xT_done, 1)

                pe.wait_ge(m["weights_in"], m["weights_count"])
                def project(g, u):
                    pe.wait_ge(ret_ready, g + 1)
                    wait(pe, in_ready, g)
                    pe.matmul(in_ps[:], m["mat"]["r_wi"], ret[:, u], start=True, stop=True).then_inc(in_done, 1)

                turn(0, 0)
                turn(1, 1)
                project(0, 0)

                def step(g, u, last=None):
                    if not (isinstance(g, int) and g == last):
                        project(g + 1, 1 - u)
                    if not (isinstance(g, int) and g + 2 >= NG):
                        turn(g + 2, u)
                    pe.wait_ge(in_ready, g + 1)
                    wait(pe, gate_ready, g)
                    pe.matmul(g_ps[:], m["mat"]["r_wg"], cols(inp, g), start=True, stop=True).then_inc(g_done, 1)

                over_batches(pe, step, NG)

            @block.scalar
            def _(act):
                act.preload_act_table(ACT.Sigmoid)

                def keep(g):
                    act.wait_ge(in_done, g + 1)
                    act.activation(cols(inp, g), in_ps[:], ACT.Identity, bias=m["col"]["r_bi"]).then_inc(in_ready, 1)

                keep(0)

                def step(g, u, last=None):
                    if not (isinstance(g, int) and g == last):
                        keep(g + 1)
                    act.wait_ge(g_done, g + 1)
                    act.activation(cols(gate, g), g_ps[:], ACT.Sigmoid, bias=m["col"]["r_bg"]).then_inc(gate_ready, 1)

                over_batches(act, step, NG)

        def over_chunks(eng, chunk):
            with eng.Fori(0, T // C // 2 - 1) as i:
                for v in range(2):
                    chunk(2 * i + v, v)
            chunk(T // C - 2, 0)
            chunk(T // C - 1, 1)

        with nc.Block() as block:

            @block.tensor
            def _(pe):
                def inputs(c, v, k):
                    z = z_ps[:, v, 4 * k:4 * k + 4, :]
                    pe.matmul(z, m["mat"]["r_bm"], inp[:, bass.ds(C * c + 4 * k, 4), :], start=(k == 0), stop=False,
                              skip_group_check=True)
                    pe.matmul(z, m["mat"]["r_a"], rest[:, bass.ds(C * c + 4 * k, 4), :], start=False, stop=False,
                              skip_group_check=True)

                for k in range(C // 4):
                    inputs(0, 0, k)

                def chunk(c, v):
                    for j in range(C):
                        t = C * c + j
                        pe.wait_ge(ms_ready, t + 1)
                        pe.matmul(z_ps[:, v, j, :], m["mat"]["r_a"], ms[:, j % 2, :], start=False, stop=True,
                                  skip_group_check=True).then_inc(z_done, 1)
                        if j >= 2 and j % 2 == 0 and j // 2 <= C // 4 and not (isinstance(c, int) and c == T // C - 1):
                            inputs(c + 1, 1 - v, j // 2 - 1)

                over_chunks(pe, chunk)

            @block.scalar
            def _(act):
                act.preload_act_table(ACT.Tanh)

                def chunk(c, v):
                    for j in range(C):
                        t = C * c + j
                        act.wait_ge(z_done, t + 1)
                        act.activation(state[:, t, :], z_ps[:, v, j, :], ACT.Tanh).then_inc(s_ready, 1)

                over_chunks(act, chunk)

            @block.vector
            def _(dve):
                dve.memset(ms[:, 0, :], 0.0).then_inc(ms_ready, 1)

                def chunk(c, v):
                    for j in range(C):
                        t = C * c + j
                        if isinstance(t, int) and t == T - 1:
                            return
                        dve.wait_ge(s_ready, t + 1)
                        dve.tensor_tensor(ms[:, (j + 1) % 2, :], gate[:, t + 1, :], state[:, t, :], ALU.mult)\
                            .then_inc(ms_ready, 1)

                over_chunks(dve, chunk)

        with nc.Block() as block:

            @block.gpsimd
            def _(pool):
                def step(g, u, last=None):
                    x = m["x"][:, bass.ds(G * g, G), :]
                    bo = m["row"]["r_bo"].unsqueeze(1).broadcast_to([P, G, D])
                    nc.gpsimd.tensor_tensor(x, x, bo, ALU.add).then_inc(xb_ready, 1)

                over_batches(pool, step, NG)

            @block.scalar
            def _(act):
                def step(g, u, last=None):
                    wait(act, y_done, g - 1)
                    act.activation(sT[:, u], cols(state, g), ACT.Copy).then_inc(sT_ready, 1)

                over_batches(act, step, NG)

            @block.tensor
            def _(pe):
                def step(g, u, last=None):
                    pe.wait_ge(sT_ready, g + 1)
                    wait(pe, x_done, g - 1)
                    for i in range(G):
                        last_op = pe.matmul(y_ps[:, u, i, :], sT[:, u, i, :], m["mat"]["r_wo"], start=True, stop=True)
                    last_op.then_inc(y_done, 1)

                over_batches(pe, step, NG)

            @block.vector
            def _(dve):
                def step(g, u, last=None):
                    dve.wait_ge(y_done, g + 1)
                    dve.wait_ge(xb_ready, g + 1)
                    x = m["x"][:, bass.ds(G * g, G), :]
                    dve.tensor_tensor(x, x, y_ps[:, u], ALU.add).then_inc(x_done, 1)
                    dve.wait_ge(x_done, g + 1)
                    for i in range(G):
                        dve.bn_stats(m["stats"][:, G * g + i, :], m["x"][:, G * g + i, :])

                over_batches(dve, step, NG)

        sem.clear()


def softmax_experts(nc, dve, act_ready, exp_ready, c, lg, tmp, rows):
    n = lg.shape[1]
    wide = [rows, n, E]
    c(dve.tensor_reduce(tmp, lg, AX.X, ALU.max))
    c(dve.tensor_tensor(lg, lg, tmp.unsqueeze(2).broadcast_to(wide), ALU.subtract))
    dve.sem_inc(act_ready, 1)
    dve.wait_ge(exp_ready, 1)
    c(dve.tensor_reduce(tmp, lg, AX.X, ALU.add))
    c(dve.reciprocal(tmp, tmp))
    c(dve.tensor_tensor(lg, lg, tmp.unsqueeze(2).broadcast_to(wide), ALU.mult))


def top_two_mixture(nc, m):
    G = 4
    NG = B // G
    F = 2
    WS = 64.0
    with ExitStack() as ctx:
        def sb(n, shape, dt=F32):
            return ctx.enter_context(nc.sbuf_tensor(f"m_{n}", shape, dt))

        def ps(n, shape):
            return ctx.enter_context(nc.psum_tensor(f"m_{n}", shape, F32))

        sem = Semaphores(nc, ctx, "m")

        lg = m["logits"]
        wgt = sb("wgt", [P, B, E])
        pick = sb("pick", [P, B, E])
        left = sb("left", [P, B, E])
        t1, t2, t3 = sb("t1", [P, B]), sb("t2", [P, B]), sb("t3", [P, B])
        wT = sb("wT", [P, 2, P])
        wgt_s = sb("wgt_s", [P, B, E])
        h = sb("h", [P, 2, F, G * P])
        h_hi, h_lo = sb("h_hi", [P, 4, F, G * P], F16), sb("h_lo", [P, 4, F, G * P], F16)
        w1, w1_hi, w1_lo = m["m_w1"], m["m_w1_parts"][:, 0], m["m_w1_parts"][:, 1]
        w2, w2_hi, w2_lo = m["m_w2"], m["m_w2_parts"][:, 0], m["m_w2_parts"][:, 1]
        turn_ps = ps("turn_ps", [P, 512])
        h_ps, z_ps = ps("h_ps", [P, 2, G * P]), ps("z_ps", [P, 2, G, D])
        b_ps = ps("b_ps", [P, 2, 512])
        steps, act_ready, exp_ready, w_ready, wT_done, wT_ready = (sem("steps"), sem("act_ready"), sem("exp_ready"),
                                                                   sem("w_ready"), sem("wT_done"), sem("wT_ready"))
        b_done, b_added, h_done, h_ready, z_done, z_added = (
            sem("b_done"), sem("b_added"), sem("h_done"), sem("h_ready"), sem("z_done"), sem("z_added"))
        parts_high, hhi_ready, hlo_ready = sem("parts_high"), sem("hhi_ready"), sem("hlo_ready")

        with nc.Block() as block:

            @block.scalar
            def _(act):
                act.wait_ge(act_ready, 1)
                act.activation(lg[:], lg[:], ACT.Exp).then_inc(exp_ready, 1)
                act.wait_ge(m["m_in"], 48)
                act.activation(w1_hi, w1, ACT.Copy, scale=WS).then_inc(parts_high, 1)
                act.activation(w2_hi, w2, ACT.Copy, scale=WS).then_inc(parts_high, 1)

            @block.vector
            def _(dve):
                c = Chain(dve, steps)
                softmax_experts(nc, dve, act_ready, exp_ready, c, lg[:], t1[:], P)
                wide = [P, B, E]

                def choose(src, top):
                    c(dve.tensor_reduce(top[:], src[:], AX.X, ALU.max))
                    c(dve.tensor_tensor(pick[:], src[:], top[:].unsqueeze(2).broadcast_to(wide), ALU.is_equal))
                    c(dve.tensor_tensor(pick[:], pick[:], m["down"][:].unsqueeze(1).broadcast_to(wide), ALU.mult))
                    c(dve.tensor_reduce(t3[:], pick[:], AX.X, ALU.max))
                    c(dve.tensor_tensor(pick[:], pick[:], t3[:].unsqueeze(2).broadcast_to(wide), ALU.is_equal))

                choose(lg, t1)
                c(dve.tensor_tensor(wgt[:], pick[:], t1[:].unsqueeze(2).broadcast_to(wide), ALU.mult))
                c(dve.scalar_tensor_tensor(left[:].rearrange("p b e -> p (b e)"), pick[:].rearrange("p b e -> p (b e)"), -4.0,
                                           lg[:].rearrange("p b e -> p (b e)"), ALU.mult, ALU.add))
                choose(left, t2)
                c(dve.tensor_tensor(pick[:], pick[:], t2[:].unsqueeze(2).broadcast_to(wide), ALU.mult))
                c(dve.tensor_tensor(wgt[:], wgt[:], pick[:], ALU.add))
                c(dve.tensor_tensor(t1[:], t1[:], t2[:], ALU.add))
                c(dve.tensor_scalar(t1[:], t1[:], 1e-8, None, ALU.add))
                c(dve.reciprocal(t1[:], t1[:]))
                c(dve.tensor_scalar(t1[:], t1[:], 0.3, None, ALU.mult))
                dve.tensor_tensor(wgt[:], wgt[:], t1[:].unsqueeze(2).broadcast_to(wide), ALU.mult).then_inc(w_ready, 1)
                dve.wait_ge(w_ready, 1)
                dve.tensor_scalar(wgt_s[:], wgt[:], 1.0 / WS, None, ALU.mult)
                dve.wait_ge(parts_high, 2)
                dve.scalar_tensor_tensor(w1_lo, w1, WS, w1_hi, ALU.mult, ALU.subtract)
                dve.scalar_tensor_tensor(w2_lo, w2, WS, w2_hi, ALU.mult, ALU.subtract)
                dve.wait_ge(wT_done, 1)
                dve.tensor_copy(wT[:], turn_ps[:, 0:2 * P].rearrange("p (h t) -> p h t", h=2)).then_inc(wT_ready, 1)

            @block.tensor
            def _(pe):
                pe.wait_ge(w_ready, 1)
                for half in range(2):
                    last = pe.transpose(turn_ps[:, half * P:(half + 1) * P],
                                        wgt[:, 16 * half:16 * half + 16, :].rearrange("p b e -> p (b e)"), m["mat"]["ident"])
                last.then_inc(wT_done, 1)

        with nc.Block() as block:

            @block.tensor
            def _(pe):
                pe.wait_ge(m["m_in"], 48)
                for half in range(2):
                    def bias(b, u, last=None):
                        wait(pe, b_added, b + 16 * half - 1)
                        pe.matmul(b_ps[:, u, 0:D], wT[:, half, :], m["m_b2"][:, b, :], start=True, stop=True)\
                            .then_inc(b_done, 1)

                    over_batches(pe, bias, 16)

                def up(g, e):
                    n = E * g + e
                    y_hi, y_lo = (m["y_parts"][:, i, bass.ds(G * g, G), :] for i in range(2))
                    for f in range(F):
                        w = slice(f * P, (f + 1) * P)
                        wait(pe, h_ready, F * (n - 1) + f + 1)
                        pe.matmul(h_ps[:, f, :], w1_hi[:, e, w], y_hi, start=True, stop=False)
                        pe.matmul(h_ps[:, f, :], w1_hi[:, e, w], y_lo, start=False, stop=False)
                        pe.matmul(h_ps[:, f, :], w1_lo[:, e, w], y_hi, start=False, stop=True).then_inc(h_done, 1)

                def down(g, e):
                    n = E * g + e
                    pe.wait_ge(hhi_ready, F * (n + 1))
                    pe.wait_ge(hlo_ready, F * (n + 1))
                    wait(pe, z_added, n - 1)
                    for i in range(G):
                        t = slice(i * P, (i + 1) * P)
                        for f in range(F):
                            pe.matmul(z_ps[:, e % 2, i, :], h_hi[:, e % 4, f, t], w2_hi[:, e, f, :], start=(f == 0), stop=False)
                            pe.matmul(z_ps[:, e % 2, i, :], h_hi[:, e % 4, f, t], w2_lo[:, e, f, :], start=False, stop=False)
                            last = pe.matmul(z_ps[:, e % 2, i, :], h_lo[:, e % 4, f, t], w2_hi[:, e, f, :], start=False,
                                             stop=(f == F - 1))
                    last.then_inc(z_done, 1)

                def group(g, u, last=None):
                    for e in range(E):
                        up(g, e)
                        if e >= 2:
                            down(g, e - 2)
                        elif not (isinstance(g, int) and g == 0):
                            down(g - 1, E - 2 + e)

                over_batches(pe, group, NG)
                down(NG - 1, E - 2)
                down(NG - 1, E - 1)

            @block.scalar
            def _(act):
                act.preload_act_table(ACT.Gelu)

                def group(g, u, last=None):
                    for e in range(E):
                        n = E * g + e
                        for f in range(F):
                            act.wait_ge(h_done, F * n + f + 1)
                            wait(act, hlo_ready, F * (n - 2) + f + 1)
                            act.activation(h[:, e % 2, f, :], h_ps[:, f, :], ACT.Gelu, scale=1.0 / WS,
                                           bias=m["col"][f"m_b1_{F * e + f}"]).then_inc(h_ready, 1)
                        wait(act, z_done, n - 3)
                        for f in range(F):
                            act.wait_ge(h_ready, F * n + f + 1)
                            act.activation(h_hi[:, e % 4, f, :], h[:, e % 2, f, :], ACT.Copy).then_inc(hhi_ready, 1)

                over_batches(act, group, NG)

            @block.gpsimd
            def _(pool):
                def group(g, u, last=None):
                    for e in range(E):
                        n = E * g + e
                        wait(pool, z_done, n - 3)
                        for f in range(F):
                            pool.wait_ge(hhi_ready, F * n + f + 1)
                            nc.gpsimd.tensor_tensor(h_lo[:, e % 4, f, :], h[:, e % 2, f, :], h_hi[:, e % 4, f, :],
                                                    ALU.subtract).then_inc(hlo_ready, 1)

                over_batches(pool, group, NG)

            @block.vector
            def _(dve):
                for half in range(2):
                    def bias(b, u, last=None):
                        dve.wait_ge(b_done, b + 16 * half + 1)
                        x = m["x"][:, b + 16 * half, :]
                        dve.tensor_tensor(x, x, b_ps[:, u, 0:D], ALU.add).then_inc(b_added, 1)

                    over_batches(dve, bias, 16)
                dve.wait_ge(b_added, B)

                def group(g, u, last=None):
                    for e in range(E):
                        n = E * g + e
                        dve.wait_ge(z_done, n + 1)
                        wait(dve, z_added, n)
                        for i in range(G):
                            x = m["x"][:, G * g + i, :]
                            w = wgt_s[:, G * g + i, e:e + 1]
                            last_op = dve.scalar_tensor_tensor(x, z_ps[:, e % 2, i, :], w, x, ALU.mult, ALU.add)
                        last_op.then_inc(z_added, 1)
                    dve.wait_ge(z_added, E * (g + 1))
                    for i in range(G):
                        dve.bn_stats(m["stats"][:, G * g + i, :], m["x"][:, G * g + i, :])

                over_batches(dve, group, NG)

        sem.clear()




def expert_choice(nc, m):
    G, NG, K, F = 4, 8, 32, 4
    WS = 256.0
    with ExitStack() as ctx:
        def sb(n, shape, dt=F32):
            return ctx.enter_context(nc.sbuf_tensor(f"e_{n}", shape, dt))

        sem = Semaphores(nc, ctx, "e")

        lg = m["logits"]
        w1_hi, w1_lo = (m["split_a"][:, i].rearrange("p (e f) -> p e f", e=E) for i in range(2))
        w2_hi, w2_lo = (m["split_b"][:, i].rearrange("p (e c d) -> p e c d", e=E, c=F) for i in range(2))
        lnv, rstd, nmr = sb("lnv", [P, 6, B]), sb("rstd", [P, B]), sb("nmr", [P, B])
        xn = sb("xn", [P, 2, G, D])
        rank = sb("rank", [P, B, E])
        half_set, ln_ready, pow_ready, steps = sem("half_set"), sem("ln_ready"), sem("pow_ready"), sem("steps")

        with ExitStack() as inner:
            xnT = inner.enter_context(nc.sbuf_tensor("e_xnT", [P, 2, G, P], F32))
            xT_ps = inner.enter_context(nc.psum_tensor("e_xT_ps", [P, 2, G, P], F32))
            lg_ps = inner.enter_context(nc.psum_tensor("e_lg_ps", [P, 2, 512], F32))
            xn_ready, xT_done, xnT_ready, lg_done, lg_ready = (sem("r_xn_ready"), sem("r_xT_done"), sem("r_xnT_ready"),
                                                               sem("r_lg_done"), sem("r_lg_ready"))
            a_high, a_low, b_high = sem("a_high"), sem("a_low"), sem("b_high")
            with nc.Block() as block:

                @block.gpsimd
                def _(pool):
                    pool.memset(lnv[:, 5, :], -0.5).then_inc(half_set, 1)
                    pool.wait_ge(half_set, 1)
                    pool.wait_ge(ln_ready, 1)
                    nc.gpsimd.tensor_tensor(rstd[:], lnv[:, 4, :], lnv[:, 5, :], ALU.pow).then_inc(pow_ready, 1)

                @block.vector
                def _(dve):
                    layernorm_stats(nc, dve, m, lnv, rstd, nmr, steps, ln_ready, pow_ready)

                    def normalise(g, u):
                        wait(dve, xT_done, g - 1)
                        for i in range(G):
                            last = dve.tensor_scalar(xn[:, u, i, :], m["x"][:, G * g + i, :], rstd[:, bass.ds(G * g + i, 1)],
                                                     nmr[:, bass.ds(G * g + i, 1)], ALU.mult, ALU.add)
                        last.then_inc(xn_ready, 1)

                    normalise(0, 0)

                    def step(g, u, last=None):
                        if not (isinstance(g, int) and g == last):
                            normalise(g + 1, 1 - u)
                        dve.wait_ge(lg_done, g + 1)
                        dve.tensor_copy(lg[:, bass.ds(G * g, G), :], lg_ps[:, u, 0:G * E].rearrange("p (i e) -> p i e", e=E))\
                            .then_inc(lg_ready, 1)

                    over_batches(dve, step, NG)
                    dve.wait_ge(a_high, 1)
                    dve.scalar_tensor_tensor(w1_lo, m["e_w1"], WS, w1_hi, ALU.mult, ALU.subtract).then_inc(a_low, 1)
                    dve.wait_ge(b_high, 1)
                    dve.scalar_tensor_tensor(w2_lo, m["e_w2"], WS, w2_hi, ALU.mult, ALU.subtract)

                @block.scalar
                def _(act):
                    def step(g, u, last=None):
                        act.wait_ge(xT_done, g + 1)
                        wait(act, lg_done, g - 1)
                        act.activation(xnT[:, u], xT_ps[:, u], ACT.Copy).then_inc(xnT_ready, 1)

                    over_batches(act, step, NG)
                    act.wait_ge(m["weights_in"], m["weights_count"])
                    act.activation(w1_hi, m["e_w1"], ACT.Copy, scale=WS).then_inc(a_high, 1)
                    act.wait_ge(a_low, 1)
                    act.activation(w2_hi, m["e_w2"], ACT.Copy, scale=WS).then_inc(b_high, 1)

                @block.tensor
                def _(pe):
                    def turn(g, u):
                        pe.wait_ge(xn_ready, g + 1)
                        wait(pe, xnT_ready, g - 1)
                        for i in range(G):
                            last = pe.transpose(xT_ps[:, u, i, :], xn[:, u, i, :], m["mat"]["ident"])
                        last.then_inc(xT_done, 1)

                    turn(0, 0)

                    def step(g, u, last=None):
                        if not (isinstance(g, int) and g == last):
                            turn(g + 1, 1 - u)
                        pe.wait_ge(xnT_ready, g + 1)
                        wait(pe, lg_ready, g - 1)
                        for i in range(G):
                            last_op = pe.matmul(lg_ps[:, u, E * i:E * i + E], xnT[:, u, i, :], m["gate_w"][:], start=True, stop=True)
                        last_op.then_inc(lg_done, 1)

                    over_batches(pe, step, NG)

        with ExitStack() as inner:
            def ib(n, shape):
                return inner.enter_context(nc.sbuf_tensor(f"e_{n}", shape, F32))

            t1 = ib("t1", [P, B])
            pT, left, took = ib("pT", [P, 2, P]), ib("left", [P, 2, P]), ib("took", [P, 2, P])
            top = ib("top", [P, 2, 8])
            tk = ib("tk", [P, 2, P])
            pT_ps = inner.enter_context(nc.psum_tensor("e_pT_ps", [P, 512], F32))
            tk_ps = inner.enter_context(nc.psum_tensor("e_tk_ps", [P, 512], F32))
            rk_ps = inner.enter_context(nc.psum_tensor("e_rk_ps", [P, 512], F32))
            c_steps, act_ready, exp_ready, p_ready = sem("c_steps"), sem("act_ready"), sem("exp_ready"), sem("p_ready")
            pT_done, took_ready, tk_done, tk_ready, rk_done = (sem("pT_done"), sem("took_ready"), sem("tk_done"),
                                                               sem("tk_ready"), sem("rk_done"))
            with nc.Block() as block:

                @block.scalar
                def _(act):
                    act.wait_ge(act_ready, 1)
                    act.activation(lg[:], lg[:], ACT.Exp).then_inc(exp_ready, 1)

                @block.vector
                def _(dve):
                    c = Chain(dve, c_steps)
                    softmax_experts(nc, dve, act_ready, exp_ready, c, lg[:], t1[:], P)
                    dve.sem_inc(p_ready, 1)
                    dve.wait_ge(pT_done, 1)
                    c(dve.tensor_copy(pT[:], pT_ps[:, 0:2 * P].rearrange("p (h t) -> p h t", h=2)))
                    src = pT
                    for _ in range(K // 8):
                        for half in range(2):
                            c(dve.max(top[:, half, :], src[:, half, :]))
                            c(dve.match_replace(left[:, half, :], top[:, half, :], src[:, half, :], -1.0))
                        src = left
                    dve.tensor_scalar(took[:], left[:], 0.0, None, ALU.is_lt).then_inc(took_ready, 1)
                    dve.wait_ge(tk_done, 1)
                    dve.tensor_copy(tk[:], tk_ps[:, 0:2 * P].rearrange("p (h t) -> p h t", h=2)).then_inc(tk_ready, 1)
                    dve.wait_ge(rk_done, 1)
                    dve.tensor_tensor(rank[:].rearrange("p b e -> p (b e)"), rk_ps[:, 0:2 * P],
                                      tk[:].rearrange("p h t -> p (h t)"), ALU.mult)

                @block.tensor
                def _(pe):
                    pe.wait_ge(p_ready, 1)
                    for half in range(2):
                        last = pe.transpose(pT_ps[:, half * P:(half + 1) * P],
                                            lg[:, 16 * half:16 * half + 16, :].rearrange("p b e -> p (b e)"), m["mat"]["ident"])
                    last.then_inc(pT_done, 1)
                    pe.wait_ge(took_ready, 1)
                    for half in range(2):
                        last = pe.transpose(tk_ps[:, half * P:(half + 1) * P], took[:, half, :], m["mat"]["ident"])
                    last.then_inc(tk_done, 1)
                    pe.wait_ge(tk_ready, 1)
                    pe.matmul(rk_ps[:, 0:2 * P], m["mat"]["tri"], tk[:].rearrange("p h t -> p (h t)"), start=True, stop=True)\
                        .then_inc(rk_done, 1)

        oh = sb("oh", [P, 2, G, E, K])
        ohw = m["big"][:].rearrange("p b t -> p (b t)")[:, 0:2 * E * P].rearrange("p (u e i k) -> p u e i k", u=2, e=E, i=G)
        xe_hi, xe_lo = sb("xe_hi", [P, 2, E, G, K], F16), sb("xe_lo", [P, 2, E, G, K], F16)
        back = sb("back", [P, 2, E, P], F16)
        prob = sb("prob", [P, 2, E])
        h = sb("h", [P, 2, F, P])
        h_hi, h_lo = sb("h_hi", [P, 4, F, P], F16), sb("h_lo", [P, 4, F, P], F16)
        z_hi, z_lo = sb("z_hi", [P, 2, E, D], F16), sb("z_lo", [P, 2, E, D], F16)
        yb = sb("yb", [P, 2, D], BF16)
        g_ps = ctx.enter_context(nc.psum_tensor("e_g_ps", [P, 512], F32))
        h_ps = ctx.enter_context(nc.psum_tensor("e_h_ps", [P, 2, F, P], F32))
        z_ps = ctx.enter_context(nc.psum_tensor("e_z_ps", [P, 512], F32))
        y_ps = ctx.enter_context(nc.psum_tensor("e_y_ps", [P, G, 512], F32))
        xn_ready, oh_ready, ohw_ready = sem("xn_ready"), sem("oh_ready"), sem("ohw_ready")
        gx_done, xhi_ready, xlo_ready, gw_done = sem("gx_done"), sem("xhi_ready"), sem("xlo_ready"), sem("gw_done")
        back_ready, gw_ready, hhi_ready, hlo_ready, zhi_ready = (sem("back_ready"), sem("gw_ready"), sem("hhi_ready"),
                                                                 sem("hlo_ready"), sem("zhi_ready"))
        h_done, h_ready, z_done, z_ready, y_done, y_read, x_done = (
            sem("h_done"), sem("h_ready"), sem("z_done"), sem("z_ready"), sem("y_done"), sem("y_read"), sem("x_done"))

        with nc.Block() as block:

            @block.gpsimd
            def _(pool):
                def weigh(g, u, i):
                    wait(pool, gw_done, 2 * (g - 1))
                    pool.wait_ge(oh_ready, G * g + i + 1)
                    nc.gpsimd.tensor_tensor(ohw[:, u, :, i, :], oh[:, u, i],
                                            lg[:, G * g + i, :].unsqueeze(2).broadcast_to([P, E, K]), ALU.mult)\
                        .then_inc(ohw_ready, 1)

                def h_low(g, e):
                    n = E * g + e
                    pool.wait_ge(hhi_ready, n + 1)
                    wait(pool, z_done, n - 3)
                    nc.gpsimd.tensor_tensor(h_lo[:, e % 4], h[:, e % 2], h_hi[:, e % 4], ALU.subtract).then_inc(hlo_ready, 1)

                for i in range(G):
                    weigh(0, 0, i)

                def step(g, u, last=None):
                    for e in range(E):
                        h_low(g, e)
                        if e < G and not (isinstance(g, int) and g == last):
                            weigh(g + 1, 1 - u, e)

                over_batches(pool, step, NG)

            @block.vector
            def _(dve):
                def ready(g, u):
                    wait(dve, gx_done, 2 * (g - 1))
                    wait(dve, ohw_ready, G * (g - 1))
                    for i in range(G):
                        dve.tensor_scalar(xn[:, u, i, :], m["x"][:, G * g + i, :], rstd[:, bass.ds(G * g + i, 1)],
                                          nmr[:, bass.ds(G * g + i, 1)], ALU.mult, ALU.add).then_inc(xn_ready, 1)
                        dve.tensor_tensor(oh[:, u, i], m["iota"][:].unsqueeze(1).broadcast_to([P, E, K]),
                                          rank[:, G * g + i, :].unsqueeze(2).broadcast_to([P, E, K]), ALU.is_equal)\
                            .then_inc(oh_ready, 1)

                def x_low(g, u, half):
                    dve.wait_ge(xhi_ready, 2 * g + half + 1)
                    dve.tensor_tensor(xe_lo[:, u, :, 2 * half:2 * half + 2, :],
                                      g_ps[:].rearrange("p (i e k) -> p e i k", i=2, e=E),
                                      xe_hi[:, u, :, 2 * half:2 * half + 2, :], ALU.subtract).then_inc(xlo_ready, 1)

                def keep_weights(g, u, half):
                    w = g_ps[:].rearrange("p (e t) -> p e t", e=4)
                    dve.wait_ge(gw_done, 2 * g + half + 1)
                    wait(dve, y_done, g - 1)
                    dve.tensor_scalar(back[:, u, 4 * half:4 * half + 4, :], w, 0.0, None, ALU.is_gt).then_inc(back_ready, 1)
                    dve.tensor_reduce(prob[:, u, 4 * half:4 * half + 4], w, AX.X, ALU.max).then_inc(gw_ready, 1)

                def keep_z(g, u, e):
                    n = E * g + e
                    p = prob[:, u, e:e + 1]
                    dve.wait_ge(z_done, n + 1)
                    if e == 0:
                        dve.wait_ge(gw_ready, 2 * (g + 1))
                        wait(dve, y_done, g - 1)
                    dve.tensor_scalar(z_hi[:, u, e, :], z_ps[:, 0:D], p, None, ALU.mult).then_inc(zhi_ready, 1)
                    dve.wait_ge(zhi_ready, n + 1)
                    dve.scalar_tensor_tensor(z_lo[:, u, e, :], z_ps[:, 0:D], p, z_hi[:, u, e, :], ALU.mult, ALU.subtract)\
                        .then_inc(z_ready, 1)

                def finish(g, i):
                    if i == 0:
                        dve.wait_ge(y_done, g + 1)
                    wait(dve, x_done, G * g + i - 1)
                    dve.tensor_scalar(yb[:, i % 2, :], y_ps[:, i, 0:D], 1.0 / WS, None, ALU.mult).then_inc(y_read, 1)
                    dve.wait_ge(y_read, G * g + i + 1)
                    x = m["x"][:, G * g + i, :]
                    dve.tensor_tensor(x, x, yb[:, i % 2, :], ALU.add).then_inc(x_done, 1)

                def statistics(g):
                    dve.wait_ge(x_done, G * (g + 1))
                    for i in range(G):
                        dve.bn_stats(m["stats"][:, G * g + i, :], m["x"][:, G * g + i, :])

                ready(0, 0)
                for half in range(2):
                    x_low(0, 0, half)
                for half in range(2):
                    keep_weights(0, 0, half)

                def step(g, u, last=None):
                    more = not (isinstance(g, int) and g == last)
                    before = not (isinstance(g, int) and g == 0)
                    if before:
                        keep_z(g - 1, 1 - u, E - 2)
                    if more:
                        ready(g + 1, 1 - u)
                    if before:
                        keep_z(g - 1, 1 - u, E - 1)
                    for e in range(E - 2):
                        keep_z(g, u, e)
                        if more and e in (1, 2):
                            x_low(g + 1, 1 - u, e - 1)
                        if before and e >= 4:
                            for i in range(2):
                                finish(g - 1, 2 * (e - 4) + i)
                        if more and e in (3, 4):
                            keep_weights(g + 1, 1 - u, e - 3)
                    if before:
                        statistics(g - 1)

                over_batches(dve, step, NG)
                keep_z(NG - 1, 1, E - 2)
                keep_z(NG - 1, 1, E - 1)
                for i in range(G):
                    finish(NG - 1, i)
                statistics(NG - 1)

            @block.scalar
            def _(act):
                act.preload_act_table(ACT.Gelu_apprx_tanh)

                def keep_tokens(g, u, half):
                    act.wait_ge(gx_done, 2 * g + half + 1)
                    wait(act, h_done, E * (g - 1))
                    act.activation(xe_hi[:, u, :, 2 * half:2 * half + 2, :],
                                   g_ps[:].rearrange("p (i e k) -> p e i k", i=2, e=E), ACT.Copy).then_inc(xhi_ready, 1)

                for half in range(2):
                    keep_tokens(0, 0, half)

                def step(g, u, last=None):
                    for e in range(E):
                        n = E * g + e
                        act.wait_ge(h_done, n + 1)
                        wait(act, hlo_ready, n - 1)
                        act.activation(h[:, e % 2], h_ps[:, e % 2], ACT.Gelu_apprx_tanh, scale=1.0 / WS).then_inc(h_ready, 1)
                        act.wait_ge(h_ready, n + 1)
                        wait(act, z_done, n - 3)
                        act.activation(h_hi[:, e % 4], h[:, e % 2], ACT.Copy).then_inc(hhi_ready, 1)
                        if e in (3, 4) and not (isinstance(g, int) and g == last):
                            keep_tokens(g + 1, 1 - u, e - 3)

                over_batches(act, step, NG)

            @block.tensor
            def _(pe):
                def gather(g, u, half):
                    if half == 0:
                        wait(pe, gw_ready, 2 * g)
                    else:
                        pe.wait_ge(xlo_ready, 2 * g + 1)
                    for j in range(2):
                        i = 2 * half + j
                        pe.wait_ge(xn_ready, G * g + i + 1)
                        pe.wait_ge(oh_ready, G * g + i + 1)
                        last = pe.matmul(g_ps[:, j * 256:(j + 1) * 256], xn[:, u, i, :],
                                         oh[:, u, i].rearrange("p e k -> p (e k)"), start=True, stop=True)
                    last.then_inc(gx_done, 1)

                def turn_weights(g, u, half):
                    if half == 0:
                        pe.wait_ge(ohw_ready, G * (g + 1))
                        pe.wait_ge(xlo_ready, 2 * g + 2)
                    else:
                        pe.wait_ge(gw_ready, 2 * g + 1)
                    for j in range(4):
                        last = pe.transpose(g_ps[:, j * P:(j + 1) * P],
                                            ohw[:, u, 4 * half + j].rearrange("p i k -> p (i k)"), m["mat"]["ident"])
                    last.then_inc(gw_done, 1)

                def up(g, u, e):
                    n = E * g + e
                    if e == 0:
                        pe.wait_ge(xlo_ready, 2 * (g + 1))
                    wait(pe, h_ready, n - 1)
                    x_hi, x_lo = (t[:, u, e].rearrange("p i k -> p (i k)") for t in (xe_hi, xe_lo))
                    for f in range(F):
                        w = slice(f * P, (f + 1) * P)
                        pe.matmul(h_ps[:, e % 2, f, :], w1_hi[:, e, w], x_hi, start=True, stop=False)
                        pe.matmul(h_ps[:, e % 2, f, :], w1_hi[:, e, w], x_lo, start=False, stop=False)
                        last = pe.matmul(h_ps[:, e % 2, f, :], w1_lo[:, e, w], x_hi, start=False, stop=True)
                    last.then_inc(h_done, 1)

                def down(g, e):
                    n = E * g + e
                    pe.wait_ge(hhi_ready, n + 1)
                    pe.wait_ge(hlo_ready, n + 1)
                    wait(pe, z_ready, n)
                    for f in range(F):
                        pe.matmul(z_ps[:, 0:D], h_hi[:, e % 4, f, :], w2_hi[:, e, f, :], start=(f == 0), stop=False)
                        pe.matmul(z_ps[:, 0:D], h_hi[:, e % 4, f, :], w2_lo[:, e, f, :], start=False, stop=False)
                        last = pe.matmul(z_ps[:, 0:D], h_lo[:, e % 4, f, :], w2_hi[:, e, f, :], start=False, stop=(f == F - 1))
                    last.then_inc(z_done, 1)

                def scatter(g, u, part):
                    if part == 0:
                        pe.wait_ge(z_ready, E * (g + 1))
                        pe.wait_ge(gw_ready, 2 * (g + 1))
                        wait(pe, y_read, G * g)
                    for e in (2 * part, 2 * part + 1):
                        for i in range(G):
                            r = slice(K * i, K * i + K)
                            pe.matmul(y_ps[:, i, 0:D], back[r, u, e, :], z_hi[r, u, e, :], start=(e == 0), stop=False)
                            last = pe.matmul(y_ps[:, i, 0:D], back[r, u, e, :], z_lo[r, u, e, :], start=False, stop=(e == E - 1))
                    if part == 3:
                        last.then_inc(y_done, 1)

                for half in range(2):
                    gather(0, 0, half)
                for half in range(2):
                    turn_weights(0, 0, half)

                def step(g, u, last=None):
                    more = not (isinstance(g, int) and g == last)
                    before = not (isinstance(g, int) and g == 0)
                    for e in range(E):
                        up(g, u, e)
                        if e >= 2:
                            if before and e < 6:
                                scatter(g - 1, 1 - u, e - 2)
                            down(g, e - 2)
                        elif before:
                            down(g - 1, E - 2 + e)
                        if more and e in (3, 4):
                            gather(g + 1, 1 - u, e - 3)
                        if more and e in (5, 6):
                            turn_weights(g + 1, 1 - u, e - 5)

                over_batches(pe, step, NG)
                down(NG - 1, E - 2)
                down(NG - 1, E - 1)
                for part in range(4):
                    scatter(NG - 1, 1, part)

        sem.clear()


def hashed_mixture(nc, m):
    G, NG = 4, 8
    WS = 64.0
    with ExitStack() as ctx:
        def sb(n, shape, dt=F32):
            return ctx.enter_context(nc.sbuf_tensor(f"s_{n}", shape, dt))

        def ps(n, shape):
            return ctx.enter_context(nc.psum_tensor(f"s_{n}", shape, F32))

        sem = Semaphores(nc, ctx, "s")

        lnv, rstd, nmr = sb("lnv", [P, 6, B]), sb("rstd", [P, B]), sb("nmr", [P, B])
        xn = sb("xn", [P, 2, G, D])
        xT_hi, xT_lo = sb("xT_hi", [P, 2, 8, 64], F16), sb("xT_lo", [P, 2, 8, 64], F16)
        av = sb("av", [P, 512])
        sg = sb("sg", [P, 512])
        gt = sb("gt", [P, 512])
        hs = sb("hs", [P, 2, 512])
        hs_hi, hs_lo = sb("hs_hi", [P, 2, 512], F16), sb("hs_lo", [P, 2, 512], F16)
        hr = sb("hr", [P, 2, 8, 64])
        hr_hi, hr_lo = sb("hr_hi", [P, 2, 8, 64], F16), sb("hr_lo", [P, 2, 8, 64], F16)
        hot = sb("hot16", [E + 1, 3, 512], F16)
        b1, b2 = sb("b1_parts", [E, 2, P], F16), sb("b2_parts", [E + 1, 2, P], F16)
        sb3 = sb("sb3", [P, 2])
        w_hi, w_lo = m["s_parts"][0], m["s_parts"][1]
        yT = sb("yT", [P, 64, 8])
        x_ps, a_ps, y_ps, t_ps = ps("x_ps", [P, G, P]), ps("a_ps", [P, 4, 512]), ps("y_ps", [P, 512]), ps("t_ps", [P, G, P])
        half_set, ln_ready, pow_ready, steps = sem("half_set"), sem("ln_ready"), sem("pow_ready"), sem("steps")
        av_ready, parts_high, parts_ready = sem("av_ready"), sem("parts_high"), sem("parts_ready")
        xhi_ready, hshi_ready, hslo_ready, hrhi_ready, hrlo_ready = (sem("xhi_ready"), sem("hshi_ready"), sem("hslo_ready"),
                                                                     sem("hrhi_ready"), sem("hrlo_ready"))
        xn_ready, x_turned, xT_ready = sem("xn_ready"), sem("x_turned"), sem("xT_ready")
        gate_done, up_done, sg_ready, gt_ready, hs_ready = (sem("gate_done"), sem("up_done"), sem("sg_ready"),
                                                            sem("gt_ready"), sem("hs_ready"))
        r_done, hr_ready = sem("r_done"), sem("hr_ready")
        y_done, yT_ready, y_turned, x_done = sem("y_done"), sem("yT_ready"), sem("y_turned"), sem("x_done")

        with nc.Block() as block:

            @block.gpsimd
            def _(pool):
                pool.memset(lnv[:, 5, :], -0.5).then_inc(half_set, 1)
                pool.wait_ge(half_set, 1)
                pool.wait_ge(ln_ready, 1)
                nc.gpsimd.tensor_tensor(rstd[:], lnv[:, 4, :], lnv[:, 5, :], ALU.pow).then_inc(pow_ready, 1)

                def step(g, u, last=None):
                    wait(pool, y_done, g)
                    for k in range(2):
                        pool.wait_ge(hrhi_ready, 2 * g + k + 1)
                        nc.gpsimd.tensor_tensor(hr_lo[:, k], hr[:, k], hr_hi[:, k], ALU.subtract).then_inc(hrlo_ready, 1)

                over_batches(pool, step, NG)

            @block.vector
            def _(dve):
                layernorm_stats(nc, dve, m, lnv, rstd, nmr, steps, ln_ready, pow_ready)

                def normalise(g, u):
                    wait(dve, x_turned, g - 1)
                    for i in range(G):
                        last = dve.tensor_scalar(xn[:, u, i, :], m["x"][:, G * g + i, :], rstd[:, bass.ds(G * g + i, 1)],
                                                 nmr[:, bass.ds(G * g + i, 1)], ALU.mult, ALU.add)
                    last.then_inc(xn_ready, 1)

                def x_low(g, u):
                    dve.wait_ge(xhi_ready, g + 1)
                    wait(dve, r_done, 2 * (g - 1))
                    dve.tensor_tensor(xT_lo[:, u].rearrange("p r q -> p q r"), x_ps[:].rearrange("p i t -> p (i t)")
                                      .rearrange("p (q r) -> p q r", r=8), xT_hi[:, u].rearrange("p r q -> p q r"),
                                      ALU.subtract).then_inc(xT_ready, 1)

                normalise(0, 0)
                normalise(1, 1)
                dve.wait_ge(parts_high, 3)
                dve.scalar_tensor_tensor(w_lo["all"], m["s_all"][:], WS, w_hi["all"], ALU.mult, ALU.subtract).then_inc(parts_ready, 1)
                dve.scalar_tensor_tensor(b1[:, 1, :], m["s_b1"][:], WS, b1[:, 0, :], ALU.mult, ALU.subtract).then_inc(parts_ready, 1)
                dve.scalar_tensor_tensor(b2[:, 1, :], m["s_b2"][:], WS, b2[:, 0, :], ALU.mult, ALU.subtract).then_inc(parts_ready, 1)
                dve.tensor_copy(hot[:], m["s_hot"][:]).then_inc(parts_ready, 1)
                for k in range(2):
                    dve.tensor_scalar(sb3[:, k:k + 1], m["col"][f"sb3_{k}"], WS, None, ALU.mult).then_inc(parts_ready, 1)
                dve.wait_ge(parts_ready, 6)
                x_low(0, 0)

                def step(g, u, last=None):
                    for k in range(2):
                        dve.wait_ge(sg_ready, 2 * g + k + 1)
                        wait(dve, hs_ready, 2 * g + k)
                        dve.scalar_tensor_tensor(gt[:], sg[:], 1.0, av[:], ALU.add, ALU.mult)\
                            .then_inc(gt_ready, 1)
                        dve.wait_ge(gt_ready, 2 * g + k + 1)
                        dve.wait_ge(up_done, 2 * g + k + 1)
                        dve.scalar_tensor_tensor(hs[:, k, :], a_ps[:, 1, :], sb3[:, k:k + 1], gt[:], ALU.add, ALU.mult)\
                            .then_inc(hs_ready, 1)
                        dve.wait_ge(hs_ready, 2 * g + k + 1)
                        wait(dve, y_done, g)
                        dve.tensor_scalar(hs_hi[:, k, :], hs[:, k, :], 1.0 / WS, None, ALU.mult).then_inc(hshi_ready, 1)
                        dve.wait_ge(hshi_ready, 2 * g + k + 1)
                        dve.scalar_tensor_tensor(hs_lo[:, k, :], hs[:, k, :], 1.0 / WS, hs_hi[:, k, :], ALU.mult, ALU.subtract)\
                            .then_inc(hslo_ready, 1)
                    if not (isinstance(g, int) and g == last):
                        x_low(g + 1, 1 - u)
                    if not (isinstance(g, int) and g + 2 >= NG):
                        normalise(g + 2, u)
                    for i in range(G):
                        if i == 0:
                            dve.wait_ge(y_turned, g + 1)
                        x = m["x"][:, G * g + i, :]
                        last_op = dve.scalar_tensor_tensor(x, t_ps[:, i, :], 0.25 / WS, x, ALU.mult, ALU.add)
                    last_op.then_inc(x_done, 1)
                    dve.wait_ge(x_done, g + 1)
                    for i in range(G):
                        dve.bn_stats(m["stats"][:, G * g + i, :], m["x"][:, G * g + i, :])

                over_batches(dve, step, NG)

            @block.scalar
            def _(act):
                act.preload_act_table(ACT.Gelu)

                def x_keep(g, u):
                    act.wait_ge(x_turned, g + 1)
                    wait(act, r_done, 2 * (g - 1))
                    act.activation(xT_hi[:, u].rearrange("p r q -> p q r"), x_ps[:].rearrange("p i t -> p (i t)")
                                   .rearrange("p (q r) -> p q r", r=8), ACT.Copy).then_inc(xhi_ready, 1)

                act.wait_ge(m["weights_in"], m["weights_count"])
                act.activation(w_hi["all"], m["s_all"][:], ACT.Copy, scale=WS).then_inc(parts_high, 1)
                act.activation(b1[:, 0, :], m["s_b1"][:], ACT.Copy, scale=WS).then_inc(parts_high, 1)
                act.activation(b2[:, 0, :], m["s_b2"][:], ACT.Copy, scale=WS).then_inc(parts_high, 1)
                x_keep(0, 0)

                def step(g, u, last=None):
                    for k in range(2):
                        act.wait_ge(gate_done, 2 * g + k + 1)
                        wait(act, gt_ready, 2 * g + k)
                        act.activation(av[:], a_ps[:, 0, :], ACT.Identity, scale=1.0 / WS,
                                       bias=m["col"][f"sb1_{k}"]).then_inc(av_ready, 1)
                        act.wait_ge(av_ready, 2 * g + k + 1)
                        act.activation(sg[:], av[:], ACT.Tanh, scale=0.5).then_inc(sg_ready, 1)
                    for k in range(2):
                        act.wait_ge(r_done, 2 * g + k + 1)
                        wait(act, hrlo_ready, 2 * (g - 1) + k + 1)
                        act.activation(hr[:, k].rearrange("p r q -> p (r q)"), a_ps[:, 2 + k, :], ACT.Gelu, scale=1.0 / WS)\
                            .then_inc(hr_ready, 1)
                        act.wait_ge(hr_ready, 2 * g + k + 1)
                        wait(act, y_done, g)
                        act.activation(hr_hi[:, k], hr[:, k], ACT.Copy).then_inc(hrhi_ready, 1)
                    if not (isinstance(g, int) and g == last):
                        x_keep(g + 1, 1 - u)
                    act.wait_ge(y_done, g + 1)
                    wait(act, y_turned, g)
                    act.activation(yT[:].rearrange("p q r -> p r q"), y_ps[:].rearrange("p (r q) -> p r q", r=8), ACT.Copy)\
                        .then_inc(yT_ready, 1)

                over_batches(act, step, NG)

            @block.tensor
            def _(pe):
                def turn(g, u):
                    pe.wait_ge(xn_ready, g + 1)
                    wait(pe, xT_ready, g)
                    for i in range(G):
                        last = pe.transpose(x_ps[:, i, :], xn[:, u, i, :], m["mat"]["ident"])
                    last.then_inc(x_turned, 1)

                def product(to, w, x, start, stop):
                    pe.matmul(to, w[0], x[0], start=start, stop=False, skip_group_check=True)
                    pe.matmul(to, w[0], x[1], start=False, stop=False, skip_group_check=True)
                    return pe.matmul(to, w[1], x[0], start=False, stop=stop, skip_group_check=True)

                turn(0, 0)
                pe.wait_ge(parts_ready, 6)

                def step(g, u, last=None):
                    xin = [t[:, u].rearrange("p r q -> p (r q)") for t in (xT_hi, xT_lo)]
                    pe.wait_ge(xT_ready, g + 1)
                    for k in range(2):
                        wait(pe, av_ready, 2 * g + k)
                        product(a_ps[:, 0, :], [w["w1"][:, k, :] for w in (w_hi, w_lo)], xin, True, True).then_inc(gate_done, 1)
                        wait(pe, hs_ready, 2 * g + k)
                        product(a_ps[:, 1, :], [w["w3"][:, k, :] for w in (w_hi, w_lo)], xin, True, True).then_inc(up_done, 1)
                    for k in range(2):
                        wait(pe, hr_ready, 2 * (g - 1) + k + 1)
                        for part in range(2):
                            pe.matmul(a_ps[:, 2 + k, :], b1[:, part, :], hot[0:E, k, :], start=(part == 0), stop=False,
                                      skip_group_check=True)
                        for r in range(8):
                            last_op = product(a_ps[:, 2 + k, 64 * r:64 * r + 64], [w["up"][:, HASHED[k][r], :] for w in (w_hi, w_lo)],
                                              [xT_hi[:, u, r, :], xT_lo[:, u, r, :]], False, r == 7)
                        last_op.then_inc(r_done, 1)
                    if not (isinstance(g, int) and g == last):
                        turn(g + 1, 1 - u)
                    wait(pe, yT_ready, g)
                    for part in range(2):
                        pe.matmul(y_ps[:], b2[:, part, :], hot[:, 2, :], start=(part == 0), stop=False, skip_group_check=True)
                    for k in range(2):
                        pe.wait_ge(hslo_ready, 2 * g + k + 1)
                        product(y_ps[:], [w["w2"][:, k, :] for w in (w_hi, w_lo)], [hs_hi[:, k, :], hs_lo[:, k, :]], False, False)
                    for k in range(2):
                        pe.wait_ge(hrhi_ready, 2 * g + k + 1)
                        pe.wait_ge(hrlo_ready, 2 * g + k + 1)
                        for r in range(8):
                            last_op = product(y_ps[:, 64 * r:64 * r + 64], [w["down"][:, HASHED[k][r], :] for w in (w_hi, w_lo)],
                                              [hr_hi[:, k, r, :], hr_lo[:, k, r, :]], False, k == 1 and r == 7)
                    last_op.then_inc(y_done, 1)
                    pe.wait_ge(yT_ready, g + 1)
                    wait(pe, x_done, g)
                    y = yT[:].rearrange("p q r -> p (q r)")
                    for i in range(G):
                        last_op = pe.transpose(t_ps[:, i, :], y[:, i * P:(i + 1) * P], m["mat"]["ident"])
                    last_op.then_inc(y_turned, 1)

                over_batches(pe, step, NG)

        sem.clear()


def zones(nc, m, a, out):
    TOP, F = 3, 4
    G = 4
    NG = B // G
    WS = 64.0
    with ExitStack() as ctx:
        def sb(n, shape, dt=F32):
            return ctx.enter_context(nc.sbuf_tensor(f"z_{n}", shape, dt))

        def ps(n, shape):
            return ctx.enter_context(nc.psum_tensor(f"zp_{n}", shape, F32))

        sem = Semaphores(nc, ctx, "z")

        lnv, rstd, nmr = sb("lnv", [P, 6, B]), sb("rstd", [P, B]), sb("nmr", [P, B])
        xn = sb("xn", [P, 2, G, D])
        xs = sb("xs", [P, B, 2, P], F16)
        wa_hi, wa_lo = (m["z_split_a"][:, i] for i in range(2))
        wb = m["z_split_b"]
        wb_hi, wb_lo, wb_in = wb[:, :, :, 0, :], wb[:, :, :, 1, :], m["z_wb"].rearrange("p e (f n) -> p e f n", f=F)
        meanT = sb("meanT", [P, B])
        hid, hidT = sb("hid", [B, 32]), sb("hidT", [32, B])
        lg, t1 = sb("lg", [B, 1, E]), sb("t1", [B, 1])
        top, idx, wt = sb("top", [B, 8]), sb("idx", [B, 8], U32), sb("wt", [B, 3])
        idx_f, packed_f, packed = sb("idx_f", [B, TOP]), sb("packed_f", [B, 1]), sb("packed", [B, 1], U32)
        idx_row, w_row = sb("idx_row", [1, B], U32), sb("w_row", [1, B * TOP])
        w_all = sb("w_all", [P, B * TOP])
        h, h_hi, h_lo = sb("h", [P, TOP, F, P]), sb("h_hi", [P, TOP, F, P], F16), sb("h_lo", [P, TOP, F, P], F16)
        o = sb("o", [P, 2, D])
        x_ps, h_ps, z_ps = ps("x_ps", [P, 2, 512]), ps("h_ps", [P, TOP, F, P]), ps("z_ps", [P, 2, 512])
        p_ps = ps("p_ps", [P, 512])
        half_set, ln_ready, pow_ready, steps = sem("half_set"), sem("ln_ready"), sem("pow_ready"), sem("steps")
        xn_ready, x_turned, xT_ready, x_sum = sem("xn_ready"), sem("x_turned"), sem("xT_ready"), sem("x_sum")
        xlo_ready, a_high, a_low, b_high = sem("xlo_ready"), sem("a_high"), sem("a_low"), sem("b_high")

        with nc.Block() as block:

            @block.gpsimd
            def _(pool):
                pool.memset(lnv[:, 5, :], -0.5).then_inc(half_set, 1)
                pool.wait_ge(half_set, 1)
                pool.wait_ge(ln_ready, 1)
                nc.gpsimd.tensor_tensor(rstd[:], lnv[:, 4, :], lnv[:, 5, :], ALU.pow).then_inc(pow_ready, 1)

                def step(g, u, last=None):
                    pool.wait_ge(xn_ready, g + 1)
                    x = m["x"][:, bass.ds(G * g, G), :]
                    nc.gpsimd.tensor_tensor(x, x, xn[:, u], ALU.add).then_inc(x_sum, 1)

                over_batches(pool, step, NG)

            @block.vector
            def _(dve):
                layernorm_stats(nc, dve, m, lnv, rstd, nmr, steps, ln_ready, pow_ready)

                def low(g, u):
                    dve.wait_ge(xT_ready, g + 1)
                    dve.tensor_tensor(xs[:, bass.ds(G * g, G), 1, :], x_ps[:, u].rearrange("p (i t) -> p i t", i=G),
                                      xs[:, bass.ds(G * g, G), 0, :], ALU.subtract).then_inc(xlo_ready, 1)

                def step(g, u, last=None):
                    wait(dve, x_turned, g - 1)
                    wait(dve, x_sum, g - 1)
                    for i in range(G):
                        last_op = dve.tensor_scalar(xn[:, u, i, :], m["x"][:, G * g + i, :], rstd[:, bass.ds(G * g + i, 1)],
                                                    nmr[:, bass.ds(G * g + i, 1)], ALU.mult, ALU.add)
                    last_op.then_inc(xn_ready, 1)
                    if not (isinstance(g, int) and g == 0):
                        low(g - 1, 1 - u)

                over_batches(dve, step, NG)
                low(NG - 1, 1)
                dve.tensor_copy(meanT[:], p_ps[:, 0:B])
                dve.wait_ge(a_high, 1)
                dve.scalar_tensor_tensor(wa_lo, m["z_wa"], WS, wa_hi, ALU.mult, ALU.subtract).then_inc(a_low, 1)
                dve.wait_ge(b_high, 1)
                dve.scalar_tensor_tensor(wb_lo, wb_in, WS, wb_hi, ALU.mult, ALU.subtract)

            @block.scalar
            def _(act):
                def step(g, u, last=None):
                    act.wait_ge(x_turned, g + 1)
                    act.activation(xs[:, bass.ds(G * g, G), 0, :], x_ps[:, u].rearrange("p (i t) -> p i t", i=G), ACT.Copy)\
                        .then_inc(xT_ready, 1)

                over_batches(act, step, NG)
                act.wait_ge(m["z_in"], 32)
                act.activation(wa_hi, m["z_wa"], ACT.Copy, scale=WS).then_inc(a_high, 1)
                act.wait_ge(a_low, 1)
                act.activation(wb_hi, wb_in, ACT.Copy, scale=WS).then_inc(b_high, 1)

            @block.tensor
            def _(pe):
                def step(g, u, last=None):
                    pe.wait_ge(xn_ready, g + 1)
                    wait(pe, xlo_ready, g - 1)
                    for i in range(G):
                        pe.matmul(p_ps[:, bass.ds(G * g + i, 1)], xn[:, u, i, :], m["mean"][:], start=True, stop=True)
                        last_op = pe.transpose(x_ps[:, u, i * P:(i + 1) * P], xn[:, u, i, :], m["mat"]["ident"])
                    last_op.then_inc(x_turned, 1)

                over_batches(pe, step, NG)

        c_steps, h1_done, h1_ready, hT_done, hT_ready, l_done = (sem("c_steps"), sem("h1_done"), sem("h1_ready"),
                                                                 sem("hT_done"), sem("hT_ready"), sem("l_done"))
        tanh_ready, act_ready, exp_ready, pick_ready, row_in, w_done = (sem("tanh_ready"), sem("act_ready"), sem("exp_ready"),
                                                                        sem("pick_ready"), sem("row_in"), sem("w_done"))
        with nc.Block() as block:

            @block.tensor
            def _(pe):
                pe.matmul(p_ps[0:B, 64:96], meanT[:], m["z_w1"][:], start=True, stop=True).then_inc(h1_done, 1)
                pe.wait_ge(tanh_ready, 1)
                pe.matmul(p_ps[0:B, 128:160], hid[:], m["mat"]["ident"][0:B, 0:B], start=True, stop=True).then_inc(hT_done, 1)
                pe.wait_ge(hT_ready, 1)
                pe.matmul(p_ps[0:B, 192:192 + E], hidT[:], m["z_w2"][:], start=True, stop=True).then_inc(l_done, 1)
                pe.wait_ge(row_in, 32)
                pe.matmul(x_ps[:, 0, 0:B * TOP], m["ones"][:], w_row[:], start=True, stop=True).then_inc(w_done, 1)

            @block.scalar
            def _(act):
                act.wait_ge(h1_ready, 1)
                act.activation(hid[:], hid[:], ACT.Tanh).then_inc(tanh_ready, 1)
                act.wait_ge(act_ready, 1)
                act.activation(lg[:], lg[:], ACT.Exp).then_inc(exp_ready, 1)

            @block.vector
            def _(dve):
                c = Chain(dve, c_steps)
                dve.wait_ge(h1_done, 1)
                dve.tensor_tensor(hid[:], p_ps[0:B, 64:96], m["row"]["z_b1"][0:B, 0:32], ALU.add).then_inc(h1_ready, 1)
                dve.wait_ge(hT_done, 1)
                dve.tensor_copy(hidT[:], p_ps[0:B, 128:160]).then_inc(hT_ready, 1)
                dve.wait_ge(l_done, 1)
                c(dve.tensor_tensor(lg[:, 0, :], p_ps[0:B, 192:192 + E], m["row"]["z_b2"][0:B, 0:E], ALU.add))
                softmax_experts(nc, dve, act_ready, exp_ready, c, lg[:], t1[:], B)
                c(dve.max(top[:], lg[:, 0, :]))
                c(dve.max_index(idx[:], top[:], lg[:, 0, :]))
                c(dve.tensor_reduce(t1[:], top[:, 0:TOP], AX.X, ALU.add))
                c(dve.reciprocal(t1[:], t1[:]))
                c(dve.tensor_copy(idx_f[:], idx[:, 0:TOP]))
                c(dve.scalar_tensor_tensor(packed_f[:], idx_f[:, 1:2], 8.0, idx_f[:, 0:1], ALU.mult, ALU.add))
                c(dve.scalar_tensor_tensor(packed_f[:], idx_f[:, 2:3], 64.0, packed_f[:], ALU.mult, ALU.add))
                c(dve.tensor_copy(packed[:], packed_f[:]))
                dve.tensor_scalar(wt[:], top[:, 0:TOP], t1[:, 0:1], None, ALU.mult).then_inc(pick_ready, 1)
                dve.wait_ge(w_done, 1)
                dve.tensor_copy(w_all[:], x_ps[:, 0, 0:B * TOP])

            @block.sync
            def _(sp):
                sp.wait_ge(pick_ready, 1)
                sp.dma_start(idx_row[:], packed[:]).then_inc(row_in, 16)
                sp.dma_start(w_row[0:1, :].rearrange("p (b k) -> p b k", k=TOP), wt[:]).then_inc(row_in, 16)
                sp.wait_ge(row_in, 32)

        h_done, h_ready, hi_ready, lo_ready, z_done, x_ready, o_ready = (
            sem("h_done"), sem("h_ready"), sem("hi_ready"), sem("lo_ready"), sem("z_done"), sem("x_ready"), sem("o_ready"))
        stored = [sem("stored0"), sem("stored1")]
        with nc.Block() as block:

            @block.tensor
            def _(pe):
                def zones_of(b):
                    v = pe.value_load(idx_row[0:1, bass.ds(b, 1)], min_val=0, max_val=E ** TOP - 1)
                    return [v & 7, (v >> 3) & 7, (v >> 6) & 7]

                def up(b, k, e):
                    n = TOP * b + k
                    wait(pe, h_ready, n - 2)
                    for f in range(F):
                        w = bass.ds(e * 512 + f * P, P)
                        pe.matmul(h_ps[:, k, f, :], wa_hi[:, w], xs[:, b, 0, :], start=True, stop=False)
                        pe.matmul(h_ps[:, k, f, :], wa_hi[:, w], xs[:, b, 1, :], start=False, stop=False)
                        last = pe.matmul(h_ps[:, k, f, :], wa_lo[:, w], xs[:, b, 0, :], start=False, stop=True)
                    last.then_inc(h_done, 1)

                def down(b, u, k, e):
                    n = TOP * b + k
                    pe.wait_ge(hi_ready, n + 1)
                    pe.wait_ge(lo_ready, n + 1)
                    if k == 0:
                        wait(pe, o_ready, b - 1)
                    for f in range(F):
                        w = wb[:, bass.ds(e, 1), f]
                        pe.matmul(z_ps[:, u, 0:2 * D], h_hi[:, k, f, :], w, start=(k == 0 and f == 0), stop=False,
                                  skip_group_check=True)
                        last = pe.matmul(z_ps[:, u, 0:D], h_lo[:, k, f, :], w[:, :, 0, :], start=False,
                                         stop=(k == TOP - 1 and f == F - 1), skip_group_check=True)
                    last.then_inc(z_done, 1)

                loaded = []
                e = zones_of(0)
                up(0, 0, e[0])
                up(0, 1, e[1])

                def step(b, u, last=None):
                    more = not (isinstance(b, int) and b == last)
                    e = loaded.pop() if u else zones_of(b)
                    after = zones_of(b + 1) if more else ()
                    if not u:
                        loaded.append(after)
                    for k in range(TOP):
                        if k == 0:
                            up(b, 2, e[2])
                        elif more:
                            up(b + 1, k - 1, after[k - 1])
                        down(b, u, k, e[k])

                over_batches(pe, step)

            @block.scalar
            def _(act):
                act.preload_act_table(ACT.Gelu_apprx_tanh)

                def step(b, u, last=None):
                    for k in range(TOP):
                        n = TOP * b + k
                        act.wait_ge(h_done, n + 1)
                        wait(act, lo_ready, n - 2)
                        act.activation(h[:, k], h_ps[:, k], ACT.Gelu_apprx_tanh, scale=1.0 / WS).then_inc(h_ready, 1)

                over_batches(act, step)

            @block.vector
            def _(dve):
                def finish(b, u):
                    dve.wait_ge(z_done, TOP * (b + 1))
                    wait(dve, stored[u], 8 * (b - u))
                    x = m["x"][:, b, :]
                    dve.scalar_tensor_tensor(x, z_ps[:, u, 0:D], 1.0 / WS, x, ALU.mult, ALU.add).then_inc(x_ready, 1)
                    dve.wait_ge(x_ready, b + 1)
                    dve.scalar_tensor_tensor(o[:, u, :], z_ps[:, u, D:2 * D], 1.0 / WS, x, ALU.mult, ALU.add)\
                        .then_inc(o_ready, 1)

                def step(b, u, last=None):
                    for k in range(TOP):
                        n = TOP * b + k
                        w = w_all[:, bass.ds(n, 1)]
                        dve.wait_ge(h_ready, n + 1)
                        wait(dve, z_done, n - 2)
                        dve.tensor_scalar(h_hi[:, k], h[:, k], w, None, ALU.mult).then_inc(hi_ready, 1)
                        dve.wait_ge(hi_ready, n + 1)
                        dve.scalar_tensor_tensor(h_lo[:, k], h[:, k], w, h_hi[:, k], ALU.mult, ALU.subtract).then_inc(lo_ready, 1)
                        if k == 1 and not (isinstance(b, int) and b == 0):
                            finish(b - 1, 1 - u)

                over_batches(dve, step)
                finish(B - 1, 1)

            @block.sync
            def _(sp):
                def step(b, u, last=None):
                    sp.wait_ge(o_ready, b + 1)
                    sp.dma_start(out[:, b, :], o[:, u, :]).then_inc(stored[u], 16)

                over_batches(sp, step)
                for u in range(2):
                    sp.wait_ge(stored[u], 8 * B)

        sem.clear()




def load(nc, m, a):
    with ExitStack() as ctx:
        sem = Semaphores(nc, ctx, "load")

        x_in, c_in, w_in = sem("x_in"), sem("c_in"), sem("w_in")
        steps, lam_ready, lam_exp = sem("steps"), sem("lam_ready"), sem("lam_exp")
        lq = ctx.enter_context(nc.sbuf_tensor("lq", [P, 4, 4], F32))
        lp = ctx.enter_context(nc.sbuf_tensor("lp", [P, 2, 4], F32))
        ls = ctx.enter_context(nc.sbuf_tensor("ls", [P, 2], F32))
        small = [("cols", a["cols"]), ("router_w", a["router_w"]), ("gate_w", a["gate_w"]), ("z_w1", a["z_w1"]),
                 ("z_w2", a["z_w2"]), ("down", a["down"]), ("iota", a["iota"]),
                 ("s_b1", a["s_b1"]), ("s_b2", a["s_b2"]), ("s_hot", a["s_hot"])]
        early = 16 * (4 + len(small))
        with nc.Block() as block:

            @block.sync
            def _(sp):
                for i in range(4):
                    sp.dma_start(m["x"][:, 8 * i:8 * i + 8, :], a["x"][:, 8 * i:8 * i + 8, :]).then_inc(x_in, 16)
                sp.dma_start(m["mats"][:], a["mats"]).then_inc(w_in, 16)
                for name, src in small:
                    sp.dma_start(m[name][:], src).then_inc(w_in, 16)
                for to, part in zip(m["sel8"], "qk"):
                    sp.dma_start(to[:], a["sel8_" + part]).then_inc(w_in, 16)

            @block.scalar
            def _(act):
                act.dma_start(m["ctxT"][:], a["ctxT"]).then_inc(c_in, 16)
                act.dma_start(m["rows"][:], a["rows"].partition_broadcast(P)).then_inc(w_in, 16)
                act.dma_start(lq[:], a["lams"].partition_broadcast(P)).then_inc(c_in, 16)
                act.wait_ge(lam_ready, 1)
                act.activation(ls[:], ls[:], ACT.Exp).then_inc(lam_exp, 1)

            @block.vector
            def _(dve):
                dve.wait_ge(x_in, 64)
                with dve.Fori(0, B // 8) as i:
                    for k in range(8):
                        dve.bn_stats(m["stats"][:, 8 * i + k, :], m["x"][:, 8 * i + k, :])
                dve.memset(m["onesb"][:], 1.0)
                dve.memset(m["mean"][:], 1.0 / P)
                dve.memset(m["ones"][:], 1.0)
                dve.wait_ge(c_in, 32)
                c = Chain(dve, steps)
                c(dve.tensor_tensor(lp[:], lq[:, 0:4:2, :], lq[:, 1:4:2, :], ALU.mult))
                c(dve.tensor_reduce(ls[:], lp[:], AX.X, ALU.add))
                dve.sem_inc(lam_ready, 1)
                dve.wait_ge(lam_exp, 1)
                dve.scalar_tensor_tensor(m["lam"][:], ls[:, 0:1], LAMBDA_INIT, ls[:, 1:2], ALU.add, ALU.subtract)
                dve.wait_ge(w_in, early)
                dve.tensor_copy(m["identb"][:], m["mat"]["ident"])
                dve.tensor_scalar(m["negident"][:], m["mat"]["ident"], -1.0, None, ALU.mult)

        sem.clear()


def program(nc, a, out):
    with ExitStack() as ctx:
        def sb(n, shape, dt=F32):
            return ctx.enter_context(nc.sbuf_tensor(n, shape, dt))

        m = {}
        m["x"] = sb("x_all", [P, B, D])
        m["ctxT"] = sb("ctxT", [P, B, P])
        m["big"] = sb("big", [P, B, P])
        m["y_parts"] = m["big"][:].rearrange("p b t -> p (b t)").bitcast(F16).rearrange("p (s b t) -> p s b t", s=2, b=B)
        m["stats"] = sb("stats", [P, B, 6])
        m["mats"] = sb("mats", [P, len(MATS), P])
        m["cols"] = sb("cols", [P, len(COLS)])
        m["rows"] = sb("rows", [P, len(ROWS), P])
        m["mat"] = {n: m["mats"][:, i, :] for i, n in enumerate(MATS)}
        m["col"] = {n: m["cols"][:, i:i + 1] for i, n in enumerate(COLS)}
        m["row"] = {n: m["rows"][:, i, :] for i, n in enumerate(ROWS)}
        m["sel"] = {"sel8": (sb("sel8_q", [P, 2, 4, P], F16), sb("sel8_k", [P, 2, 4, P], F16)),
                    "sel4": (sb("sel4_q", [P, 2, 4, P], F16), sb("sel4_k", [P, 2, 4, P], F16)),
                    "sel4x2": (sb("sel4x2_q", [P, 2, 8, P], F16), sb("sel4x2_k", [P, 2, 8, P], F16))}
        m.update({"sel8": m["sel"]["sel8"], "sel4": m["sel"]["sel4"], "sel4x2": m["sel"]["sel4x2"]})
        m["maskq"] = sb("maskq", [P, B, P], U8)
        m["maskk"] = sb("maskk", [P, B, P], U8)
        m["identb"], m["negident"], m["onesb"] = (sb("identb", [P, P], BF16), sb("negident", [P, P], F16),
                                                  sb("onesb", [P, P], BF16))
        m["mean"], m["ones"], m["lam"] = sb("mean", [P, 1]), sb("ones", [1, P]), sb("lam", [P, 1])
        m["router_w"], m["gate_w"] = sb("router_w", [P, E]), sb("gate_w", [P, E])
        m["z_w1"], m["z_w2"] = sb("z_w1", [P, 32]), sb("z_w2", [32, E])
        m["down"], m["iota"] = sb("down", [P, E]), sb("iota", [P, 32])
        m["s_b1"], m["s_b2"], m["s_hot"] = sb("s_b1", [E, P]), sb("s_b2", [E + 1, P]), sb("s_hot", [E + 1, 3, 512])
        m["logits"] = sb("logits", [P, B, E])
        m["weights_in"] = ctx.enter_context(nc.semaphore("weights_in"))
        m["m_in"], m["z_in"] = (ctx.enter_context(nc.semaphore("m_in")), ctx.enter_context(nc.semaphore("z_in")))
        m["pool"] = sb("pool", [P, 3, 4096])
        m["pool16"] = m["pool"][:].rearrange("p s n -> p (s n)").bitcast(F16).rearrange("p (s n) -> p s n", s=3)
        m["split_a"], m["split_b"] = (m["pool16"][:, i].rearrange("p (s n) -> p s n", s=2) for i in (2, 0))
        m["e_w1"] = m["pool"][:, 0].rearrange("p (e f) -> p e f", e=E)
        m["e_w2"] = m["pool"][:, 1].rearrange("p (e c d) -> p e c d", e=E, c=4)
        m["z_wa"] = m["pool"][:, 0]
        m["z_wb"] = m["pool"][:, 1].rearrange("p (e n) -> p e n", e=E)
        m["z_split_a"] = m["split_a"]
        m["z_split_b"] = m["pool16"][:, 0].rearrange("p (e f s n) -> p e f s n", e=E, f=4, s=2)
        m["m_w1"] = m["pool"][:, 0, 0:2048].rearrange("p (e f) -> p e f", e=E)
        m["m_w2"] = m["pool"][:, 0, 2048:4096].rearrange("p (e c d) -> p e c d", e=E, c=2)
        parts = m["pool16"][:, 2].rearrange("p (w s n) -> p w s n", w=2, s=2)
        m["m_w1_parts"] = parts[:, 0].rearrange("p s (e f) -> p s e f", e=E)
        m["m_w2_parts"] = parts[:, 1].rearrange("p s (e c d) -> p s e c d", e=E, c=2)
        m["m_b2"] = m["pool"][:, 1, 0:2048].rearrange("p (b d) -> p b d", b=16)
        m["s_all"] = sb("s_all", [P, (6 + 2 * E) * P])

        def hashed_views(t):
            v = {"all": t}
            for n, at, k in (("w1", 0, 2), ("w3", 2, 2), ("w2", 4, 2), ("up", 6, E), ("down", 6 + E, E)):
                v[n] = t[:, at * P:(at + k) * P].rearrange("p (k n) -> p k n", k=k)
            return v

        m.update({"s_" + n: v for n, v in hashed_views(m["s_all"][:]).items() if n != "all"})
        m["s_parts"] = [hashed_views(m["pool16"][:, 2, i * 4096:i * 4096 + (6 + 2 * E) * P]) for i in range(2)]

        late = [(m[n][:], a[n]) for n in ("e_w1", "e_w2", "s_w1", "s_w2", "s_w3", "s_up", "s_down", "maskq", "maskk")]
        late += [(to[:], a[f"{n}_{part}"]) for n in ("sel4", "sel4x2") for to, part in zip(m[n], "qk")]
        m["weights_count"] = 16 * len(late)

        load(nc, m, a)
        attention(nc, m, "a0", 16, 8, 8, 8 ** -0.5, False, False, False, "x", "sel8", late, m["weights_in"])
        expert_choice(nc, m)
        recurrence(nc, m)
        attention(nc, m, "a1", 16, 4, 4, 0.5, True, False, False, "moe", "sel4",
                  [(m["m_w1"], a["m_w1"]), (m["m_w2"], a["m_w2"]), (m["m_b2"], a["m_b2"])], m["m_in"])
        top_two_mixture(nc, m)
        attention(nc, m, "a2", 16, 8, 8, 8 ** -0.5, False, True, False, "x", "sel8")
        hashed_mixture(nc, m)
        attention(nc, m, "a3", 32, 4, 8, 0.5, False, False, True, "x", "sel4x2",
                  [(m["z_wa"], a["z_wa"]), (m["z_wb"], a["z_wb"])], m["z_in"])
        zones(nc, m, a, out)



def lay_out(i):
    f = np.float32

    def t(n):
        return np.ascontiguousarray(np.asarray(i[n]).T)

    def g(n):
        return np.asarray(i[n])

    def spread(w, n=4, by=8):
        w = w.reshape(-1, H, n)
        o = np.zeros((w.shape[0], H, by), f)
        o[:, :, :n] = w
        return o.reshape(-1, H * by)

    def wide(w):
        o = np.zeros((P, P), f)
        o[:w.shape[0], :w.shape[1]] = w
        return o

    def row(v):
        o = np.zeros(P, f)
        o[:v.size] = v.reshape(-1)
        return o

    ip, ib = g("L3_xattn_in_proj_weight"), g("L3_xattn_in_proj_bias")
    mats = {"a0_q": t("L0_xattn_w_q"), "a0_k": t("L0_xattn_w_k"), "a0_v": t("L0_xattn_w_v"), "a0_o": t("L0_xattn_w_o"),
            "r_wi": t("L1_xattn_Wi"), "r_wg": t("L1_xattn_Wg"), "r_a": t("L1_xattn_A"), "r_bm": t("L1_xattn_Bm"),
            "r_wo": t("L1_xattn_Wo"), "a1_q": g("L1_ffn_q_w"), "a1_k": spread(g("L1_ffn_k_w")),
            "a1_v": wide(g("L1_ffn_v_w")), "a1_o": g("L1_ffn_o_w"), "a2_q": g("L2_xattn_Wq"), "a2_k": g("L2_xattn_Wk"),
            "a2_v": g("L2_xattn_Wv"), "a2_o": g("L2_xattn_Wo"), "a3_q": ip[:P].T, "a3_k": ip[P:2 * P].T,
            "a3_v": ip[2 * P:].T, "a3_o": t("L3_xattn_out_proj_weight"), "ident": np.eye(P, dtype=f),
            "tri": np.triu(np.ones((P, P), f))}
    b1 = g("L1_ffn_b1").reshape(-1, P)
    cols = {"a0_q": g("L0_xattn_b_q"), "a0_k": g("L0_xattn_b_k"), "a1_q": g("L1_ffn_q_b"),
            "a1_k": spread(g("L1_ffn_k_b")[None])[0], "a1_o": g("L1_ffn_o_b"), "a2_q": g("L2_xattn_bq"),
            "a2_k": g("L2_xattn_bk"), "a3_q": ib[:P], "a3_k": ib[P:2 * P], "r_bi": g("L1_xattn_bi"), "r_bg": g("L1_xattn_bg"),
            "decay": np.repeat(g("L1_xattn_decay").reshape(H), D // H), "sb1_0": g("L2_ffn_sb1")[:P],
            "sb1_1": g("L2_ffn_sb1")[P:], "sb3_0": g("L2_ffn_sb3")[:P], "sb3_1": g("L2_ffn_sb3")[P:]}
    cols.update({f"m_b1_{k}": b1[k] for k in range(16)})
    rows = {"a0_v": g("L0_xattn_b_v"), "a0_o": g("L0_xattn_b_o"), "a1_v": row(g("L1_ffn_v_b")), "a2_v": g("L2_xattn_bv"),
            "a2_o": g("L2_xattn_bo"), "a3_v": ib[2 * P:], "a3_o": g("L3_xattn_out_proj_bias"), "r_bo": g("L1_xattn_bo"),
            "router_b": row(g("L1_ffn_router_b")), "z_b1": row(g("L3_ffn_b1")), "z_b2": row(g("L3_ffn_b2"))}

    def select(nblk, hd, parts, rows_of=None):
        o = np.zeros((P, 2, nblk, P), np.float16)
        for blk in range(nblk):
            for grp in range(4):
                src = (4 * blk + grp) * (P // (4 * nblk))
                for s, part in enumerate(parts):
                    for d in range(hd):
                        o[src + d, part, blk, 32 * grp + s * hd + d] = 1
        return o

    mask = g("mask_Bx1xSxS2_bk0").reshape(B, P, P)
    b2 = g("L1_ffn_b2")
    m_b2 = np.zeros((16, E, 16, P), f)
    for k in range(16):
        m_b2[k, :, k] = b2
    hot = np.zeros((E + 1, 3, 8, 64), f)
    for r in range(8):
        for k in range(2):
            hot[HASHED[k][r], k, r] = 1
            hot[HASHED[k][r], 2, r] += 1
    hot[E, 2] = 2
    w2 = g("L0_ffn_w2").reshape(E, 4, P, D)
    return {
        "x": g("x").transpose(1, 0, 2), "ctxT": g("ctx_1024").transpose(2, 0, 1),
        "mats": np.stack([mats[n] for n in MATS], 1), "cols": np.stack([cols[n] for n in COLS], 1),
        "rows": np.stack([rows[n] for n in ROWS], 0),
        "sel8_q": select(4, 8, (0, 1, 0)), "sel8_k": select(4, 8, (0, 0, 1)),
        "sel4_q": select(4, 4, (0, 1, 0)), "sel4_k": select(4, 4, (0, 0, 1)),
        "sel4x2_q": select(8, 4, (0, 1, 0)), "sel4x2_k": select(8, 4, (0, 0, 1)),
        "maskq": mask.transpose(1, 0, 2), "maskk": mask.transpose(2, 0, 1),
        "router_w": g("L1_ffn_router_w"), "gate_w": g("L0_ffn_gate_w"), "z_w1": g("L3_ffn_W1"), "z_w2": g("L3_ffn_W2"),
        "down": np.tile(np.arange(E, 0, -1, dtype=f), (P, 1)), "iota": np.tile(np.arange(1, 33, dtype=f), (P, 1)),
        "s_b1": g("L2_ffn_b1"), "s_b2": np.concatenate([g("L2_ffn_b2"), g("L2_ffn_sb2")[None]], 0),
        "s_hot": hot.reshape(E + 1, 3, 512),
        "lams": np.stack([g("L3_xattn_lambda_q1"), g("L3_xattn_lambda_k1"), g("L3_xattn_lambda_q2"),
                          g("L3_xattn_lambda_k2")]),
        "e_w1": g("L0_ffn_w1").transpose(1, 0, 2), "e_w2": w2.transpose(2, 0, 1, 3),
        "m_w1": g("L1_ffn_w1").transpose(1, 0, 2), "m_w2": g("L1_ffn_w2").reshape(E, 2, P, D).transpose(2, 0, 1, 3),
        "m_b2": m_b2.reshape(P, 16, P),
        "s_w1": g("L2_ffn_sw1").reshape(P, 2, P), "s_w3": g("L2_ffn_sw3").reshape(P, 2, P),
        "s_w2": g("L2_ffn_sw2").reshape(2, P, P).transpose(1, 0, 2),
        "s_up": g("L2_ffn_w1").transpose(1, 0, 2), "s_down": g("L2_ffn_w2").transpose(1, 0, 2),
        "z_wa": g("L3_ffn_Wa").transpose(1, 0, 2).reshape(P, 4096),
        "z_wb": g("L3_ffn_Wb").reshape(E, 4, P, D).transpose(2, 0, 1, 3).reshape(P, E, 512),
    }


def kernel(**inputs):
    import concourse.bacc as bacc
    from concourse.bass_utils import run_bass_kernel_spmd

    nc = bacc.Bacc("TRN2", target_bir_lowering=False, num_devices=1)
    arrays = {f"in_{n}": np.ascontiguousarray(v) for n, v in lay_out(inputs).items()}
    a = {n[3:]: nc.dram_tensor(n, v.shape, mybir.dt.from_np(v.dtype), kind="ExternalInput").ap() for n, v in arrays.items()}
    out = nc.dram_tensor("out", (P, B, D), F32, kind="ExternalOutput").ap()
    program(nc, a, out)
    r = run_bass_kernel_spmd(nc, [arrays], core_ids=[0])
    return np.ascontiguousarray(r.results[0]["out"].transpose(1, 0, 2))
```
